# Optimizing a Trainium2 kernel written in Bass

```python
import numpy as np
import jax
import jax.numpy as jnp

def _softmax(x, axis=-1):
    return jax.nn.softmax(x, axis=axis)

def _gelu(x):
    return jax.nn.gelu(x, approximate=True)

def _silu(x):
    return jax.nn.silu(x)

def _sigmoid(x):
    return jax.nn.sigmoid(x)

def _layernorm(x, axis=-1, eps=1e-05):
    m = jnp.mean(x, axis=axis, keepdims=True)
    v = jnp.var(x, axis=axis, keepdims=True)
    return (x - m) / jnp.sqrt(v + eps)

def _scatter_add(tgt, idx, src, axis=0):
    return tgt.at[idx].add(src)

def _segment_sum(src, seg, n):
    return jax.ops.segment_sum(src, seg, n)
kernel_name = 'mk_cond_seq_d4_seqx_r8_278857'

def setup_inputs(seed: int=0):
    np.random.seed(seed)
    _w = jnp.asarray

    def _rec_inputs():
        import jax
        import jax.numpy as jnp
        _rk = jax.random.key(seed)
        x = 1.648e-05 + 1 * jax.random.normal(jax.random.fold_in(_rk, 1), (2, 512, 144), jnp.float32)
        _lenS = 512 - jax.random.randint(jax.random.fold_in(_rk, 7), (2,), 0, max(1, 512 // 4) + 1, jnp.int32)
        _lenS2 = 512 - jax.random.randint(jax.random.fold_in(_rk, 8), (2,), 0, max(1, 512 // 4) + 1, jnp.int32)
        cond_1152 = 0.00914911 + 1.00357 * jax.random.normal(jax.random.fold_in(_rk, 11), (2, 144), jnp.float32)
        return (x, cond_1152)
    x, cond_1152 = _rec_inputs()

    def _L0_cond_setup():
        import jax, jax.numpy as jnp
        import numpy as np
        B, L, C = (8, 128, 144)
        H = 16
        D = C // H
        FF = int(C * 4.0)
        EPS = 1e-06

        def _layernorm(x):
            mu = jnp.mean(x, axis=-1, keepdims=True)
            var = jnp.mean(jnp.square(x - mu), axis=-1, keepdims=True)
            return (x - mu) * jax.lax.rsqrt(var + EPS)

        def _modulate(x, shift, scale):
            return x * (1.0 + scale) + shift

        def _attention(h, W_qkv, b_qkv, W_proj, b_proj):
            b, l, c = h.shape
            qkv = h @ W_qkv + b_qkv
            qkv = qkv.reshape(b, l, 3, H, D)
            q, k, v = (qkv[:, :, 0], qkv[:, :, 1], qkv[:, :, 2])
            scale = D ** (-0.5)
            scores = jnp.einsum('blhd,bmhd->bhlm', q * scale, k)
            attn = jax.nn.softmax(scores, axis=-1)
            o = jnp.einsum('bhlm,bmhd->blhd', attn, v).reshape(b, l, c)
            return o @ W_proj + b_proj
        key = jax.random.key(seed)
        ks = jax.random.split(key, 12)
        s = 0.02
        return {'x': jax.random.normal(ks[0], (B, L, C), jnp.float32), 'c': jax.random.normal(ks[1], (B, 1, C), jnp.float32), 'W_qkv': jax.random.normal(ks[2], (C, 3 * C), jnp.float32) * s, 'b_qkv': jnp.zeros((3 * C,), jnp.float32), 'W_proj': jax.random.normal(ks[3], (C, C), jnp.float32) * s, 'b_proj': jnp.zeros((C,), jnp.float32), 'W_fc1': jax.random.normal(ks[4], (C, FF), jnp.float32) * s, 'b_fc1': jnp.zeros((FF,), jnp.float32), 'W_fc2': jax.random.normal(ks[5], (FF, C), jnp.float32) * s, 'b_fc2': jnp.zeros((C,), jnp.float32), 'W_ada': jax.random.normal(ks[6], (C, 6 * C), jnp.float32) * s, 'b_ada': jnp.zeros((6 * C,), jnp.float32)}
    _L0_cond_all = _L0_cond_setup()
    _L0_cond_in = {k: v for k, v in _L0_cond_all.items() if k in ('W_qkv', 'b_qkv', 'W_proj', 'b_proj', 'W_fc1', 'b_fc1', 'W_fc2', 'b_fc2', 'W_ada', 'b_ada')}
    del _L0_cond_all

    def _L1_cond_setup():
        import jax, jax.numpy as jnp
        import numpy as np
        DIM = 144
        HEADS = 16
        HEAD_DIM = DIM // HEADS
        HIDDEN = int(DIM * 4.0)
        EPS = 1e-12

        def rmsnorm(x, g, d):
            n = jnp.linalg.norm(x, axis=-1, keepdims=True)
            return x / jnp.maximum(n, EPS) * d ** 0.5 * g

        def modulate(x, scale, shift):
            return x * (1.0 + scale[:, None, :]) + shift[:, None, :]
        key = jax.random.key(seed)
        ks = jax.random.split(key, 12)
        B, N = (8, 128)
        s = 0.02
        return {'x': jax.random.normal(ks[0], (B, N, DIM), jnp.float32), 'c': jax.random.normal(ks[1], (B, DIM), jnp.float32), 'g1': jnp.ones((1,), jnp.float32), 'g2': jnp.ones((1,), jnp.float32), 'qkv_w': jax.random.normal(ks[2], (3 * DIM, DIM), jnp.float32) * s, 'qkv_b': jnp.zeros((3 * DIM,), jnp.float32), 'qg': jnp.ones((1,), jnp.float32), 'kg': jnp.ones((1,), jnp.float32), 'proj_w': jax.random.normal(ks[3], (DIM, DIM), jnp.float32) * s, 'proj_b': jnp.zeros((DIM,), jnp.float32), 'fc1_w': jax.random.normal(ks[4], (HIDDEN, DIM), jnp.float32) * s, 'fc1_b': jnp.zeros((HIDDEN,), jnp.float32), 'fc2_w': jax.random.normal(ks[5], (DIM, HIDDEN), jnp.float32) * s, 'fc2_b': jnp.zeros((DIM,), jnp.float32), 'ada_w': jax.random.normal(ks[6], (6 * DIM, DIM), jnp.float32) * s, 'ada_b': jnp.zeros((6 * DIM,), jnp.float32)}
    _L1_cond_all = _L1_cond_setup()
    _L1_cond_in = {k: v for k, v in _L1_cond_all.items() if k in ('g1', 'g2', 'qkv_w', 'qkv_b', 'qg', 'kg', 'proj_w', 'proj_b', 'fc1_w', 'fc1_b', 'fc2_w', 'fc2_b', 'ada_w', 'ada_b')}
    del _L1_cond_all

    def _L2_cond_setup():
        import jax, jax.numpy as jnp
        import numpy as np
        NUM_HEADS = 16
        NUM_EXPERTS = 4
        TOP_K = 2
        LN_EPS = 1e-06

        def _ln(h):
            mu = jnp.mean(h, axis=-1, keepdims=True)
            var = jnp.var(h, axis=-1, keepdims=True)
            return (h - mu) * jax.lax.rsqrt(var + LN_EPS)

        def _modulate(h, shift, scale):
            return h * (1.0 + scale[:, None, :]) + shift[:, None, :]
        key = jax.random.key(seed)
        ks = jax.random.split(key, 12)
        B, N, C = (8, 128, 144)
        H = 4 * C
        E = NUM_EXPERTS
        s = 0.02
        return {'x': jax.random.normal(ks[0], (B, N, C), jnp.float32), 'c': jax.random.normal(ks[1], (B, C), jnp.float32), 'w_adaln': jax.random.normal(ks[2], (C, 6 * C), jnp.float32) * s, 'b_adaln': jnp.zeros((6 * C,), jnp.float32), 'w_qkv': jax.random.normal(ks[3], (C, 3 * C), jnp.float32) * s, 'b_qkv': jnp.zeros((3 * C,), jnp.float32), 'w_proj': jax.random.normal(ks[4], (C, C), jnp.float32) * s, 'b_proj': jnp.zeros((C,), jnp.float32), 'w_gate': jax.random.normal(ks[5], (C, E), jnp.float32) * s, 'w1': jax.random.normal(ks[6], (E, C, H), jnp.float32) * s, 'b1': jnp.zeros((E, H), jnp.float32), 'w2': jax.random.normal(ks[7], (E, H, C), jnp.float32) * s, 'b2': jnp.zeros((E, C), jnp.float32)}
    _L2_cond_all = _L2_cond_setup()
    _L2_cond_in = {k: v for k, v in _L2_cond_all.items() if k in ('w_adaln', 'b_adaln', 'w_qkv', 'b_qkv', 'w_proj', 'b_proj', 'w_gate', 'w1', 'b1', 'w2', 'b2')}
    del _L2_cond_all

    def _L3_cond_setup():
        import jax, jax.numpy as jnp
        import numpy as np
        H = 144
        NH = 16
        HD = H // NH
        MLP = int(H * 4.0)
        EPS = 1e-06

        def _ln(z, scale=None):
            m = jnp.mean(z, axis=-1, keepdims=True)
            v = jnp.mean(jnp.square(z - m), axis=-1, keepdims=True)
            y = (z - m) * jax.lax.rsqrt(v + EPS)
            if scale is not None:
                y = y * scale
            return y
        key = jax.random.key(seed)
        ks = jax.random.split(key, 16)
        B, N = (16, 128)
        x = jax.random.normal(ks[0], (B, N, H), dtype=jnp.float32)
        c = jax.random.normal(ks[1], (B, H), dtype=jnp.float32)

        def xav(k, fan_in, fan_out):
            lim = np.sqrt(6.0 / (fan_in + fan_out))
            return jax.random.uniform(k, (fan_in, fan_out), jnp.float32, -lim, lim)
        w_mod = 0.02 * jax.random.normal(ks[2], (H, 6 * H), dtype=jnp.float32)
        b_mod = 0.02 * jax.random.normal(ks[3], (6 * H,), dtype=jnp.float32)
        w_qkv = xav(ks[4], H, 3 * H)
        b_qkv = jnp.zeros((3 * H,), jnp.float32)
        g_q = jnp.ones((HD,), jnp.float32)
        g_k = jnp.ones((HD,), jnp.float32)
        w_proj = xav(ks[5], H, H)
        b_proj = jnp.zeros((H,), jnp.float32)
        w1 = xav(ks[6], H, MLP)
        b1 = jnp.zeros((MLP,), jnp.float32)
        w2 = xav(ks[7], MLP, H)
        b2 = jnp.zeros((H,), jnp.float32)
        return dict(x=x, c=c, w_mod=w_mod, b_mod=b_mod, w_qkv=w_qkv, b_qkv=b_qkv, g_q=g_q, g_k=g_k, w_proj=w_proj, b_proj=b_proj, w1=w1, b1=b1, w2=w2, b2=b2)
    _L3_cond_all = _L3_cond_setup()
    _L3_cond_in = {k: v for k, v in _L3_cond_all.items() if k in ('w_mod', 'b_mod', 'w_qkv', 'b_qkv', 'g_q', 'g_k', 'w_proj', 'b_proj', 'w1', 'b1', 'w2', 'b2')}
    del _L3_cond_all
    return {'x': x, 'cond_1152': cond_1152, 'L0_cond_W_qkv': _L0_cond_in['W_qkv'], 'L0_cond_b_qkv': _L0_cond_in['b_qkv'], 'L0_cond_W_proj': _L0_cond_in['W_proj'], 'L0_cond_b_proj': _L0_cond_in['b_proj'], 'L0_cond_W_fc1': _L0_cond_in['W_fc1'], 'L0_cond_b_fc1': _L0_cond_in['b_fc1'], 'L0_cond_W_fc2': _L0_cond_in['W_fc2'], 'L0_cond_b_fc2': _L0_cond_in['b_fc2'], 'L0_cond_W_ada': _L0_cond_in['W_ada'], 'L0_cond_b_ada': _L0_cond_in['b_ada'], 'L1_cond_g1': _L1_cond_in['g1'], 'L1_cond_g2': _L1_cond_in['g2'], 'L1_cond_qkv_w': _L1_cond_in['qkv_w'], 'L1_cond_qkv_b': _L1_cond_in['qkv_b'], 'L1_cond_qg': _L1_cond_in['qg'], 'L1_cond_kg': _L1_cond_in['kg'], 'L1_cond_proj_w': _L1_cond_in['proj_w'], 'L1_cond_proj_b': _L1_cond_in['proj_b'], 'L1_cond_fc1_w': _L1_cond_in['fc1_w'], 'L1_cond_fc1_b': _L1_cond_in['fc1_b'], 'L1_cond_fc2_w': _L1_cond_in['fc2_w'], 'L1_cond_fc2_b': _L1_cond_in['fc2_b'], 'L1_cond_ada_w': _L1_cond_in['ada_w'], 'L1_cond_ada_b': _L1_cond_in['ada_b'], 'L2_cond_w_adaln': _L2_cond_in['w_adaln'], 'L2_cond_b_adaln': _L2_cond_in['b_adaln'], 'L2_cond_w_qkv': _L2_cond_in['w_qkv'], 'L2_cond_b_qkv': _L2_cond_in['b_qkv'], 'L2_cond_w_proj': _L2_cond_in['w_proj'], 'L2_cond_b_proj': _L2_cond_in['b_proj'], 'L2_cond_w_gate': _L2_cond_in['w_gate'], 'L2_cond_w1': _L2_cond_in['w1'], 'L2_cond_b1': _L2_cond_in['b1'], 'L2_cond_w2': _L2_cond_in['w2'], 'L2_cond_b2': _L2_cond_in['b2'], 'L3_cond_w_mod': _L3_cond_in['w_mod'], 'L3_cond_b_mod': _L3_cond_in['b_mod'], 'L3_cond_w_qkv': _L3_cond_in['w_qkv'], 'L3_cond_b_qkv': _L3_cond_in['b_qkv'], 'L3_cond_g_q': _L3_cond_in['g_q'], 'L3_cond_g_k': _L3_cond_in['g_k'], 'L3_cond_w_proj': _L3_cond_in['w_proj'], 'L3_cond_b_proj': _L3_cond_in['b_proj'], 'L3_cond_w1': _L3_cond_in['w1'], 'L3_cond_b1': _L3_cond_in['b1'], 'L3_cond_w2': _L3_cond_in['w2'], 'L3_cond_b2': _L3_cond_in['b2']}

def reference(x, cond_1152, L0_cond_W_qkv, L0_cond_b_qkv, L0_cond_W_proj, L0_cond_b_proj, L0_cond_W_fc1, L0_cond_b_fc1, L0_cond_W_fc2, L0_cond_b_fc2, L0_cond_W_ada, L0_cond_b_ada, L1_cond_g1, L1_cond_g2, L1_cond_qkv_w, L1_cond_qkv_b, L1_cond_qg, L1_cond_kg, L1_cond_proj_w, L1_cond_proj_b, L1_cond_fc1_w, L1_cond_fc1_b, L1_cond_fc2_w, L1_cond_fc2_b, L1_cond_ada_w, L1_cond_ada_b, L2_cond_w_adaln, L2_cond_b_adaln, L2_cond_w_qkv, L2_cond_b_qkv, L2_cond_w_proj, L2_cond_b_proj, L2_cond_w_gate, L2_cond_w1, L2_cond_b1, L2_cond_w2, L2_cond_b2, L3_cond_w_mod, L3_cond_b_mod, L3_cond_w_qkv, L3_cond_b_qkv, L3_cond_g_q, L3_cond_g_k, L3_cond_w_proj, L3_cond_b_proj, L3_cond_w1, L3_cond_b1, L3_cond_w2, L3_cond_b2):
    import jax
    import jax.numpy as jnp

    def _L0_cond_ref(x, c, W_qkv, b_qkv, W_proj, b_proj, W_fc1, b_fc1, W_fc2, b_fc2, W_ada, b_ada):
        import jax, jax.numpy as jnp
        import numpy as np
        B, L, C = (8, 128, 144)
        H = 16
        D = C // H
        FF = int(C * 4.0)
        EPS = 1e-06

        def _layernorm(x):
            mu = jnp.mean(x, axis=-1, keepdims=True)
            var = jnp.mean(jnp.square(x - mu), axis=-1, keepdims=True)
            return (x - mu) * jax.lax.rsqrt(var + EPS)

        def _modulate(x, shift, scale):
            return x * (1.0 + scale) + shift

        def _attention(h, W_qkv, b_qkv, W_proj, b_proj):
            b, l, c = h.shape
            qkv = h @ W_qkv + b_qkv
            qkv = qkv.reshape(b, l, 3, H, D)
            q, k, v = (qkv[:, :, 0], qkv[:, :, 1], qkv[:, :, 2])
            scale = D ** (-0.5)
            scores = jnp.einsum('blhd,bmhd->bhlm', q * scale, k)
            attn = jax.nn.softmax(scores, axis=-1)
            o = jnp.einsum('bhlm,bmhd->blhd', attn, v).reshape(b, l, c)
            return o @ W_proj + b_proj
        ada = jax.nn.silu(c) @ W_ada + b_ada
        shift_msa, scale_msa, gate_msa, shift_mlp, scale_mlp, gate_mlp = jnp.split(ada, 6, axis=-1)
        h = _modulate(_layernorm(x), shift_msa, scale_msa)
        x = x + gate_msa * _attention(h, W_qkv, b_qkv, W_proj, b_proj)
        h = _modulate(_layernorm(x), shift_mlp, scale_mlp)
        mlp = jax.nn.gelu(h @ W_fc1 + b_fc1, approximate=True) @ W_fc2 + b_fc2
        x = x + gate_mlp * mlp
        return x

    def _L1_cond_ref(x, c, g1, g2, qkv_w, qkv_b, qg, kg, proj_w, proj_b, fc1_w, fc1_b, fc2_w, fc2_b, ada_w, ada_b):
        import jax, jax.numpy as jnp
        import numpy as np
        DIM = 144
        HEADS = 16
        HEAD_DIM = DIM // HEADS
        HIDDEN = int(DIM * 4.0)
        EPS = 1e-12

        def rmsnorm(x, g, d):
            n = jnp.linalg.norm(x, axis=-1, keepdims=True)
            return x / jnp.maximum(n, EPS) * d ** 0.5 * g

        def modulate(x, scale, shift):
            return x * (1.0 + scale[:, None, :]) + shift[:, None, :]
        B, N, D = x.shape
        mod = jax.nn.silu(c) @ ada_w.T + ada_b
        shift_msa, scale_msa, gate_msa, shift_mlp, scale_mlp, gate_mlp = jnp.split(mod, 6, axis=-1)
        gate_msa = jnp.tanh(gate_msa)
        gate_mlp = jnp.tanh(gate_mlp)
        h = modulate(rmsnorm(x, g1, D), scale_msa, shift_msa)
        qkv = h @ qkv_w.T + qkv_b
        qkv = qkv.reshape(B, N, 3, HEADS, HEAD_DIM).transpose(2, 0, 3, 1, 4)
        q, k, v = (qkv[0], qkv[1], qkv[2])
        q = rmsnorm(q, qg, HEAD_DIM)
        k = rmsnorm(k, kg, HEAD_DIM)
        q = q * HEAD_DIM ** (-0.5)
        attn = jax.nn.softmax(jnp.einsum('bhqd,bhkd->bhqk', q, k), axis=-1)
        o = jnp.einsum('bhqk,bhkd->bhqd', attn, v)
        o = o.transpose(0, 2, 1, 3).reshape(B, N, D)
        o = o @ proj_w.T + proj_b
        x = x + gate_msa[:, None, :] * o
        h2 = modulate(rmsnorm(x, g2, D), scale_mlp, shift_mlp)
        m = jax.nn.gelu(h2 @ fc1_w.T + fc1_b, approximate=True) @ fc2_w.T + fc2_b
        x = x + gate_mlp[:, None, :] * m
        return x

    def _L2_cond_ref(x, c, w_adaln, b_adaln, w_qkv, b_qkv, w_proj, b_proj, w_gate, w1, b1, w2, b2):
        import jax, jax.numpy as jnp
        import numpy as np
        NUM_HEADS = 16
        NUM_EXPERTS = 4
        TOP_K = 2
        LN_EPS = 1e-06

        def _ln(h):
            mu = jnp.mean(h, axis=-1, keepdims=True)
            var = jnp.var(h, axis=-1, keepdims=True)
            return (h - mu) * jax.lax.rsqrt(var + LN_EPS)

        def _modulate(h, shift, scale):
            return h * (1.0 + scale[:, None, :]) + shift[:, None, :]
        B, N, C = x.shape
        nh = NUM_HEADS
        hd = C // nh
        mod = jax.nn.silu(c) @ w_adaln + b_adaln
        sh_msa, sc_msa, g_msa, sh_mlp, sc_mlp, g_mlp = jnp.split(mod, 6, axis=-1)
        h = _modulate(_ln(x), sh_msa, sc_msa)
        qkv = (h @ w_qkv + b_qkv).reshape(B, N, 3, nh, hd).transpose(2, 0, 3, 1, 4)
        q, k, v = (qkv[0], qkv[1], qkv[2])
        attn = jax.nn.softmax(jnp.einsum('bhqd,bhkd->bhqk', q, k) * hd ** (-0.5), axis=-1)
        o = jnp.einsum('bhqk,bhkd->bhqd', attn, v).transpose(0, 2, 1, 3).reshape(B, N, C)
        o = o @ w_proj + b_proj
        x = x + g_msa[:, None, :] * o
        xn = _modulate(_ln(x), sh_mlp, sc_mlp)
        xf = xn.reshape(-1, C)
        gate_logits = xf @ w_gate
        topk_logits, topk_idx = jax.lax.top_k(gate_logits, TOP_K)
        gates = jax.nn.softmax(topk_logits, axis=-1)
        cw = jnp.sum(jax.nn.one_hot(topk_idx, NUM_EXPERTS, dtype=xf.dtype) * gates[..., None], axis=1)
        hmid = jax.nn.gelu(jnp.einsum('tc,ech->eth', xf, w1) + b1[:, None, :], approximate=True)
        eo = jnp.einsum('eth,ehc->etc', hmid, w2) + b2[:, None, :]
        moe = jnp.einsum('te,etc->tc', cw, eo).reshape(B, N, C)
        return x + g_mlp[:, None, :] * moe

    def _L3_cond_ref(x, c, w_mod, b_mod, w_qkv, b_qkv, g_q, g_k, w_proj, b_proj, w1, b1, w2, b2):
        import jax, jax.numpy as jnp
        import numpy as np
        H = 144
        NH = 16
        HD = H // NH
        MLP = int(H * 4.0)
        EPS = 1e-06

        def _ln(z, scale=None):
            m = jnp.mean(z, axis=-1, keepdims=True)
            v = jnp.mean(jnp.square(z - m), axis=-1, keepdims=True)
            y = (z - m) * jax.lax.rsqrt(v + EPS)
            if scale is not None:
                y = y * scale
            return y
        B, N, _ = x.shape
        mod = jax.nn.swish(c) @ w_mod + b_mod
        sh_msa, sc_msa, g_msa, sh_mlp, sc_mlp, g_mlp = jnp.split(mod, 6, axis=1)
        xn = _ln(x) * (1 + sc_msa[:, None, :]) + sh_msa[:, None, :]
        qkv = xn @ w_qkv + b_qkv
        qkv = qkv.reshape(B, N, 3, NH, HD).transpose(2, 0, 3, 1, 4)
        q, k, v = (qkv[0], qkv[1], qkv[2])
        q = _ln(q, g_q)
        k = _ln(k, g_k)
        attn = jax.nn.softmax(jnp.einsum('bhqd,bhkd->bhqk', q, k) * HD ** (-0.5), axis=-1)
        o = jnp.einsum('bhqk,bhkd->bhqd', attn, v)
        o = o.transpose(0, 2, 1, 3).reshape(B, N, H) @ w_proj + b_proj
        x = x + g_msa[:, None, :] * o
        xn2 = _ln(x) * (1 + sc_mlp[:, None, :]) + sh_mlp[:, None, :]
        h = jax.nn.gelu(xn2 @ w1 + b1, approximate=True)
        x = x + g_mlp[:, None, :] * (h @ w2 + b2)
        return x
    x = _L0_cond_ref(x, cond_1152[:, None, :], L0_cond_W_qkv, L0_cond_b_qkv, L0_cond_W_proj, L0_cond_b_proj, L0_cond_W_fc1, L0_cond_b_fc1, L0_cond_W_fc2, L0_cond_b_fc2, L0_cond_W_ada, L0_cond_b_ada)
    x = _L1_cond_ref(x, cond_1152, L1_cond_g1, L1_cond_g2, L1_cond_qkv_w, L1_cond_qkv_b, L1_cond_qg, L1_cond_kg, L1_cond_proj_w, L1_cond_proj_b, L1_cond_fc1_w, L1_cond_fc1_b, L1_cond_fc2_w, L1_cond_fc2_b, L1_cond_ada_w, L1_cond_ada_b)
    x = _L2_cond_ref(x, cond_1152, L2_cond_w_adaln, L2_cond_b_adaln, L2_cond_w_qkv, L2_cond_b_qkv, L2_cond_w_proj, L2_cond_b_proj, L2_cond_w_gate, L2_cond_w1, L2_cond_b1, L2_cond_w2, L2_cond_b2)
    x = _L3_cond_ref(x, cond_1152, L3_cond_w_mod, L3_cond_b_mod, L3_cond_w_qkv, L3_cond_b_qkv, L3_cond_g_q, L3_cond_g_k, L3_cond_w_proj, L3_cond_b_proj, L3_cond_w1, L3_cond_b1, L3_cond_w2, L3_cond_b2)
    return x

_drawn_inputs = setup_inputs


def setup_inputs(seed=0):
    import zlib

    import numpy as np

    out = dict(_drawn_inputs(seed))
    spreads = {'L0_cond_b_qkv': (0.0, 0.8),
     'L0_cond_b_proj': (0.0, 0.475),
     'L0_cond_b_fc1': (0.0, 0.8),
     'L0_cond_b_fc2': (0.0, 0.51),
     'L0_cond_b_ada': (0.0, 0.494),
     'L1_cond_qkv_b': (0.0, 0.8),
     'L1_cond_proj_b': (0.0, 0.49),
     'L1_cond_fc1_b': (0.0, 0.8),
     'L1_cond_fc2_b': (0.0, 0.423),
     'L1_cond_ada_b': (0.0, 0.588),
     'L2_cond_b_adaln': (0.0, 0.598),
     'L2_cond_b_qkv': (0.0, 0.8),
     'L2_cond_b_proj': (0.0, 0.4),
     'L2_cond_b1': (0.0, 0.8),
     'L2_cond_b2': (0.0, 0.614),
     'L3_cond_b_qkv': (0.0, 2.0),
     'L3_cond_g_q': (1.0, 0.6),
     'L3_cond_g_k': (1.0, 0.6),
     'L3_cond_b_proj': (0.0, 2.0),
     'L3_cond_b1': (0.0, 2.0),
     'L3_cond_b2': (0.0, 2.0)}
    factors = {'L0_cond_W_qkv': 8.0,
     'L0_cond_W_proj': 8.0,
     'L0_cond_W_fc1': 5.462,
     'L0_cond_W_fc2': 5.137,
     'L0_cond_W_ada': 2.737,
     'L1_cond_qkv_w': 8.0,
     'L1_cond_proj_w': 8.0,
     'L1_cond_fc1_w': 5.326,
     'L1_cond_fc2_w': 4.966,
     'L2_cond_w_adaln': 2.907,
     'L2_cond_w_qkv': 8.0,
     'L2_cond_w_proj': 8.0,
     'L2_cond_w_gate': 4.818,
     'L2_cond_w1': 6.904,
     'L2_cond_w2': 6.32,
     'L3_cond_b_mod': 5.075,
     'L3_cond_w_qkv': 2.8,
     'L3_cond_w1': 4.083,
     'L3_cond_w2': 3.045}
    for name, (base, spread) in spreads.items():
        noise = np.random.default_rng([zlib.crc32(name.encode()), seed]).standard_normal(out[name].shape)
        drawn = base * np.exp(spread * noise) if base else spread * noise
        out[name] = jnp.asarray(drawn.astype(out[name].dtype))
    for name, factor in factors.items():
        out[name] = (out[name] * factor).astype(out[name].dtype)
    return out
```

```python
from contextlib import ExitStack

import concourse.bass as bass
from concourse import mybir

ALU = mybir.AluOpType
ACT = mybir.ActivationFunctionType
AX = mybir.AxisListType
F32 = mybir.dt.float32
BF16 = mybir.dt.bfloat16

P = 128
B, L, C = 2, 512, 144
H, HD = 16, 9
TAIL = C - P
ONE = TAIL
FF = 4 * C
FC = -(-FF // P)
FR = FF - (FC - 1) * P
NT = L // P
NK = L // P
G = 4
NG = H // G
NE = 4
SPLIT = 3
BLOCK = 32
MROW = SPLIT * BLOCK
KW = (SPLIT - 1) * HD + BLOCK
KROWS = MROW + 2
OC = 32
STEPS = G * NK
LAYERS = 4
PHASES = LAYERS * B
JOBS = PHASES + 2
LN_EPS = 1e-6
TINY = 1e-24
NORMED = (1, 3)
SHIFT1, SCALE1, SHIFT2, SCALE2 = range(4)
ADA = {SHIFT1: 0, SCALE1: 1, SHIFT2: 3, SCALE2: 4}
GATES = (2, 5)


def has_post(j):
    return j >= 2


def has_pre(j):
    return j < PHASES


def post_layer(j):
    return (j - 2) // 2


def pre_layer(j):
    return j // 2


def is_moe(j):
    return has_post(j) and post_layer(j) == 2


def normed(j):
    return has_pre(j) and pre_layer(j) in NORMED


def start_of(job, j, t):
    return j == job and isinstance(t, int) and t == 0


def experts(j):
    return (NE if is_moe(j) else 1) if has_post(j) else 0


class Steps:

    def __init__(self, sem, per):
        self.sem, self.per = sem, per

    def upto(self, j, t, k):
        return sum(NT * int(self.per(i)) for i in range(j)) + t * int(self.per(j)) + k


class Chain:

    def __init__(self, eng, sem):
        self.eng, self.sem, self.base, self.n = eng, sem, 0, 0

    def __call__(self, ins):
        self.n += 1
        ins.then_inc(self.sem, 1)
        self.eng.wait_ge(self.sem, self.base + self.n)

    def loop(self, i, first, per):
        self.start, self.per = self.base + self.n, per
        self.base, self.n = self.start + (i - first) * per, 0

    def end_loop(self, count):
        assert self.n == self.per, f"links in the loop's body: {self.n}"
        self.base, self.n = self.start + count * self.per, 0


def build(nc, a, out):
    with ExitStack() as ctx:
        def sb(name, shape, dt=F32):
            return ctx.enter_context(nc.sbuf_tensor(name, shape, dt))

        def sem(name):
            return ctx.enter_context(nc.semaphore(name))

        ps = ctx.enter_context(nc.psum_tensor("ps", [P, 8, 512], F32))
        MAXB, KEYB, OUTB, MISC, D0, D1 = 0, 2, 4, 5, 6, 7
        ident = sb("ident", [P, P])
        identb = sb("identb", [P, P], BF16)
        X = sb("X", [P, B * NT * C])
        q_rows = sb("q_rows", [P, B * H * L], BF16)
        k_rows = sb("k_rows", [P, B * H * L], BF16)
        probs = sb("probs", [P, NK, G, L])
        v_all = sb("v_all", [P, B * NT * C])
        v_unit = sb("v_unit", [P, NK, G, OC])
        attn = sb("attn", [P, B * NT * C])
        attn_t = sb("attn_t", [P, L])
        mx = sb("mx", [P, G, NK])
        mx_parts = sb("mx_parts", [P, G, NK, 2], BF16)
        rsum = sb("rsum", [P, NT, G])
        o_tile = sb("o_tile", [P, C])
        oT = sb("oT", [P, P])
        oT_tail = sb("oT_tail", [P, P])
        hT = sb("hT", [P, P])
        hT_tail = sb("hT_tail", [P, P])
        xa = sb("xa", [P, C])
        xm = sb("xm", [P, C])
        xn = sb("xn", [P, C])
        tmp = sb("tmp", [P, C])
        acc = sb("acc", [P, C])
        st = sb("st", [P, 6])
        mv = sb("mv", [P, 2])
        var = sb("var", [P, 1])
        pause = sb("pause", [P, 1])
        rstd = sb("rstd", [P, 1])
        hid = sb("hid", [P, FC, P])
        qk = sb("qk", [P, 2 * H, HD])
        sq = sb("sq", [P, 2 * H, HD])
        rest = sb("rest", [P, 2 * H, HD])
        q_parts = sb("q_parts", [P, H, BLOCK], BF16)
        k_parts = sb("k_parts", [P, H, KW], BF16)
        hsum = sb("hsum", [P, 2 * H])
        hvar = sb("hvar", [P, 2 * H])
        hrstd = sb("hrstd", [P, 2 * H])
        half = sb("half", [P, 2 * H])
        one_gain = sb("one_gain", [P, 4])
        head_gain = sb("head_gain", [P, 2, HD])
        lg = sb("lg", [P, NE])
        neg_top = sb("neg_top", [P, 1])
        above = sb("above", [P, NE, NE])
        ties = sb("ties", [P, NE, NE])
        earlier = sb("earlier", [P, NE, NE])
        rank = sb("rank", [P, NE])
        gex = sb("gex", [P, NE])
        gsum = sb("gsum", [P, 1])
        cw = sb("cw", [P, NE])
        cT = sb("cT", [P, B])
        cT_tail = sb("cT_tail", [P, B])
        sT = sb("sT", [P, B])
        sT_tail = sb("sT_tail", [P, B])
        sB = sb("sB", [P, B, P])
        sB_tail = sb("sB_tail", [P, B, P])
        mod = sb("mod", [P, LAYERS, 4, B])
        mod_tail = sb("mod_tail", [P, LAYERS, 4, B])
        gate = sb("gate", [P, LAYERS, 2, B, C])

        wset = []
        for n in range(3):
            wset.append({
                "qkv": sb(f"wqkv{n}", [P, 3 * C]), "qkv_tail": sb(f"wqkv_tail{n}", [P, 3 * C]),
                "proj": sb(f"wproj{n}", [P, C]), "proj_tail": sb(f"wproj_tail{n}", [P, C]),
            })
            if n < 2:
                wset[n].update({"w1": sb(f"w1_{n}", [P, 1, FF]), "w1_tail": sb(f"w1_tail{n}", [P, 1, FF]),
                                "w2": sb(f"w2_{n}", [P, 1, FC, C])})
        W = [wset[0], wset[1], wset[2], wset[0]]
        big = sb("big", [P, NE * (2 * FF + FC * C)])
        W[2]["w1"] = big[:, 0:NE * FF].rearrange("p (e f) -> p e f", e=NE)
        W[2]["w1_tail"] = big[:, NE * FF:2 * NE * FF].rearrange("p (e f) -> p e f", e=NE)
        W[2]["w2"] = big[:, 2 * NE * FF:].rearrange("p (e c n) -> p e c n", e=NE, c=FC)
        w_gate = sb("w_gate", [P, NE])
        w_gate_tail = sb("w_gate_tail", [P, NE])
        ada = big[:, 0:LAYERS * 6 * C].rearrange("p (l n) -> p l n", l=LAYERS)
        assert LAYERS * 6 * C <= 2 * NE * FF
        ada_tail = probs[:].rearrange("p k g q -> p (k g q)")[:, 0:LAYERS * 6 * C].rearrange(
            "p (l n) -> p l n", l=LAYERS)
        raw = probs[:].rearrange("p k g q -> p (k g q)")[:, LAYERS * 6 * C:]
        raw_qkv = raw[:, 0:4 * C].rearrange("p (r n) -> p r n", r=4)
        raw_proj = raw[:, 4 * C:6 * C].rearrange("p (r n) -> p r n", r=2)
        raw2 = k_rows[:].bitcast(F32)
        raw_fc1 = raw2[:, 0:5 * C].rearrange("p (r n) -> p r n", r=5)
        raw_fc2 = raw2[:, 5 * C:5 * C + 2 * FF].rearrange("p (r n) -> p r n", r=2)
        raw_ada = raw2[:, 13 * C:20 * C].rearrange("p (r n) -> p r n", r=7)

        x_in = sem("x_in")
        c_in = sem("c_in")
        small_in = sem("small_in")
        ada_in = sem("ada_in")
        raw_in = sem("raw_in")
        w_in = [sem(f"w{n}_in") for n in range(LAYERS)]
        out_stored = sem("out_stored")
        ident_made = sem("ident_made")
        presets = sem("presets")
        pool_presets = sem("pool_presets")
        half_ready = sem("half_ready")
        silu_exp = sem("silu_exp")
        tail_set = sem("tail_set")
        silu_ready = sem("silu_ready")
        turn_psum = sem("turn_psum")
        turn_sbuf = sem("turn_sbuf")
        mods_psum = sem("mods_psum")
        mods_ready = sem("mods_ready")
        gates_psum = sem("gates_psum")
        gates_ready = sem("gates_ready")
        wq_scaled = sem("wq_scaled")
        vchain = sem("vchain")
        pchain = sem("pchain")

        key_scores = sem("key_scores")
        exp_done = sem("exp_done")
        max_scores = sem("max_scores")
        max_taken = sem("max_taken")
        max_split = sem("max_split")
        max_rows = sem("max_rows")
        max_rows_stored = sem("max_rows_stored")
        v_staged = sem("v_staged")
        pv_done = sem("pv_done")
        attn_t_ready = sem("attn_t_ready")
        attn_psum = sem("attn_psum")
        attn_done = sem("attn_done")

        def unit(p, u):
            return p * NG + u

        norms = lambda j: has_post(j) + has_pre(j)
        o_staged = Steps(sem("o_staged"), has_post)
        oT_psum = Steps(sem("oT_psum"), has_post)
        oT_ready = Steps(sem("oT_ready"), has_post)
        proj_psum = Steps(sem("proj_psum"), has_post)
        var_ready = Steps(sem("var_ready"), norms)
        rstd_ready = Steps(sem("rstd_ready"), norms)
        x_normed = Steps(sem("x_normed"), norms)
        xT_psum = Steps(sem("xT_psum"), norms)
        hT_ready = Steps(sem("hT_ready"), norms)
        logits_psum = Steps(sem("logits_psum"), is_moe)
        logits_read = Steps(sem("logits_read"), is_moe)
        top_ready = Steps(sem("top_ready"), is_moe)
        gate_exp = Steps(sem("gate_exp"), is_moe)
        hid_psum = Steps(sem("hid_psum"), experts)
        hid_ready = Steps(sem("hid_ready"), experts)
        mlp_psum = Steps(sem("mlp_psum"), experts)
        mlp_read = Steps(sem("mlp_read"), experts)
        x_stored = Steps(sem("x_stored"), has_post)
        qkv_psum = Steps(sem("qkv_psum"), has_pre)
        v_stored = Steps(sem("v_stored"), has_pre)
        qk_centred = Steps(sem("qk_centred"), lambda j: normed(j) and pre_layer(j) == 3)
        qk_squared = Steps(sem("qk_squared"), normed)
        hvar_ready = Steps(sem("hvar_ready"), normed)
        hrstd_ready = Steps(sem("hrstd_ready"), normed)
        qk_ready = Steps(sem("qk_ready"), normed)
        high_ready = Steps(sem("high_ready"), has_pre)
        parts_ready = Steps(sem("parts_ready"), has_pre)
        rows_psum = Steps(sem("rows_psum"), lambda j: 2 * NG * has_pre(j))
        q_stored = Steps(sem("q_stored"), lambda j: NG * has_pre(j))
        k_stored = Steps(sem("k_stored"), lambda j: NG * has_pre(j))

        block = ctx.enter_context(nc.Block())

        turns = []
        for r in range(4):
            n = min(P, 3 * C - P * r)
            turns.append((raw_qkv[0:n, r, 0:P], W[1]["qkv"][:, P * r:P * r + n]))
            turns.append((raw_qkv[0:n, r, P:C], W[1]["qkv_tail"][0:TAIL, P * r:P * r + n]))
        for r in range(2):
            n = min(P, C - P * r)
            turns.append((raw_proj[0:n, r, 0:P], W[1]["proj"][:, P * r:P * r + n]))
            turns.append((raw_proj[0:n, r, P:C], W[1]["proj_tail"][0:TAIL, P * r:P * r + n]))
        for r in range(5):
            n = min(P, FF - P * r)
            turns.append((raw_fc1[0:n, r, 0:P], W[1]["w1"][:, 0, P * r:P * r + n]))
            turns.append((raw_fc1[0:n, r, P:C], W[1]["w1_tail"][0:TAIL, 0, P * r:P * r + n]))
        for c in range(FC):
            m = min(P, FF - P * c)
            for r in range(2):
                n = min(P, C - P * r)
                turns.append((raw_fc2[0:n, r, P * c:P * c + m], W[1]["w2"][0:m, 0, c, P * r:P * r + n]))
        for r in range(7):
            n = min(P, 6 * C - P * r)
            turns.append((raw_ada[0:n, r, 0:P], ada[:, 1, P * r:P * r + n]))
            turns.append((raw_ada[0:n, r, P:C], ada_tail[0:TAIL, 1, P * r:P * r + n]))
        gate_list = [(l, g, b) for l in range(LAYERS) for g in range(2) for b in range(B)]

        def rows_of(rows, j, t, g):
            n = (j % B) * H + g * G
            return rows[0:MROW].rearrange("p (n l) -> p n l", l=L)[:, n:n + G, bass.ds(t * P, P)]

        def group_of(m, p, u):
            n = (p % B) * NT
            return m[:].rearrange("p (t h d) -> p t h d", t=B * NT, d=HD)[:, n:n + NT, bass.ds(u * G, G), :]

        @block.sync
        def _(sp):
            n_small = [0]

            def rows(dst, src, s):
                sp.dma_start(dst, src).then_inc(s, 16)

            sp.dma_start(X[:].rearrange("p (t c) -> p t c", c=C),
                         a["x"].rearrange("b (t p) c -> p (b t) c", p=P)).then_inc(x_in, 16)
            cond = a["cond_1152"].rearrange("b c -> c b")
            sp.dma_start(cT[:], cond[0:P], allow_slow_non_contiguous=True).then_inc(c_in, 16)
            sp.dma_start(cT_tail[0:TAIL, :], cond[P:C], allow_slow_non_contiguous=True).then_inc(c_in, 16)
            ada_w = {0: "L0_cond_W_ada", 2: "L2_cond_w_adaln", 3: "L3_cond_w_mod"}
            ada_b = ["L0_cond_b_ada", "L1_cond_ada_b", "L2_cond_b_adaln", "L3_cond_b_mod"]
            rows(raw_ada[:, 0:6], a["L1_cond_ada_w"][0:6 * P].rearrange("(r p) n -> p r n", p=P), raw_in)
            rows(raw_ada[0:6 * C - 6 * P, 6], a["L1_cond_ada_w"][6 * P:6 * C], raw_in)
            for l in range(LAYERS):
                if l != 1:
                    rows(ada[:, l], a[ada_w[l]][0:P], ada_in)
                    rows(ada_tail[0:TAIL, l], a[ada_w[l]][P:C], ada_in)
                rows(ada_tail[ONE:ONE + 1, l], a[ada_b[l]].rearrange("(o n) -> o n", o=1), ada_in)
            for n, g in enumerate(("g1", "g2", "qg", "kg")):
                rows(one_gain[:, n:n + 1], a["L1_cond_" + g].rearrange("(o n) -> o n", o=1).broadcast_to([P, 1]), small_in)
            rows(head_gain[:, 0, :], a["L3_cond_g_q"].rearrange("(o n) -> o n", o=1).broadcast_to([P, HD]), small_in)
            rows(head_gain[:, 1, :], a["L3_cond_g_k"].rearrange("(o n) -> o n", o=1).broadcast_to([P, HD]), small_in)

            def flat(name):
                return a[name].rearrange("(o n) -> o n", o=1)

            def load(l, qkv, bqkv, proj, bproj, w1=None, b1=None, w2=None, b2=None):
                w, s = W[l], w_in[l]
                rows(w["qkv"][:], a[qkv][0:P], s)
                rows(w["qkv_tail"][0:TAIL], a[qkv][P:C], s)
                rows(w["qkv_tail"][ONE:ONE + 1], flat(bqkv), s)
                rows(w["proj"][:], a[proj][0:P], s)
                rows(w["proj_tail"][0:TAIL], a[proj][P:C], s)
                rows(w["proj_tail"][ONE:ONE + 1], flat(bproj), s)
                if w1:
                    rows(w["w1"][:, 0], a[w1][0:P], s)
                    rows(w["w1_tail"][0:TAIL, 0], a[w1][P:C], s)
                    rows(w["w1_tail"][ONE:ONE + 1, 0], flat(b1), s)
                    rows(w["w2"][:, 0, 0:FC - 1], a[w2][0:(FC - 1) * P].rearrange("(c p) n -> p c n", p=P), s)
                    rows(w["w2"][0:FR, 0, FC - 1], a[w2][(FC - 1) * P:FF], s)
                    rows(w["w2"][FR:FR + 1, 0, FC - 1], flat(b2), s)

            load(0, *["L0_cond_" + n for n in ("W_qkv", "b_qkv", "W_proj", "b_proj",
                                               "W_fc1", "b_fc1", "W_fc2", "b_fc2")])
            w = W[1]
            rows(raw_qkv[:, 0:3], a["L1_cond_qkv_w"][0:3 * P].rearrange("(r p) n -> p r n", p=P), raw_in)
            rows(raw_qkv[0:3 * C - 3 * P, 3], a["L1_cond_qkv_w"][3 * P:3 * C], raw_in)
            rows(raw_proj[:, 0], a["L1_cond_proj_w"][0:P], raw_in)
            rows(raw_proj[0:TAIL, 1], a["L1_cond_proj_w"][P:C], raw_in)
            rows(raw_fc1[:, 0:4], a["L1_cond_fc1_w"][0:4 * P].rearrange("(r p) n -> p r n", p=P), raw_in)
            rows(raw_fc1[0:FR, 4], a["L1_cond_fc1_w"][4 * P:FF], raw_in)
            rows(raw_fc2[:, 0], a["L1_cond_fc2_w"][0:P], raw_in)
            rows(raw_fc2[0:TAIL, 1], a["L1_cond_fc2_w"][P:C], raw_in)
            rows(w["qkv_tail"][ONE:ONE + 1], flat("L1_cond_qkv_b"), w_in[1])
            rows(w["proj_tail"][ONE:ONE + 1], flat("L1_cond_proj_b"), w_in[1])
            rows(w["w1_tail"][ONE:ONE + 1, 0], flat("L1_cond_fc1_b"), w_in[1])
            rows(w["w2"][FR:FR + 1, 0, FC - 1], flat("L1_cond_fc2_b"), w_in[1])
            load(2, *["L2_cond_" + n for n in ("w_qkv", "b_qkv", "w_proj", "b_proj")])
            rows(w_gate[:], a["L2_cond_w_gate"][0:P], w_in[2])
            rows(w_gate_tail[0:TAIL], a["L2_cond_w_gate"][P:C], w_in[2])
            sp.wait_ge(mods_psum, 1)
            sp.wait_ge(gates_psum, len(gate_list))
            w = W[2]
            w1, b1 = a["L2_cond_w1"], a["L2_cond_b1"]
            w2, b2 = a["L2_cond_w2"], a["L2_cond_b2"]
            rows(w["w1"], w1[:, 0:P].rearrange("e p n -> p e n"), w_in[2])
            rows(w["w1_tail"][0:TAIL], w1[:, P:C].rearrange("e p n -> p e n"), w_in[2])
            rows(w["w1_tail"][ONE:ONE + 1], b1.rearrange("(o e) n -> o e n", o=1), w_in[2])
            for e in range(NE):
                rows(w["w2"][:, e, 0:FC - 1], w2[e, 0:(FC - 1) * P].rearrange("(c p) n -> p c n", p=P), w_in[2])
            rows(w["w2"][0:FR, :, FC - 1], w2[:, (FC - 1) * P:FF].rearrange("e p n -> p e n"), w_in[2])
            rows(w["w2"][FR:FR + 1, :, FC - 1], b2.rearrange("(o e) n -> o e n", o=1), w_in[2])
            sp.wait_ge(mlp_psum.sem, mlp_psum.upto(3, NT, 0))
            load(3, *["L3_cond_" + n for n in ("w_qkv", "b_qkv", "w_proj", "b_proj", "w1", "b1", "w2", "b2")])
            y = out.rearrange("b (t p) c -> p (b t) c", p=P)
            for j in (PHASES, PHASES + 1):
                for t in range(NT):
                    sp.wait_ge(x_stored.sem, x_stored.upto(j, t, 1))
                    n = (j % B) * NT + t
                    sp.dma_start(y[:, n], X[:, n * C:(n + 1) * C]).then_inc(out_stored, 16)
            sp.wait_ge(out_stored, 16 * B * NT)

        W_LOADS = [16 * 12, 16 * 4, 16 * (6 + 2 + 3 + NE + 2), 16 * 12]
        RAW_LOADS = 16 * 10
        ADA_LOADS = 16 * (2 * 3 + LAYERS)

        def slots(eng, slot, chain=None, links=None):
            def loop(p, j, first, count, parts):
                with eng.Fori(first, first + count) as s:
                    if chain:
                        chain.loop(s, first, links(j, *parts))
                    slot(p, j, s, *parts)
                if chain:
                    chain.end_loop(count)

            slot(0, 0, 0, False, False, True)
            loop(0, 0, 1, NT - 1, (False, False, True))
            for p in range(PHASES):
                slot(p, p + 1, 0, False, True, True)
                loop(p, p + 1, 1, NG - 1, (True, True, True))
                slot(p, p + 1, NG, True, False, False)
            loop(PHASES, JOBS - 1, 0, NT, (False, False, True))

        AT_O, AT_PROJ, AT_X1, AT_FC1, AT_FC2, AT_X2, AT_QKV, AT_ROWS = 0, 1, 4, 6, 8, 10, 12, 15

        @block.tensor
        def _(pe):
            pe.wait_ge(ident_made, 1)
            pe.wait_ge(raw_in, RAW_LOADS)
            for n, (src, dst) in enumerate(turns):
                if n >= 8:
                    pe.wait_ge(turn_sbuf, n - 7)
                k, m = src.shape[0], src.shape[1]
                pe.transpose(ps[0:m, n % 8, 0:k], src, ident[0:k, 0:k]).then_inc(turn_psum, 1)
            pe.wait_ge(turn_sbuf, len(turns))
            pe.wait_ge(ada_in, ADA_LOADS)
            pe.wait_ge(silu_ready, 2)
            for l in range(LAYERS):
                for i in range(4):
                    c0, o = ADA[i] * C, (l * 4 + i) * B
                    pe.matmul(ps[:, 0, o:o + B], ada[:, l, c0:c0 + P], sT[:], start=True, stop=False)
                    pe.matmul(ps[:, 0, o:o + B], ada_tail[0:ONE + 1, l, c0:c0 + P], sT_tail[0:ONE + 1, :],
                              start=False, stop=True)
                    pe.matmul(ps[0:TAIL, 1, o:o + B], ada[:, l, c0 + P:c0 + C], sT[:], start=True, stop=False)
                    last = pe.matmul(ps[0:TAIL, 1, o:o + B], ada_tail[0:ONE + 1, l, c0 + P:c0 + C],
                                     sT_tail[0:ONE + 1, :], start=False, stop=True)
            last.then_inc(mods_psum, 1)
            for n, (l, g, b) in enumerate(gate_list):
                if n >= 6:
                    pe.wait_ge(gates_ready, n - 5)
                c0, bank = GATES[g] * C, 2 + n % 6
                pe.matmul(ps[:, bank, 0:C], sB[:, b], ada[:, l, c0:c0 + C], start=True, stop=False)
                pe.matmul(ps[:, bank, 0:C], sB_tail[0:ONE + 1, b], ada_tail[0:ONE + 1, l, c0:c0 + C],
                          start=False, stop=True).then_inc(gates_psum, 1)
            pe.wait_ge(mods_ready, 1)
            pe.wait_ge(gates_ready, len(gate_list))
            pe.wait_ge(presets, 1)
            pe.wait_ge(pool_presets, 1)

            def score_keys(p, u, n):
                kt, h = divmod(n, G)
                if kt == 0:
                    pe.wait_ge(max_rows_stored, unit(p, u) * G + h + 1)
                pe.wait_ge(exp_done, unit(p, u) * STEPS + n + 1)
                head = ((p % B) * H + u * G + h) * L
                pe.matmul(ps[:, KEYB + n % 2], k_rows[0:KROWS, bass.ds(head + kt * P, P)],
                          q_rows[0:KROWS, bass.ds(head, L)], start=True, stop=True).then_inc(key_scores, 1)

            def score_queries(p, u, n):
                h, qt = divmod(n, NT)
                pe.wait_ge(max_taken, unit(p, u) * STEPS + n + 1)
                head = ((p % B) * H + u * G + h) * L
                pe.matmul(ps[:, MAXB + n % 2], q_rows[0:MROW, bass.ds(head + qt * P, P)],
                          k_rows[0:MROW, bass.ds(head, L)], start=True, stop=True).then_inc(max_scores, 1)

            def turn_max(p, s, h, A):
                pe.wait_ge(max_split, unit(p, s) * G + h + 1)
                if h == 0:
                    pe.wait_ge(attn_done, unit(p, s) + (not A))
                else:
                    pe.wait_ge(max_rows_stored, unit(p, s) * G + h)
                for qt in range(NT):
                    last = pe.matmul(ps[MROW:MROW + 2, MISC, qt * P:(qt + 1) * P], mx_parts[:, h, qt, :],
                                     identb[:], start=True, stop=True)
                last.then_inc(max_rows, 1)

            def values(p, u, kt):
                pe.wait_ge(exp_done, unit(p, u) * STEPS + (kt + 1) * G + 2)
                if kt == 0:
                    pe.wait_ge(v_staged, unit(p, u) + 1)
                    pe.wait_ge(attn_t_ready, unit(p, u) + 1)
                for h in range(G):
                    last = pe.matmul(ps[OC * h:OC * (h + 1), OUTB], v_unit[:, kt, h, :], probs[:, kt, h, :],
                                     start=(kt == 0), stop=(kt == NK - 1))
                if kt == NK - 1:
                    last.then_inc(pv_done, 1)

            def turn_attn(p, u, M):
                pe.wait_ge(attn_t_ready, unit(p, u) + 2)
                pe.wait_ge(max_rows_stored, (unit(p, u) + (2 if M else 1)) * G)
                if not M:
                    pe.wait_ge(attn_done, unit(p, u) + 1)
                for qt in range(NT):
                    last = pe.transpose(ps[:, MISC, qt * P:(qt + 1) * P], attn_t[:, qt * P:(qt + 1) * P], ident[:])
                last.then_inc(attn_psum, 1)

            def turn_x(j, t, k):
                pe.wait_ge(x_normed.sem, x_normed.upto(j, t, k))
                pe.transpose(ps[:, D0, 0:P], xn[:, 0:P], ident[:])
                pe.transpose(ps[0:TAIL, D0, P:2 * P], xn[:, P:C], ident[:]).then_inc(xT_psum.sem, 1)

            def dense(n, j, t):
                lp, lq = post_layer(j), pre_layer(j)
                if n == AT_O and has_post(j):
                    pe.wait_ge(o_staged.sem, o_staged.upto(j, t, 1))
                    if j <= PHASES:
                        pe.wait_ge(q_stored.sem, q_stored.upto(j, t, 0))
                    pe.transpose(ps[:, D0, 0:P], o_tile[:, 0:P], ident[:])
                    pe.transpose(ps[0:TAIL, D0, P:2 * P], o_tile[:, P:C], ident[:]).then_inc(oT_psum.sem, 1)
                if n == AT_PROJ and has_post(j):
                    if j == 2:
                        pe.wait_ge(w_in[0], W_LOADS[0])
                    if lp in (1, 2, 3) and j % 2 == 0:
                        pe.wait_ge(w_in[lp], W_LOADS[lp])
                    pe.wait_ge(oT_ready.sem, oT_ready.upto(j, t, 1))
                    pe.wait_ge(k_stored.sem, k_stored.upto(j, t, 0))
                    if not start_of(2, j, t):
                        pe.wait_ge(mlp_read.sem, mlp_read.upto(j, t, 0))
                    w = W[lp]
                    pe.matmul(ps[:, D1, 0:C], oT[:], w["proj"][:], start=True, stop=False)
                    pe.matmul(ps[:, D1, 0:C], oT_tail[0:ONE + 1, :], w["proj_tail"][0:ONE + 1, :],
                              start=False, stop=True).then_inc(proj_psum.sem, 1)
                if n == AT_X1 and has_post(j):
                    turn_x(j, t, 1)
                if n == AT_FC1 and has_post(j):
                    pe.wait_ge(hT_ready.sem, hT_ready.upto(j, t, 1))
                    if is_moe(j):
                        pe.matmul(ps[:, D1, 0:NE], hT[:], w_gate[:], start=True, stop=False)
                        pe.matmul(ps[:, D1, 0:NE], hT_tail[0:TAIL, :], w_gate_tail[0:TAIL, :],
                                  start=False, stop=True).then_inc(logits_psum.sem, 1)
                        pe.wait_ge(logits_read.sem, logits_read.upto(j, t, 1))
                    fc1(j, t, 0)
                if n == AT_FC2 and has_post(j):
                    fc2(j, t, 0)
                    if is_moe(j):
                        for e in range(1, NE):
                            fc1(j, t, e)
                            fc2(j, t, e)
                if n == AT_X2 and has_pre(j):
                    if not has_post(j) and not start_of(0, j, t):
                        pe.wait_ge(q_stored.sem, q_stored.upto(j, t, 0))
                    turn_x(j, t, 1 + has_post(j))
                if n == AT_QKV and has_pre(j):
                    if j == 0:
                        pe.wait_ge(w_in[0], W_LOADS[0])
                        pe.wait_ge(wq_scaled, 1)
                    if j == 2:
                        pe.wait_ge(w_in[1], W_LOADS[1])
                    if j == 4:
                        pe.wait_ge(wq_scaled, 2)
                    if j == 6:
                        pe.wait_ge(w_in[3], W_LOADS[3])
                    pe.wait_ge(hT_ready.sem, hT_ready.upto(j, t, 1 + has_post(j)))
                    if not has_post(j) and not start_of(0, j, t):
                        pe.wait_ge(k_stored.sem, k_stored.upto(j, t, 0))
                    w = W[lq]
                    pe.matmul(ps[:, D1, 0:3 * C], hT[:], w["qkv"][:], start=True, stop=False)
                    pe.matmul(ps[:, D1, 0:3 * C], hT_tail[0:ONE + 1, :], w["qkv_tail"][0:ONE + 1, :],
                              start=False, stop=True).then_inc(qkv_psum.sem, 1)
                if n == AT_ROWS and has_pre(j):
                    pe.wait_ge(parts_ready.sem, parts_ready.upto(j, t, 1))
                    for g in range(NG):
                        if g:
                            pe.wait_ge(q_stored.sem, q_stored.upto(j, t, g))
                        for h in range(G):
                            for i in range(SPLIT):
                                last = pe.matmul(ps[i * BLOCK:(i + 1) * BLOCK, D0, h * P:(h + 1) * P],
                                                 q_parts[:, g * G + h, :], identb[:], start=True, stop=True)
                        last.then_inc(rows_psum.sem, 1)
                        if g:
                            pe.wait_ge(k_stored.sem, k_stored.upto(j, t, g))
                        for h in range(G):
                            for i in range(SPLIT):
                                last = pe.matmul(ps[i * BLOCK:(i + 1) * BLOCK, D1, h * P:(h + 1) * P],
                                                 k_parts[:, g * G + h, i * HD:i * HD + BLOCK], identb[:],
                                                 start=True, stop=True)
                        last.then_inc(rows_psum.sem, 1)

            def fc1(j, t, e):
                w = W[post_layer(j)]
                if e:
                    pe.wait_ge(mlp_read.sem, mlp_read.upto(j, t, e))
                for c in range(FC):
                    m = min(P, FF - c * P)
                    o = ps[0:m, D1, c * P:(c + 1) * P] if c < FC - 1 else ps[0:m, D0, 2 * P:3 * P]
                    pe.matmul(o, w["w1"][:, e, c * P:c * P + m], hT[:], start=True, stop=False)
                    last = pe.matmul(o, w["w1_tail"][0:ONE + 1, e, c * P:c * P + m], hT_tail[0:ONE + 1, :],
                                     start=False, stop=True)
                last.then_inc(hid_psum.sem, 1)

            def fc2(j, t, e):
                w = W[post_layer(j)]
                pe.wait_ge(hid_ready.sem, hid_ready.upto(j, t, e + 1))
                for c in range(FC):
                    k = P if c < FC - 1 else FR + 1
                    last = pe.matmul(ps[:, D1, 0:C], hid[0:k, c, :], w["w2"][0:k, e, c, :],
                                     start=(c == 0), stop=(c == FC - 1))
                last.then_inc(mlp_psum.sem, 1)

            def slot(p, j, s, A, M, D):
                if M and isinstance(s, int) and s == 0:
                    pe.wait_ge(q_stored.sem, q_stored.upto(p, NT, 0))
                    pe.wait_ge(k_stored.sem, k_stored.upto(p, NT, 0))
                for n in range(STEPS):
                    if A:
                        score_keys(p, s - 1, n)
                    if M:
                        score_queries(p, s, n)
                    if A and n % G == 1 and n > G:
                        values(p, s - 1, n // G - 1)
                    if M and n % NT == 1 and n > NT:
                        turn_max(p, s, n // NT - 1, A)
                    if D:
                        dense(n, j, s)
                if A:
                    values(p, s - 1, NK - 1)
                if M:
                    turn_max(p, s, G - 1, A)
                if A:
                    turn_attn(p, s - 1, M)

            slots(pe, slot)

        @block.scalar
        def _(act):
            act.wait_ge(c_in, 32)
            act.wait_ge(tail_set, 1)
            act.activation(sT[:], cT[:], ACT.Exp, scale=-1.0)
            act.activation(sT_tail[0:TAIL], cT_tail[0:TAIL], ACT.Exp, scale=-1.0).then_inc(silu_exp, 1)
            for n, (l, g, b) in enumerate(gate_list):
                act.wait_ge(gates_psum, n + 1)
                act.activation(gate[:, l, g, b], ps[:, 2 + n % 6, 0:C],
                               ACT.Tanh if l == 1 else ACT.Copy).then_inc(gates_ready, 1)
            act.wait_ge(mods_ready, 1)
            act.wait_ge(presets, 1)

            def exps(p, u, n):
                act.wait_ge(key_scores, unit(p, u) * STEPS + n + 1)
                act.activation(probs[:, n // G, n % G], ps[:, KEYB + n % 2], ACT.Exp).then_inc(exp_done, 1)

            def store_max(p, s, h):
                act.wait_ge(max_rows, unit(p, s) * G + h + 1)
                head = ((p % B) * H + s * G + h) * L
                act.activation(q_rows[MROW:MROW + 2, bass.ds(head, L)], ps[MROW:MROW + 2, MISC],
                               ACT.Copy).then_inc(max_rows_stored, 1)

            def modulate(j, t, k, l, first):
                b = j % B
                act.wait_ge(xT_psum.sem, xT_psum.upto(j, t, k))
                act.activation(hT[:], ps[:, D0, 0:P], ACT.Identity,
                               bias=mod[:, l, first, b:b + 1], scale=mod[:, l, first + 1, b:b + 1])
                act.activation(hT_tail[0:TAIL], ps[0:TAIL, D0, P:2 * P], ACT.Identity,
                               bias=mod_tail[0:TAIL, l, first, b:b + 1],
                               scale=mod_tail[0:TAIL, l, first + 1, b:b + 1]).then_inc(hT_ready.sem, 1)

            def gelu(j, t, e):
                act.wait_ge(hid_psum.sem, hid_psum.upto(j, t, e + 1))
                act.activation(hid[:, 0:FC - 1].rearrange("p c q -> p (c q)"), ps[:, D1], ACT.Gelu_apprx_tanh)
                act.activation(hid[0:FR, FC - 1], ps[0:FR, D0, 2 * P:3 * P],
                               ACT.Gelu_apprx_tanh).then_inc(hid_ready.sem, 1)

            def dense(n, j, t):
                if n == AT_O and has_post(j):
                    act.wait_ge(oT_psum.sem, oT_psum.upto(j, t, 1))
                    act.activation(oT[:], ps[:, D0, 0:P], ACT.Copy)
                    act.activation(oT_tail[0:TAIL], ps[0:TAIL, D0, P:2 * P], ACT.Copy).then_inc(oT_ready.sem, 1)
                if n == AT_X1 and has_post(j):
                    modulate(j, t, 1, post_layer(j), SHIFT2)
                if n == AT_FC1 and has_post(j):
                    if is_moe(j):
                        act.wait_ge(top_ready.sem, top_ready.upto(j, t, 1))
                        act.activation(gex[:], lg[:], ACT.Exp, bias=neg_top[:]).then_inc(gate_exp.sem, 1)
                    gelu(j, t, 0)
                if n == AT_FC2 and is_moe(j):
                    for e in range(1, NE):
                        gelu(j, t, e)
                if n == AT_X2 and has_pre(j):
                    modulate(j, t, 1 + has_post(j), pre_layer(j), SHIFT1)
                if n == AT_QKV and has_pre(j):
                    act.wait_ge(qkv_psum.sem, qkv_psum.upto(j, t, 1))
                    act.activation(v_all[:, bass.ds(((j % B) * NT + t) * C, C)], ps[:, D1, 2 * C:3 * C],
                                   ACT.Copy).then_inc(v_stored.sem, 1)
                    src = ps[:, D1, 0:2 * C].rearrange("p (h d) -> p h d", d=HD)
                    if normed(j):
                        if pre_layer(j) == 3:
                            act.wait_ge(qk_centred.sem, qk_centred.upto(j, t, 1))
                            src = qk[:]
                        act.activation(sq[:], src, ACT.Square).then_inc(qk_squared.sem, 1)
                        act.wait_ge(qk_ready.sem, qk_ready.upto(j, t, 1))
                        src = qk[:]
                    act.activation(q_parts[:, :, 0:HD], src[:, 0:H], ACT.Copy)
                    act.activation(k_parts[:, :, 0:HD], src[:, H:2 * H], ACT.Copy).then_inc(high_ready.sem, 1)
                if n == AT_ROWS and has_pre(j):
                    for g in range(NG):
                        act.wait_ge(rows_psum.sem, rows_psum.upto(j, t, 2 * g + 1))
                        act.activation(rows_of(q_rows, j, t, g), ps[0:MROW, D0].rearrange("p (h q) -> p h q", h=G),
                                       ACT.Copy).then_inc(q_stored.sem, 1)

            def slot(p, j, s, A, M, D):
                for n in range(STEPS):
                    if A:
                        exps(p, s - 1, n)
                    if M and n % NT == 1 and n > NT:
                        store_max(p, s, n // NT - 1)
                    if D:
                        dense(n, j, s)
                if A:
                    act.wait_ge(pv_done, unit(p, s - 1) + 2)
                    act.activation(attn_t[:], ps[:, OUTB], ACT.Copy).then_inc(attn_t_ready, 1)
                if M:
                    store_max(p, s, G - 1)

            slots(act, slot)

        @block.vector
        def _(dve):
            link = Chain(dve, vchain)
            dve.memset(q_parts[:], 0.0)
            dve.memset(k_parts[:], 0.0)
            dve.memset(oT_tail[:], 1.0)
            dve.memset(hT_tail[:], 1.0)
            dve.memset(half[:], -0.5).then_inc(half_ready, 1)
            dve.memset(sT_tail[:], 1.0).then_inc(tail_set, 1)
            dve.memset(hid[:], 1.0).then_inc(presets, 1)
            dve.memset(mx[:], 0.0).then_inc(exp_done, 1)
            dve.memset(st[:], 0.0).then_inc(exp_done, 1)
            dve.memset(mv[:], 0.0).then_inc(max_taken, 1)
            dve.memset(var[:], 0.0).then_inc(max_taken, 1)
            dve.memset(rstd[:], 0.0).then_inc(attn_t_ready, 1)
            dve.memset(rank[:], 0.0).then_inc(attn_done, 1)
            dve.memset(gsum[:], 0.0).then_inc(pv_done, 1)
            dve.wait_ge(silu_exp, 1)
            link(dve.tensor_scalar(sT[:], sT[:], 1.0, None, ALU.add))
            link(dve.tensor_scalar(sT_tail[0:TAIL], sT_tail[0:TAIL], 1.0, None, ALU.add))
            link(dve.reciprocal(sT[:], sT[:]))
            link(dve.reciprocal(sT_tail[0:TAIL], sT_tail[0:TAIL]))
            link(dve.tensor_tensor(sT[:], sT[:], cT[:], ALU.mult))
            link(dve.tensor_tensor(sT_tail[0:TAIL], sT_tail[0:TAIL], cT_tail[0:TAIL], ALU.mult))
            dve.tensor_copy(sB[:], sT[:].unsqueeze(2).broadcast_to([P, B, P])).then_inc(silu_ready, 1)
            dve.tensor_copy(sB_tail[0:ONE + 1], sT_tail[0:ONE + 1].unsqueeze(2).broadcast_to([ONE + 1, B, P])
                            ).then_inc(silu_ready, 1)
            dve.wait_ge(w_in[0], W_LOADS[0])
            dve.tensor_scalar(W[0]["qkv"][:, 0:C], W[0]["qkv"][:, 0:C], HD ** -0.5, None, ALU.mult)
            dve.tensor_scalar(W[0]["qkv_tail"][0:ONE + 1, 0:C], W[0]["qkv_tail"][0:ONE + 1, 0:C], HD ** -0.5,
                              None, ALU.mult).then_inc(wq_scaled, 1)
            for n, (src, dst) in enumerate(turns):
                dve.wait_ge(turn_psum, n + 1)
                k, m = src.shape[0], src.shape[1]
                dve.tensor_copy(dst, ps[0:m, n % 8, 0:k]).then_inc(turn_sbuf, 1)
            dve.wait_ge(small_in, 16 * 6)
            link(dve.tensor_scalar(one_gain[:, 0:2], one_gain[:, 0:2], C ** 0.5, None, ALU.mult))
            link(dve.tensor_scalar(one_gain[:, 3:4], one_gain[:, 3:4], HD ** 0.5, None, ALU.mult))
            link(dve.tensor_scalar(head_gain[:, 0], head_gain[:, 0], HD ** -0.5, None, ALU.mult))
            dve.wait_ge(mods_psum, 1)
            for m, r, bank in ((mod, P, 0), (mod_tail, TAIL, 1)):
                link(dve.tensor_copy(m[0:r].rearrange("p l i b -> p (l i b)"), ps[0:r, bank, 0:LAYERS * 4 * B]))
                for i in (SCALE1, SCALE2):
                    link(dve.tensor_scalar(m[0:r, :, i], m[0:r, :, i], 1.0, None, ALU.add))
                    g = 0 if i == SCALE1 else 1
                    link(dve.tensor_scalar(m[0:r, 1, i], m[0:r, 1, i], one_gain[0:r, g:g + 1], None, ALU.mult))
            dve.tensor_copy(neg_top[:], var[:]).then_inc(mods_ready, 1)
            dve.wait_ge(x_in, 16)
            dve.wait_ge(pool_presets, 1)

            def maxima(p, s, n):
                h, qt = divmod(n, NT)
                dve.wait_ge(max_scores, unit(p, s) * STEPS + n + 1)
                dve.tensor_reduce(mx[:, h, qt:qt + 1], ps[:, MAXB + n % 2], AX.X, ALU.max).then_inc(max_taken, 1)

            def split_max(p, s, h):
                dve.wait_ge(max_taken, unit(p, s) * STEPS + (h + 1) * NT + 2)
                link(dve.tensor_copy(mx_parts[:, h, :, 0], mx[:, h]))
                dve.tensor_tensor(mx_parts[:, h, :, 1], mx[:, h], mx_parts[:, h, :, 0],
                                  ALU.subtract).then_inc(max_split, 1)

            def normalize(p, u):
                dve.wait_ge(attn_psum, unit(p, u) + 1)
                o = ps[:, MISC].rearrange("p (t h r) -> p t h r", t=NT, h=G)
                link(dve.reciprocal(rsum[:], o[:, :, :, HD]))
                dve.tensor_tensor(group_of(attn, p, u), o[:, :, :, 0:HD], rsum[:].unsqueeze(3).broadcast_to([P, NT, G, HD]),
                                  ALU.mult).then_inc(attn_done, 1)

            def norm(j, t, k, l, x):
                if l == 1:
                    link(dve.tensor_tensor_reduce(xn[:], x[:], x[:], 1.0, 0.0, ALU.mult, ALU.add, st[:, 0:1]))
                    dve.tensor_scalar(var[:], st[:, 0:1], TINY, None, ALU.max).then_inc(var_ready.sem, 1)
                    dve.wait_ge(rstd_ready.sem, rstd_ready.upto(j, t, k))
                    dve.tensor_scalar(xn[:], x[:], rstd[:], None, ALU.mult).then_inc(x_normed.sem, 1)
                else:
                    link(dve.bn_stats(st[:], x[:]))
                    dve.memset(pause[:], 0.0)
                    link(dve.bn_aggr(mv[:], st[:]))
                    dve.tensor_scalar(var[:], mv[:, 1:2], LN_EPS, None, ALU.add).then_inc(var_ready.sem, 1)
                    dve.wait_ge(rstd_ready.sem, rstd_ready.upto(j, t, k))
                    dve.tensor_scalar(xn[:], x[:], mv[:, 0:1], rstd[:], ALU.subtract,
                                      ALU.mult).then_inc(x_normed.sem, 1)

            def route(j, t):
                dve.wait_ge(logits_psum.sem, logits_psum.upto(j, t, 1))
                dve.tensor_copy(lg[:], ps[:, D1, 0:NE]).then_inc(logits_read.sem, 1)
                dve.wait_ge(logits_read.sem, logits_read.upto(j, t, 1))
                dve.tensor_reduce(neg_top[:], lg[:], AX.X, ALU.max, negate=True).then_inc(top_ready.sem, 1)
                own = lg[:].unsqueeze(2).broadcast_to([P, NE, NE])
                other = lg[:].unsqueeze(1).broadcast_to([P, NE, NE])
                dve.tensor_tensor(above[:], other, own, ALU.is_gt)
                link(dve.tensor_tensor(ties[:], other, own, ALU.is_equal))
                link(dve.tensor_tensor(ties[:], ties[:], earlier[:], ALU.mult))
                link(dve.tensor_tensor(above[:], above[:], ties[:], ALU.add))
                link(dve.tensor_reduce(rank[:], above[:], AX.X, ALU.add))
                link(dve.tensor_scalar(rank[:], rank[:], 1.5, None, ALU.is_lt))
                dve.wait_ge(gate_exp.sem, gate_exp.upto(j, t, 1))
                link(dve.tensor_tensor(cw[:], gex[:], rank[:], ALU.mult))
                link(dve.tensor_reduce(gsum[:], cw[:], AX.X, ALU.add))
                link(dve.reciprocal(gsum[:], gsum[:]))
                link(dve.tensor_scalar(cw[:], cw[:], gsum[:], None, ALU.mult))

            def add_mlp(j, t):
                l, b = post_layer(j), j % B
                if is_moe(j):
                    for e in range(NE):
                        dve.wait_ge(mlp_psum.sem, mlp_psum.upto(j, t, e + 1))
                        if e == 0:
                            dve.tensor_scalar(acc[:], ps[:, D1, 0:C], cw[:, 0:1], None,
                                              ALU.mult).then_inc(mlp_read.sem, 1)
                        else:
                            dve.scalar_tensor_tensor(out=acc[:], in0=ps[:, D1, 0:C], scalar=cw[:, e:e + 1],
                                                     in1=acc[:], op0=ALU.mult, op1=ALU.add).then_inc(mlp_read.sem, 1)
                        dve.wait_ge(mlp_read.sem, mlp_read.upto(j, t, e + 1))
                    link(dve.tensor_tensor(tmp[:], acc[:], gate[:, l, 1, b], ALU.mult))
                else:
                    dve.wait_ge(mlp_psum.sem, mlp_psum.upto(j, t, 1))
                    dve.tensor_tensor(tmp[:], ps[:, D1, 0:C], gate[:, l, 1, b], ALU.mult).then_inc(mlp_read.sem, 1)
                    dve.wait_ge(mlp_read.sem, mlp_read.upto(j, t, 1))
                dve.tensor_tensor(X[:, bass.ds(((j % B) * NT + t) * C, C)], xa[:], tmp[:],
                                  ALU.add).then_inc(x_stored.sem, 1)
                link(dve.tensor_tensor(xm[:], xa[:], tmp[:], ALU.add))

            def split_qk(j, t):
                dve.wait_ge(v_stored.sem, v_stored.upto(j, t, 1))
                src = ps[:, D1, 0:2 * C].rearrange("p (h d) -> p h d", d=HD)
                if normed(j):
                    if pre_layer(j) == 3:
                        link(dve.tensor_reduce(hsum[:], src, AX.X, ALU.add))
                        link(dve.tensor_scalar(hsum[:], hsum[:], 1.0 / HD, None, ALU.mult))
                        dve.tensor_tensor(qk[:], src, hsum[:].unsqueeze(2).broadcast_to([P, 2 * H, HD]),
                                          ALU.subtract).then_inc(qk_centred.sem, 1)
                    dve.wait_ge(qk_squared.sem, qk_squared.upto(j, t, 1))
                    link(dve.tensor_reduce(hvar[:], sq[:], AX.X, ALU.add))
                    if pre_layer(j) == 3:
                        dve.tensor_scalar(hvar[:], hvar[:], 1.0 / HD, LN_EPS, ALU.mult, ALU.add).then_inc(hvar_ready.sem, 1)
                    else:
                        dve.tensor_scalar(hvar[:], hvar[:], TINY, None, ALU.max).then_inc(hvar_ready.sem, 1)
                    dve.wait_ge(hrstd_ready.sem, hrstd_ready.upto(j, t, 1))
                    if pre_layer(j) == 3:
                        link(dve.tensor_tensor(qk[:], qk[:], hrstd[:].unsqueeze(2).broadcast_to([P, 2 * H, HD]), ALU.mult))
                        two = qk[:].rearrange("p (s h) d -> p s h d", s=2)
                        dve.tensor_tensor(two, two, head_gain[:].unsqueeze(2).broadcast_to([P, 2, H, HD]),
                                          ALU.mult).then_inc(qk_ready.sem, 1)
                    else:
                        for i in range(2):
                            part = hrstd[:, i * H:(i + 1) * H]
                            link(dve.tensor_scalar(part, part, one_gain[:, 2 + i:3 + i], None, ALU.mult))
                        dve.tensor_tensor(qk[:], src, hrstd[:].unsqueeze(2).broadcast_to([P, 2 * H, HD]),
                                          ALU.mult).then_inc(qk_ready.sem, 1)
                    src = qk[:]
                dve.wait_ge(high_ready.sem, high_ready.upto(j, t, 1))
                part = lambda m, i: m[:, :, i * HD:(i + 1) * HD]
                dve.tensor_tensor(rest[:, 0:H], src[:, 0:H], part(q_parts, 0), ALU.subtract)
                link(dve.tensor_tensor(rest[:, H:2 * H], src[:, H:2 * H], part(k_parts, 0), ALU.subtract))
                dve.tensor_copy(part(k_parts, 3), part(k_parts, 0))
                dve.tensor_copy(part(q_parts, 1), rest[:, 0:H])
                link(dve.tensor_copy(part(k_parts, 1), rest[:, H:2 * H]))
                dve.tensor_copy(part(k_parts, 4), part(k_parts, 1))
                dve.tensor_tensor(part(q_parts, 2), rest[:, 0:H], part(q_parts, 1), ALU.subtract)
                dve.tensor_tensor(part(k_parts, 2), rest[:, H:2 * H], part(k_parts, 1),
                                  ALU.subtract).then_inc(parts_ready.sem, 1)

            def dense(n, j, t):
                l, b = post_layer(j), j % B
                here = X[:, bass.ds((b * NT + t) * C, C)]
                if n == AT_PROJ and has_post(j):
                    dve.wait_ge(proj_psum.sem, proj_psum.upto(j, t, 1))
                    link(dve.tensor_tensor(tmp[:], ps[:, D1, 0:C], gate[:, l, 0, b], ALU.mult))
                    link(dve.tensor_tensor(xa[:], here, tmp[:], ALU.add))
                    norm(j, t, 1, l, xa)
                if n == AT_FC1 and is_moe(j):
                    route(j, t)
                if n == AT_FC2:
                    if has_post(j):
                        add_mlp(j, t)
                    else:
                        link(dve.tensor_scalar(xm[:], here, 1.0, None, ALU.mult))
                    if has_pre(j):
                        norm(j, t, 1 + has_post(j), pre_layer(j), xm)
                if n == AT_QKV and has_pre(j):
                    split_qk(j, t)
                if n == AT_ROWS and has_pre(j):
                    for g in range(NG):
                        dve.wait_ge(rows_psum.sem, rows_psum.upto(j, t, 2 * g + 2))
                        dve.tensor_scalar(rows_of(k_rows, j, t, g), ps[0:MROW, D1].rearrange("p (h q) -> p h q", h=G),
                                          1.0, None, ALU.mult).then_inc(k_stored.sem, 1)

            def links(j, A, M, D):
                norm_links = lambda l: 1 if l == 1 else 2
                n = A + G * M
                if D and has_post(j):
                    n += 3 + norm_links(post_layer(j)) + (10 if is_moe(j) else 0)
                if D and has_pre(j):
                    n += norm_links(pre_layer(j)) + 2 + (not has_post(j))
                    n += {1: 3, 3: 4}.get(pre_layer(j), 0)
                return n

            def slot(p, j, s, A, M, D):
                if isinstance(s, int) and s == 0 and j == 3:
                    dve.wait_ge(w_in[2], W_LOADS[2])
                    dve.tensor_scalar(W[2]["qkv"][:, 0:C], W[2]["qkv"][:, 0:C], HD ** -0.5, None, ALU.mult)
                    dve.tensor_scalar(W[2]["qkv_tail"][0:ONE + 1, 0:C], W[2]["qkv_tail"][0:ONE + 1, 0:C],
                                      HD ** -0.5, None, ALU.mult).then_inc(wq_scaled, 1)
                for n in range(STEPS):
                    if M:
                        maxima(p, s, n)
                        if n % NT == NT - 1:
                            split_max(p, s, n // NT)
                    if D:
                        dense(n, j, s)
                if A:
                    normalize(p, s - 1)

            slots(dve, slot, link, links)

        @block.gpsimd
        def _(pool):
            link = Chain(pool, pchain)
            for m in (ident, identb):
                link(pool.memset(m[:], 0.0))
                link(pool.affine_select(out=m[:], in_=m[:], compare_op=ALU.not_equal, fill=1.0, base=0,
                                        pattern=[[-1, P]], channel_multiplier=1))
            pool.memset(v_unit[:], 0.0).then_inc(ident_made, 1)
            pool.wait_ge(ident_made, 1)
            link(pool.memset(v_unit[:, :, :, HD:HD + 1], 1.0))
            link(pool.memset(earlier[:], 0.0))
            for e in range(1, NE):
                link(pool.memset(earlier[:, e, 0:e], 1.0))
            pool.wait_ge(turn_sbuf, len(turns))
            pool.memset(k_rows[MROW:P], -1.0).then_inc(pool_presets, 1)
            pool.wait_ge(pool_presets, 1)
            pool.wait_ge(half_ready, 1)

            def root(steps, ready, j, t, k, dst, src):
                pool.wait_ge(ready.sem, ready.upto(j, t, k))
                pool.tensor_tensor(dst, src, half[:, 0:src.shape[1]], ALU.pow).then_inc(steps.sem, 1)
                pool.wait_ge(steps.sem, steps.upto(j, t, k))

            def stage_v(p, u):
                pool.wait_ge(pv_done, unit(p, u) + 1)
                pool.tensor_copy(v_unit[:, :, :, 0:HD], group_of(v_all, p, u)).then_inc(v_staged, 1)
                pool.wait_ge(v_staged, unit(p, u) + 1)

            def slot(p, j, s, A, M, D):
                if D and has_post(j):
                    pool.wait_ge(attn_done, unit(j - 1, 0) + 1)
                    if not start_of(2, j, s):
                        pool.wait_ge(oT_psum.sem, oT_psum.upto(j, s, 0))
                    pool.tensor_copy(o_tile[:], attn[:, bass.ds(((j % B) * NT + s) * C, C)]).then_inc(o_staged.sem, 1)
                    pool.wait_ge(o_staged.sem, o_staged.upto(j, s, 1))
                if A:
                    pool.wait_ge(v_stored.sem, v_stored.upto(p, NT, 0))
                    stage_v(p, s - 1)
                if D:
                    if has_post(j):
                        root(rstd_ready, var_ready, j, s, 1, rstd[:], var[:])
                    if has_pre(j):
                        root(rstd_ready, var_ready, j, s, 1 + has_post(j), rstd[:], var[:])
                    if normed(j):
                        root(hrstd_ready, hvar_ready, j, s, 1, hrstd[:], hvar[:])

            slots(pool, slot)


_OUTS = [((2, 512, 144), "float32")]


def kernel(**inputs):
    import numpy as _np
    import concourse.bacc as _bacc
    from concourse import mybir as _mybir
    from concourse.bass_utils import run_bass_kernel_spmd as _run

    nc = _bacc.Bacc("TRN2", target_bir_lowering=False, num_devices=1)
    arrays, args = {}, {}
    for name, value in inputs.items():
        v = _np.ascontiguousarray(value)
        arrays[f"in_{name}_dram"] = v
        args[name] = nc.dram_tensor(f"in_{name}_dram", v.shape, _mybir.dt.from_np(v.dtype), kind="ExternalInput").ap()
    shape, dtype = _OUTS[0]
    out = nc.dram_tensor("out_0_dram", shape, _mybir.dt.from_np(_np.dtype(dtype)), kind="ExternalOutput").ap()
    build(nc, args, out)
    r = _run(nc, [arrays], core_ids=[0])
    return r.results[0]["out_0_dram"]
```

```python
import math
import struct
from contextlib import ExitStack

import concourse.bass as bass
from concourse import mybir

ALU = mybir.AluOpType
ACT = mybir.ActivationFunctionType
AX = mybir.AxisListType
F32 = mybir.dt.float32
BF16 = mybir.dt.bfloat16
I32 = mybir.dt.int32

P = 128
B, L, C = 2, 512, 144
H, HD = 16, 9
TAIL = C - P
ONE = TAIL
FF = 4 * C
FC = -(-FF // P)
FR = FF - (FC - 1) * P
NT = L // P
NK = L // P
G = 4
NG = H // G
NE = 4
SPLIT = 3
BLOCK = 32
MROW = SPLIT * BLOCK
KW = (SPLIT - 1) * HD + BLOCK
OC = 32
STEPS = G * NK
LAYERS = 4
PHASES = LAYERS * B
JOBS = PHASES + 2
LN_EPS = 1e-6
TINY = 1e-24
GELU_CUBE = 0.044715
GELU_SCALE = (2 / math.pi) ** 0.5
MINUS_ONES = struct.unpack("f", struct.pack("I", 0xBF80BF80))[0]
ROOT_GUESS = float(0x5F3759DF)
NORMED = (1, 3)
SHIFT1, SCALE1, SHIFT2, SCALE2 = range(4)
ADA = {SHIFT1: 0, SCALE1: 1, SHIFT2: 3, SCALE2: 4}
GATES = (2, 5)


def has_post(j):
    return j >= 2


def has_pre(j):
    return j < PHASES


def post_layer(j):
    return (j - 2) // 2


def pre_layer(j):
    return j // 2


def is_moe(j):
    return has_post(j) and post_layer(j) == 2


def normed(j):
    return has_pre(j) and pre_layer(j) in NORMED


def start_of(job, j, t):
    return j == job and isinstance(t, int) and t == 0


def experts(j):
    return (NE if is_moe(j) else 1) if has_post(j) else 0


class Steps:

    def __init__(self, sem, per):
        self.sem, self.per = sem, per

    def upto(self, j, t, k):
        return sum(NT * int(self.per(i)) for i in range(j)) + t * int(self.per(j)) + k


class Count:

    def __init__(self):
        self.base, self.n = 0, 0

    def loop(self, i, first, per):
        self.start, self.per = self.base + self.n, per
        self.base, self.n = self.start + (i - first) * per, 0

    def end_loop(self, count):
        assert self.n == self.per, f"counts in the loop's body: {self.n}"
        self.base, self.n = self.start + count * self.per, 0

    def value(self):
        return self.base + self.n


class Chain(Count):

    def __init__(self, eng, sem):
        super().__init__()
        self.eng, self.sem = eng, sem

    def __call__(self, ins):
        self.n += 1
        ins.then_inc(self.sem, 1)
        self.eng.wait_ge(self.sem, self.value())


def build(nc, a, out):
    with ExitStack() as ctx:
        def sb(name, shape, dt=F32):
            return ctx.enter_context(nc.sbuf_tensor(name, shape, dt))

        def sem(name):
            return ctx.enter_context(nc.semaphore(name))

        ps = ctx.enter_context(nc.psum_tensor("ps", [P, 8, 512], F32))
        MAXB, KEYB, OUTB, DVEB, ACTB, WIDE = 0, 2, 4, 5, 6, 7
        ident = sb("ident", [P, P])
        identb = sb("identb", [P, P], BF16)
        X = sb("X", [P, B * NT * C])
        q_rows = sb("q_rows", [P, B * H * L], BF16)
        k_rows = sb("k_rows", [P, B * H * L], BF16)
        probs = sb("probs", [P, NK, G, L])
        v_all = sb("v_all", [P, B * NT * C])
        v_unit = sb("v_unit", [P, NK, G, OC])
        attn = sb("attn", [P, B * NT * C])
        attn_t = sb("attn_t", [P, L])
        mx = sb("mx", [P, G, NK])
        mx_parts = sb("mx_parts", [P, G, NK, 2], BF16)
        rsum = sb("rsum", [P, NT, G])
        o_tile = sb("o_tile", [P, C])
        oT = sb("oT", [P, P])
        oT_tail = sb("oT_tail", [P, P])
        hT = sb("hT", [P, P])
        hT_tail = sb("hT_tail", [P, P])
        xa = sb("xa", [P, C])
        xm = sb("xm", [P, C])
        xn = sb("xn", [P, C])
        tmp = sb("tmp", [P, C])
        acc = sb("acc", [P, C])
        st = sb("st", [P, 6])
        mv = sb("mv", [P, 2])
        var = sb("var", [P, 1])
        pause = sb("pause", [P, 1])
        rstd = sb("rstd", [P, 1])
        hid = sb("hid", [P, FC, P])
        bend = sb("bend", [P, FC, P])
        x_last = sb("x_last", [FR, P])
        qk = sb("qk", [P, 2 * H, HD])
        sq = sb("sq", [P, 2 * H, HD])
        rest = sb("rest", [P, 2 * H, HD])
        q_parts = sb("q_parts", [P, H, BLOCK], BF16)
        k_parts = sb("k_parts", [P, H, KW], BF16)
        hsum = sb("hsum", [P, 2 * H])
        hvar = sb("hvar", [P, 2 * H])
        hrstd = sb("hrstd", [P, 2 * H])
        newton = sb("newton", [P, 2 * H])
        half = sb("half", [P, 1])
        one_gain = sb("one_gain", [P, 4])
        head_gain = sb("head_gain", [P, 2, HD])
        lg = sb("lg", [P, NE])
        neg_top = sb("neg_top", [P, 1])
        above = sb("above", [P, NE, NE])
        ties = sb("ties", [P, NE, NE])
        earlier = sb("earlier", [P, NE, NE])
        rank = sb("rank", [P, NE])
        gex = sb("gex", [P, NE])
        gsum = sb("gsum", [P, 1])
        cw = sb("cw", [P, NE])
        cT = sb("cT", [P, B])
        cT_tail = sb("cT_tail", [P, B])
        sT = sb("sT", [P, B])
        sT_tail = sb("sT_tail", [P, B])
        sB = sb("sB", [P, B, P])
        sB_tail = sb("sB_tail", [P, B, P])
        mod = sb("mod", [P, LAYERS, 4, B])
        mod_tail = sb("mod_tail", [P, LAYERS, 4, B])
        gate = sb("gate", [P, LAYERS, 2, B, C])

        wset = []
        for n in range(3):
            wset.append({
                "qkv": sb(f"wqkv{n}", [P, 3 * C]), "qkv_tail": sb(f"wqkv_tail{n}", [P, 3 * C]),
                "proj": sb(f"wproj{n}", [P, C]), "proj_tail": sb(f"wproj_tail{n}", [P, C]),
            })
            if n < 2:
                wset[n].update({"w1": sb(f"w1_{n}", [P, 1, FF]), "w1_tail": sb(f"w1_tail{n}", [P, 1, FF]),
                                "w2": sb(f"w2_{n}", [P, 1, FC, C])})
        W = [wset[0], wset[1], wset[2], wset[0]]
        big = sb("big", [P, NE * (2 * FF + FC * C)])
        W[2]["w1"] = big[:, 0:NE * FF].rearrange("p (e f) -> p e f", e=NE)
        W[2]["w1_tail"] = big[:, NE * FF:2 * NE * FF].rearrange("p (e f) -> p e f", e=NE)
        W[2]["w2"] = big[:, 2 * NE * FF:].rearrange("p (e c n) -> p e c n", e=NE, c=FC)
        w_gate = sb("w_gate", [P, NE])
        w_gate_tail = sb("w_gate_tail", [P, NE])
        ada = big[:, 0:LAYERS * 6 * C].rearrange("p (l n) -> p l n", l=LAYERS)
        assert LAYERS * 6 * C <= 2 * NE * FF
        ada_tail = probs[:].rearrange("p k g q -> p (k g q)")[:, 0:LAYERS * 6 * C].rearrange(
            "p (l n) -> p l n", l=LAYERS)
        raw = probs[:].rearrange("p k g q -> p (k g q)")[:, LAYERS * 6 * C:]
        raw_qkv = raw[:, 0:4 * C].rearrange("p (r n) -> p r n", r=4)
        raw_proj = raw[:, 4 * C:6 * C].rearrange("p (r n) -> p r n", r=2)
        raw2 = k_rows[:, H * L:].bitcast(F32)
        raw_fc1 = raw2[:, 0:5 * C].rearrange("p (r n) -> p r n", r=5)
        raw_fc2 = raw2[:, 5 * C:5 * C + 2 * FF].rearrange("p (r n) -> p r n", r=2)
        raw_ada = raw2[:, 13 * C:20 * C].rearrange("p (r n) -> p r n", r=7)

        x_in = sem("x_in")
        c_in = sem("c_in")
        small_in = sem("small_in")
        ada_in = sem("ada_in")
        first_ada_in = sem("first_ada_in")
        raw_in = sem("raw_in")
        w_in = [sem(f"w{n}_in") for n in range(LAYERS)]
        out_stored = sem("out_stored")
        ident_made = sem("ident_made")
        rows_cleared = sem("rows_cleared")
        first_in = sem("first_in")
        first_scaled = sem("first_scaled")
        presets = sem("presets")
        pool_presets = sem("pool_presets")
        half_ready = sem("half_ready")
        silu_exp = sem("silu_exp")
        tail_set = sem("tail_set")
        silu_ready = sem("silu_ready")
        turn_psum = sem("turn_psum")
        turns_read = sem("turns_read")
        mods_psum = sem("mods_psum")
        mods_ready = sem("mods_ready")
        gates_psum = sem("gates_psum")
        gates_ready = sem("gates_ready")
        weights_scaled = sem("weights_scaled")
        vchain = sem("vchain")
        pchain = sem("pchain")

        key_scores = sem("key_scores")
        exp_done = sem("exp_done")
        max_scores = sem("max_scores")
        max_taken = sem("max_taken")
        max_split = sem("max_split")
        max_rows = sem("max_rows")
        v_staged = sem("v_staged")
        pv_done = sem("pv_done")
        attn_t_ready = sem("attn_t_ready")
        attn_psum = sem("attn_psum")

        def unit(p, u):
            return p * NG + u

        norms = lambda j: has_post(j) + has_pre(j)
        o_staged = Steps(sem("o_staged"), has_post)
        oT_psum = Steps(sem("oT_psum"), has_post)
        proj_psum = Steps(sem("proj_psum"), has_post)
        var_ready = Steps(sem("var_ready"), norms)
        rstd_ready = Steps(sem("rstd_ready"), norms)
        x_normed = Steps(sem("x_normed"), norms)
        xT_psum = Steps(sem("xT_psum"), norms)
        logits_psum = Steps(sem("logits_psum"), is_moe)
        top_ready = Steps(sem("top_ready"), is_moe)
        gate_exp = Steps(sem("gate_exp"), is_moe)
        hid_psum = Steps(sem("hid_psum"), experts)
        hid_squared = Steps(sem("hid_squared"), experts)
        hid_inner = Steps(sem("hid_inner"), experts)
        hid_tanh = Steps(sem("hid_tanh"), experts)
        hid_ready = Steps(sem("hid_ready"), experts)
        mlp_psum = Steps(sem("mlp_psum"), experts)
        x_stored = Steps(sem("x_stored"), has_post)
        qkv_psum = Steps(sem("qkv_psum"), has_pre)
        v_stored = Steps(sem("v_stored"), has_pre)
        qk_squared = Steps(sem("qk_squared"), lambda j: has_pre(j) and pre_layer(j) == 1)
        qk_ready = Steps(sem("qk_ready"), normed)
        high_ready = Steps(sem("high_ready"), has_pre)
        parts_ready = Steps(sem("parts_ready"), has_pre)
        rows_psum = Steps(sem("rows_psum"), lambda j: 2 * NG * has_pre(j))
        act_read = sem("act_read")
        dve_read = sem("dve_read")

        block = ctx.enter_context(nc.Block())

        turns = []
        for r in range(7):
            n = min(P, 6 * C - P * r)
            turns.append((raw_ada[0:n, r, 0:P], ada[:, 1, P * r:P * r + n]))
            turns.append((raw_ada[0:n, r, P:C], ada_tail[0:TAIL, 1, P * r:P * r + n]))
        for r in range(4):
            n = min(P, 3 * C - P * r)
            turns.append((raw_qkv[0:n, r, 0:P], W[1]["qkv"][:, P * r:P * r + n]))
            turns.append((raw_qkv[0:n, r, P:C], W[1]["qkv_tail"][0:TAIL, P * r:P * r + n]))
        for r in range(2):
            n = min(P, C - P * r)
            turns.append((raw_proj[0:n, r, 0:P], W[1]["proj"][:, P * r:P * r + n]))
            turns.append((raw_proj[0:n, r, P:C], W[1]["proj_tail"][0:TAIL, P * r:P * r + n]))
        for r in range(5):
            n = min(P, FF - P * r)
            turns.append((raw_fc1[0:n, r, 0:P], W[1]["w1"][:, 0, P * r:P * r + n]))
            turns.append((raw_fc1[0:n, r, P:C], W[1]["w1_tail"][0:TAIL, 0, P * r:P * r + n]))
        for c in range(FC):
            m = min(P, FF - P * c)
            for r in range(2):
                n = min(P, C - P * r)
                turns.append((raw_fc2[0:n, r, P * c:P * c + m], W[1]["w2"][0:m, 0, c, P * r:P * r + n]))
        ada_turns = 2 * -(-6 * C // P)
        turn_groups = ([turns[i:min(i + 4, ada_turns)] for i in range(0, ada_turns, 4)]
                       + [turns[i:i + 4] for i in range(ada_turns, len(turns), 4)])
        gate_list = [(l, g) for l in range(LAYERS) for g in range(2)]
        first = -(-ada_turns // 4)
        chores = [[("turn", i) for i in range(first)]]
        for s in range(1, NT):
            share = lambda n0, n: range(n0 + (n - n0) * (s - 1) // (NT - 1), n0 + (n - n0) * s // (NT - 1))
            chores.append([("mods", s)] + [("gate", i) for i in share(0, len(gate_list))]
                          + [("turn", i) for i in share(first, len(turn_groups))])
        assert NT == LAYERS

        def chores_at(n, p, s):
            if p >= 0 or is_turnover(s):
                return []
            todo = chores[s]
            return todo[len(todo) * n // STEPS:len(todo) * (n + 1) // STEPS]

        def rows_of(rows, j, t, g):
            n = (j % B) * H + g * G
            return rows[0:MROW].rearrange("p (n l) -> p n l", l=L)[:, n:n + G, bass.ds(t * P, P)]

        def flat(m):
            return m.rearrange("p c q -> p (c q)")

        def group_of(m, p, u):
            n = (p % B) * NT
            return m[:].rearrange("p (t h d) -> p t h d", t=B * NT, d=HD)[:, n:n + NT, bass.ds(u * G, G), :]

        @block.sync
        def _(sp):
            n_small = [0]

            def rows(dst, src, s):
                sp.dma_start(dst, src).then_inc(s, 16)

            sp.dma_start(X[:].rearrange("p (t c) -> p t c", c=C),
                         a["x"].rearrange("b (t p) c -> p (b t) c", p=P)).then_inc(x_in, 16)
            cond = a["cond_1152"].rearrange("b c -> c b")
            sp.dma_start(cT[:], cond[0:P], allow_slow_non_contiguous=True).then_inc(c_in, 16)
            sp.dma_start(cT_tail[0:TAIL, :], cond[P:C], allow_slow_non_contiguous=True).then_inc(c_in, 16)
            ada_w = {0: "L0_cond_W_ada", 2: "L2_cond_w_adaln", 3: "L3_cond_w_mod"}
            ada_b = ["L0_cond_b_ada", "L1_cond_ada_b", "L2_cond_b_adaln", "L3_cond_b_mod"]
            def load_ada(l, s):
                if l != 1:
                    rows(ada[:, l], a[ada_w[l]][0:P], s)
                    rows(ada_tail[0:TAIL, l], a[ada_w[l]][P:C], s)
                rows(ada_tail[ONE:ONE + 1, l], a[ada_b[l]].rearrange("(o n) -> o n", o=1), s)

            load_ada(0, first_ada_in)
            for n, g in enumerate(("g1", "g2", "qg", "kg")):
                rows(one_gain[:, n:n + 1], a["L1_cond_" + g].rearrange("(o n) -> o n", o=1).broadcast_to([P, 1]), small_in)
            rows(head_gain[:, 0, :], a["L3_cond_g_q"].rearrange("(o n) -> o n", o=1).broadcast_to([P, HD]), small_in)
            rows(head_gain[:, 1, :], a["L3_cond_g_k"].rearrange("(o n) -> o n", o=1).broadcast_to([P, HD]), small_in)

            def line(name):
                return a[name].rearrange("(o n) -> o n", o=1)

            def load_qkv(l, qkv, bqkv, s):
                rows(W[l]["qkv"][:], a[qkv][0:P], s)
                rows(W[l]["qkv_tail"][0:TAIL], a[qkv][P:C], s)
                rows(W[l]["qkv_tail"][ONE:ONE + 1], line(bqkv), s)

            def load(l, proj, bproj, w1=None, b1=None, w2=None, b2=None):
                w, s = W[l], w_in[l]
                rows(w["proj"][:], a[proj][0:P], s)
                rows(w["proj_tail"][0:TAIL], a[proj][P:C], s)
                rows(w["proj_tail"][ONE:ONE + 1], line(bproj), s)
                if w1:
                    rows(w["w1"][:, 0], a[w1][0:P], s)
                    rows(w["w1_tail"][0:TAIL, 0], a[w1][P:C], s)
                    rows(w["w1_tail"][ONE:ONE + 1, 0], line(b1), s)
                    rows(w["w2"][:, 0, 0:FC - 1], a[w2][0:(FC - 1) * P].rearrange("(c p) n -> p c n", p=P), s)
                    rows(w["w2"][0:FR, 0, FC - 1], a[w2][(FC - 1) * P:FF], s)
                    rows(w["w2"][FR:FR + 1, 0, FC - 1], line(b2), s)

            sp.wait_ge(rows_cleared, 1)
            load_qkv(0, "L0_cond_W_qkv", "L0_cond_b_qkv", first_in)
            rows(raw_ada[:, 0:6], a["L1_cond_ada_w"][0:6 * P].rearrange("(r p) n -> p r n", p=P), raw_in)
            rows(raw_ada[0:6 * C - 6 * P, 6], a["L1_cond_ada_w"][6 * P:6 * C], raw_in)
            for l in range(1, LAYERS):
                load_ada(l, ada_in)
            w = W[1]
            rows(raw_qkv[:, 0:3], a["L1_cond_qkv_w"][0:3 * P].rearrange("(r p) n -> p r n", p=P), raw_in)
            rows(raw_qkv[0:3 * C - 3 * P, 3], a["L1_cond_qkv_w"][3 * P:3 * C], raw_in)
            rows(raw_proj[:, 0], a["L1_cond_proj_w"][0:P], raw_in)
            rows(raw_proj[0:TAIL, 1], a["L1_cond_proj_w"][P:C], raw_in)
            rows(raw_fc1[:, 0:4], a["L1_cond_fc1_w"][0:4 * P].rearrange("(r p) n -> p r n", p=P), raw_in)
            rows(raw_fc1[0:FR, 4], a["L1_cond_fc1_w"][4 * P:FF], raw_in)
            rows(raw_fc2[:, 0], a["L1_cond_fc2_w"][0:P], raw_in)
            rows(raw_fc2[0:TAIL, 1], a["L1_cond_fc2_w"][P:C], raw_in)
            rows(w["qkv_tail"][ONE:ONE + 1], line("L1_cond_qkv_b"), w_in[1])
            rows(w["proj_tail"][ONE:ONE + 1], line("L1_cond_proj_b"), w_in[1])
            rows(w["w1_tail"][ONE:ONE + 1, 0], line("L1_cond_fc1_b"), w_in[1])
            rows(w["w2"][FR:FR + 1, 0, FC - 1], line("L1_cond_fc2_b"), w_in[1])
            load(0, *["L0_cond_" + n for n in ("W_proj", "b_proj", "W_fc1", "b_fc1", "W_fc2", "b_fc2")])
            load_qkv(2, "L2_cond_w_qkv", "L2_cond_b_qkv", w_in[2])
            load(2, "L2_cond_w_proj", "L2_cond_b_proj")
            rows(w_gate[:], a["L2_cond_w_gate"][0:P], w_in[2])
            rows(w_gate_tail[0:TAIL], a["L2_cond_w_gate"][P:C], w_in[2])
            sp.wait_ge(mods_psum, LAYERS)
            sp.wait_ge(gates_psum, len(gate_list))
            sp.wait_ge(rows_cleared, 2)
            w = W[2]
            w1, b1 = a["L2_cond_w1"], a["L2_cond_b1"]
            w2, b2 = a["L2_cond_w2"], a["L2_cond_b2"]
            rows(w["w1"], w1[:, 0:P].rearrange("e p n -> p e n"), w_in[2])
            rows(w["w1_tail"][0:TAIL], w1[:, P:C].rearrange("e p n -> p e n"), w_in[2])
            rows(w["w1_tail"][ONE:ONE + 1], b1.rearrange("(o e) n -> o e n", o=1), w_in[2])
            for e in range(NE):
                rows(w["w2"][:, e, 0:FC - 1], w2[e, 0:(FC - 1) * P].rearrange("(c p) n -> p c n", p=P), w_in[2])
            rows(w["w2"][0:FR, :, FC - 1], w2[:, (FC - 1) * P:FF].rearrange("e p n -> p e n"), w_in[2])
            rows(w["w2"][FR:FR + 1, :, FC - 1], b2.rearrange("(o e) n -> o e n", o=1), w_in[2])
            sp.wait_ge(mlp_psum.sem, mlp_psum.upto(3, NT, 0))
            load_qkv(3, "L3_cond_w_qkv", "L3_cond_b_qkv", w_in[3])
            load(3, *["L3_cond_" + n for n in ("w_proj", "b_proj", "w1", "b1", "w2", "b2")])
            y = out.rearrange("b (t p) c -> p (b t) c", p=P)
            for j in (PHASES, PHASES + 1):
                for t in range(NT):
                    sp.wait_ge(x_stored.sem, x_stored.upto(j, t, 1))
                    n = (j % B) * NT + t
                    sp.dma_start(y[:, n], X[:, n * C:(n + 1) * C]).then_inc(out_stored, 16)
            sp.wait_ge(out_stored, 16 * B * NT)

        SCALED = (1, 2, 3, 4)
        QKV_LOADS = 16 * 3
        W_LOADS = [16 * 9, 16 * 4, 16 * (6 + 2 + 3 + NE + 2), 16 * 12]
        RAW_LOADS = 16 * 10
        FIRST_ADA_LOADS, ADA_LOADS = 16 * 3, 16 * (2 * 2 + 3)

        def act_uses(j, A, M, N, D, R):
            return A + (G - 1) * M + D * (2 * has_post(j) + experts(j)) + (1 + NG) * R

        def dve_uses(j, A, M, N, D, R):
            return N + D * (has_post(j) + is_moe(j) + experts(j)) + NG * R

        def attended(p):
            n = 1
            for i in range(-1, p + 1):
                R = has_pre(i + 1)
                n += sum(dve_uses(i + 1, i >= 0, i >= 0 and s < NG - 1, i >= 0 and s > 0, True, R and s > 0)
                         for s in range(NG))
                if i < p:
                    n += dve_uses(i + 1, False, R, i >= 0, False, R)
            return n + 1

        def slots(slot, eng, *counts):
            def loop(p, last, parts):
                with eng.Fori(1, last + 1) as s:
                    for count, per in counts:
                        count.loop(s, 1, per(p + 1, *parts))
                    slot(p, p + 1, s, *parts)
                for count, per in counts:
                    count.end_loop(last)

            slot(-1, 0, 0, False, False, False, True, False)
            for s in range(1, NG):
                slot(-1, 0, s, False, False, False, True, True)
            slot(-1, 0, NG, False, True, False, False, True)
            for p in range(PHASES):
                R = has_pre(p + 1)
                slot(p, p + 1, 0, True, True, False, True, False)
                loop(p, NG - 2, (True, True, True, True, R))
                slot(p, p + 1, NG - 1, True, False, True, True, R)
                slot(p, p + 1, NG, False, R, True, False, R)
            slot(PHASES, JOBS - 1, 0, False, False, False, True, False)
            loop(PHASES, NG - 1, (False, False, False, True, False))

        X2, QKV = 0, 2
        VARIANCE, ROOT, HEADS, NORMED_SPLIT = 4, 4, 5, 6
        SPLIT, SPLIT_REST = 3, 1
        O, PROJ, SUM, XN1, X1 = 2, 3, 4, 5, 6
        FC1, INNER, OUTER, FC2 = 8, 1, 1, 3
        MOE_FC1, MOE_INNER, MOE_OUTER, MOE_FC2 = 8, 0, 1, 2
        ROWS = (6, 7, 9, 10, 11, 13, 14, 15)
        NORMED_ROWS = (7, 8, 9, 10, 11, 12, 13, 14)
        VALUES, TURN = 0, 3
        TURNOVER_ROWS = (5, 6, 8, 10, 12, 14, 16, 18)
        TURNOVER_MAX = 8
        TURNOVER_LAG = 3

        def fc1_at(j, e):
            return MOE_FC1 + e * MOE_FC2 if is_moe(j) else FC1 + e * FC2

        def inner_at(j, e):
            return fc1_at(j, e) + (MOE_INNER if is_moe(j) else INNER)

        def outer_at(j, e):
            return fc1_at(j, e) + (MOE_OUTER if is_moe(j) else OUTER)

        def added_at(j):
            return fc1_at(j, experts(j)) if has_post(j) else 1

        def split_at(j):
            return NORMED_SPLIT if normed(j) else SPLIT

        def length(j, s, M, D, R):
            n = STEPS + of_maxima(j - 1, s)[2]
            if not M and is_turnover(s):
                n = TURN + 1
            return max(n, added_at(j) + 2 if D else 0)

        def is_turnover(s):
            return isinstance(s, int) and s == NG

        def of_maxima(p, s):
            if is_turnover(s):
                return p + 1, 0, TURNOVER_MAX + TURNOVER_LAG * normed(p + 1)
            return p, s + 1, 0

        def rows_at(n, j, s):
            if is_turnover(s):
                table, n = TURNOVER_ROWS, n - TURNOVER_LAG * normed(j)
            else:
                table = NORMED_ROWS if normed(j) else ROWS
            return table.index(n) if n in table else None

        @block.tensor
        def _(pe):
            act_bank, dve_bank = Count(), Count()

            def take(bank):
                read = act_read if bank is act_bank else dve_read
                pe.wait_ge(read, bank.value() + 1)
                bank.n += 1
                return read, bank.value() + 1

            def mods(l):
                if l:
                    pe.wait_ge(mods_ready, l)
                for i in range(4):
                    c0, o = ADA[i] * C, i * B
                    pe.matmul(ps[:, OUTB, o:o + B], ada[:, l, c0:c0 + P], sT[:], start=True, stop=False)
                    pe.matmul(ps[:, OUTB, o:o + B], ada_tail[0:ONE + 1, l, c0:c0 + P], sT_tail[0:ONE + 1, :],
                              start=False, stop=True)
                    o += P
                    pe.matmul(ps[0:TAIL, OUTB, o:o + B], ada[:, l, c0 + P:c0 + C], sT[:], start=True, stop=False)
                    last = pe.matmul(ps[0:TAIL, OUTB, o:o + B], ada_tail[0:ONE + 1, l, c0 + P:c0 + C],
                                     sT_tail[0:ONE + 1, :], start=False, stop=True)
                last.then_inc(mods_psum, 1)

            def chore(kind, i):
                if kind == "turn":
                    if i == 0:
                        pe.wait_ge(raw_in, RAW_LOADS)
                    if i > 1:
                        pe.wait_ge(turns_read, i - 1)
                    for n, (src, _) in enumerate(turn_groups[i]):
                        k, m = src.shape[0], src.shape[1]
                        last = pe.transpose(ps[0:m, MAXB + i % 2, n * P:n * P + k], src, ident[0:k, 0:k])
                    last.then_inc(turn_psum, 1)
                if kind == "mods":
                    if i == 1:
                        pe.wait_ge(ada_in, ADA_LOADS)
                        pe.wait_ge(turns_read, len(chores[0]))
                    mods(i)
                if kind == "gate":
                    if i > 1:
                        pe.wait_ge(gates_ready, i - 1)
                    l, g = gate_list[i]
                    w = slice(GATES[g] * C, (GATES[g] + 1) * C)
                    for b in range(B):
                        o = ps[:, KEYB + i % 2, b * C:(b + 1) * C]
                        pe.matmul(o, sB[:, b], ada[:, l, w], start=True, stop=False)
                        last = pe.matmul(o, sB_tail[0:ONE + 1, b], ada_tail[0:ONE + 1, l, w],
                                         start=False, stop=True)
                    last.then_inc(gates_psum, 1)

            pe.wait_ge(ident_made, 1)
            pe.wait_ge(presets, 1)
            pe.wait_ge(silu_ready, 2)
            pe.wait_ge(first_ada_in, FIRST_ADA_LOADS)
            mods(0)

            def score_keys(p, u, n, last_rows):
                kt, h = divmod(n, G)
                if kt == 0 and h == G - 1:
                    pe.wait_ge(*last_rows)
                pe.wait_ge(exp_done, unit(p, u) * STEPS + n + 1)
                head = ((p % B) * H + u * G + h) * L
                pe.matmul(ps[:, KEYB + n % 2], k_rows[:, bass.ds(head + kt * P, P)],
                          q_rows[:, bass.ds(head, L)], start=True, stop=True).then_inc(key_scores, 1)

            def score_queries(p, u, n):
                h, qt = divmod(n, NT)
                pe.wait_ge(max_taken, unit(p, u) * STEPS + n + 1)
                head = ((p % B) * H + u * G + h) * L
                pe.matmul(ps[:, MAXB + n % 2], q_rows[0:MROW, bass.ds(head + qt * P, P)],
                          k_rows[0:MROW, bass.ds(head, L)], start=True, stop=True).then_inc(max_scores, 1)

            def turn_max(p, s, h):
                pe.wait_ge(max_split, unit(p, s) * G + h + 1)
                rows_stored = take(act_bank)
                for qt in range(NT):
                    last = pe.matmul(ps[MROW:MROW + 2, ACTB, qt * P:(qt + 1) * P], mx_parts[:, h, qt, :],
                                     identb[:], start=True, stop=True)
                last.then_inc(max_rows, 1)
                return rows_stored

            def values(p, u, kt):
                pe.wait_ge(exp_done, unit(p, u) * STEPS + (kt + 1) * G + 2)
                if kt == 0:
                    pe.wait_ge(v_staged, unit(p, u) + 1)
                    pe.wait_ge(attn_t_ready, unit(p, u) + 1)
                for h in range(G):
                    last = pe.matmul(ps[OC * h:OC * (h + 1), OUTB], v_unit[:, kt, h, :], probs[:, kt, h, :],
                                     start=(kt == 0), stop=(kt == NK - 1))
                if kt == NK - 1:
                    last.then_inc(pv_done, 1)

            def turn_attn(p, u):
                pe.wait_ge(attn_t_ready, unit(p, u) + 2)
                take(dve_bank)
                for qt in range(NT):
                    last = pe.transpose(ps[:, DVEB, qt * P:(qt + 1) * P], attn_t[:, qt * P:(qt + 1) * P], ident[:])
                last.then_inc(attn_psum, 1)

            def turn_x(j, t, k):
                pe.wait_ge(x_normed.sem, x_normed.upto(j, t, k))
                hT_ready = take(act_bank)
                pe.transpose(ps[:, ACTB, 0:P], xn[:, 0:P], ident[:])
                pe.transpose(ps[0:TAIL, ACTB, P:2 * P], xn[:, P:C], ident[:]).then_inc(xT_psum.sem, 1)
                return hT_ready

            ready = {}

            def post(n, j, t):
                l = post_layer(j)
                if n == O:
                    pe.wait_ge(o_staged.sem, o_staged.upto(j, t, 1))
                    ready["oT"] = take(act_bank)
                    pe.transpose(ps[:, ACTB, 0:P], o_tile[:, 0:P], ident[:])
                    pe.transpose(ps[0:TAIL, ACTB, P:2 * P], o_tile[:, P:C], ident[:]).then_inc(oT_psum.sem, 1)
                if n == PROJ:
                    if isinstance(t, int) and t == 0 and j % 2 == 0:
                        pe.wait_ge(w_in[l], W_LOADS[l])
                        pe.wait_ge(weights_scaled, SCALED[l])
                    pe.wait_ge(*ready["oT"])
                    take(dve_bank)
                    w = W[l]
                    pe.matmul(ps[:, DVEB, 0:C], oT[:], w["proj"][:], start=True, stop=False)
                    pe.matmul(ps[:, DVEB, 0:C], oT_tail[:], w["proj_tail"][:],
                              start=False, stop=True).then_inc(proj_psum.sem, 1)
                if n == X1:
                    ready["hT"] = turn_x(j, t, 1)
                if n == fc1_at(j, 0):
                    pe.wait_ge(*ready["hT"])
                    pe.wait_ge(parts_ready.sem, parts_ready.upto(j, t, 0))
                    if is_moe(j):
                        take(dve_bank)
                        pe.matmul(ps[:, DVEB, 0:NE], hT[:], w_gate[:], start=True, stop=False)
                        pe.matmul(ps[:, DVEB, 0:NE], hT_tail[:], w_gate_tail[:],
                                  start=False, stop=True).then_inc(logits_psum.sem, 1)
                for e in range(experts(j) + 1):
                    if n == fc1_at(j, e):
                        if e:
                            pe.wait_ge(hid_ready.sem, hid_ready.upto(j, t, e))
                        if e < experts(j):
                            fc1(j, t, e)
                        if e:
                            fc2(j, t, e - 1)

            def pre(n, j, t):
                l = pre_layer(j)
                if n == X2:
                    ready["hT before QKV"] = turn_x(j, t, 1 + has_post(j))
                if n == QKV:
                    if start_of(0, j, t):
                        pe.wait_ge(first_in, QKV_LOADS)
                        pe.wait_ge(first_scaled, 1)
                    elif isinstance(t, int) and t == 0 and j % 2 == 0:
                        pe.wait_ge(w_in[l], W_LOADS[l])
                        pe.wait_ge(weights_scaled, SCALED[l])
                    pe.wait_ge(*ready["hT before QKV"])
                    if not has_post(j) and not start_of(0, j, t):
                        pe.wait_ge(parts_ready.sem, parts_ready.upto(j, t, 0))
                    w = W[l]
                    pe.matmul(ps[:, WIDE, 0:3 * C], hT[:], w["qkv"][:], start=True, stop=False)
                    pe.matmul(ps[:, WIDE, 0:3 * C], hT_tail[:], w["qkv_tail"][:],
                              start=False, stop=True).then_inc(qkv_psum.sem, 1)

            def turn_rows(j, t, i):
                if i == 0:
                    pe.wait_ge(parts_ready.sem, parts_ready.upto(j, t, 1))
                take(dve_bank if i % 2 else act_bank)
                bank = DVEB if i % 2 else ACTB
                g, parts, step = i // 2, k_parts if i % 2 else q_parts, HD if i % 2 else 0
                for h in range(G):
                    for r in range(SPLIT):
                        last = pe.matmul(ps[r * BLOCK:(r + 1) * BLOCK, bank, h * P:(h + 1) * P],
                                         parts[:, g * G + h, r * step:r * step + BLOCK], identb[:],
                                         start=True, stop=True)
                last.then_inc(rows_psum.sem, 1)

            def fc1(j, t, e):
                take(act_bank)
                w = W[post_layer(j)]
                for c in range(FC):
                    m = min(P, FF - c * P)
                    o = ps[0:m, WIDE, c * P:(c + 1) * P] if c < FC - 1 else ps[0:m, ACTB, 0:P]
                    pe.matmul(o, w["w1"][:, e, c * P:c * P + m], hT[:], start=True, stop=False)
                    last = pe.matmul(o, w["w1_tail"][:, e, c * P:c * P + m], hT_tail[:],
                                     start=False, stop=True)
                last.then_inc(hid_psum.sem, 1)

            def fc2(j, t, e):
                w = W[post_layer(j)]
                take(dve_bank)
                for c in range(FC):
                    last = pe.matmul(ps[:, DVEB, 0:C], hid[:, c, :], w["w2"][:, e, c, :],
                                     start=(c == 0), stop=(c == FC - 1))
                last.then_inc(mlp_psum.sem, 1)

            def slot(p, j, s, A, M, N, D, R):
                if p in (0, 1) and isinstance(s, int) and s == 0:
                    pe.wait_ge(pool_presets, p + 1)
                if p == -1 and is_turnover(s):
                    pe.wait_ge(turns_read, len(turn_groups))
                    pe.wait_ge(gates_ready, len(gate_list))
                    pe.wait_ge(mods_ready, LAYERS)
                mp, mg, m0 = of_maxima(p, s)
                for n in range(length(j, s, M, D, R)):
                    m = n - m0
                    for kind, i in chores_at(n, p, s):
                        chore(kind, i)
                    if A and n < STEPS:
                        score_keys(p, s, n, ready.get("rows"))
                    if M and 0 <= m < STEPS:
                        if is_turnover(s) and m == 0:
                            pe.wait_ge(act_read, act_bank.value() + 1)
                            pe.wait_ge(dve_read, dve_bank.value() + 1)
                        score_queries(mp, mg, m)
                    if A and n == 0:
                        ready["rows"] = turn_max(p, s, G - 1)
                    if A and n % G == 1 and G < n < STEPS:
                        values(p, s, n // G - 1)
                    if M and m % NT == 1 and NT < m < STEPS:
                        turn_max(mp, mg, m // NT - 1)
                    if N and n == VALUES:
                        values(p, s - 1, NK - 1)
                    if N and n == TURN:
                        turn_attn(p, s - 1)
                    if R and rows_at(n, j, s) is not None:
                        turn_rows(j, s - 1, rows_at(n, j, s))
                    if R:
                        pre(n, j, s - 1)
                    if D and has_post(j):
                        post(n, j, s)

            slots(slot, pe, (act_bank, act_uses), (dve_bank, dve_uses))

        @block.scalar
        def _(act):
            act.wait_ge(c_in, 32)
            act.wait_ge(tail_set, 1)
            act.activation(sT[:], cT[:], ACT.Exp, scale=-1.0)
            act.activation(sT_tail[0:TAIL], cT_tail[0:TAIL], ACT.Exp, scale=-1.0).then_inc(silu_exp, 1)
            act.wait_ge(presets, 1)
            act.wait_ge(mods_ready, 1)

            def take_gate(i):
                l, g = gate_list[i]
                act.wait_ge(gates_psum, i + 1)
                act.activation(gate[:, l, g], ps[:, KEYB + i % 2, 0:B * C].rearrange("p (b c) -> p b c", b=B),
                               ACT.Tanh if l == 1 else ACT.Copy).then_inc(gates_ready, 1)

            def exps(p, u, n):
                act.wait_ge(key_scores, unit(p, u) * STEPS + n + 1)
                act.activation(probs[:, n // G, n % G], ps[:, KEYB + n % 2], ACT.Exp).then_inc(exp_done, 1)

            def store_max(p, s, h):
                act.wait_ge(max_rows, unit(p, s) * G + h + 1)
                head = ((p % B) * H + s * G + h) * L
                act.activation(q_rows[MROW:MROW + 2, bass.ds(head, L)], ps[MROW:MROW + 2, ACTB],
                               ACT.Copy).then_inc(act_read, 1)

            def modulate(j, t, k, l, first):
                b = j % B
                act.wait_ge(xT_psum.sem, xT_psum.upto(j, t, k))
                act.activation(hT[:], ps[:, ACTB, 0:P], ACT.Identity,
                               bias=mod[:, l, first, b:b + 1], scale=mod[:, l, first + 1, b:b + 1])
                act.activation(hT_tail[0:TAIL], ps[0:TAIL, ACTB, P:2 * P], ACT.Identity,
                               bias=mod_tail[0:TAIL, l, first, b:b + 1],
                               scale=mod_tail[0:TAIL, l, first + 1, b:b + 1]).then_inc(act_read, 1)

            def square_hidden(j, t, e):
                act.wait_ge(hid_psum.sem, hid_psum.upto(j, t, e + 1))
                act.activation(bend[0:FR, FC - 1], ps[0:FR, ACTB, 0:P], ACT.Square, scale=GELU_CUBE ** 0.5)
                act.activation(x_last[:], ps[0:FR, ACTB, 0:P], ACT.Copy).then_inc(act_read, 1)
                act.activation(flat(bend[:, 0:FC - 1]), ps[:, WIDE], ACT.Square,
                               scale=GELU_CUBE ** 0.5).then_inc(hid_squared.sem, 1)

            def tanh_hidden(j, t, e):
                act.wait_ge(hid_inner.sem, hid_inner.upto(j, t, e + 1))
                act.activation(flat(bend[:]), flat(bend[:]), ACT.Tanh, scale=GELU_SCALE).then_inc(hid_tanh.sem, 1)

            def post(n, j, t):
                if n == O:
                    act.wait_ge(oT_psum.sem, oT_psum.upto(j, t, 1))
                    act.activation(oT[:], ps[:, ACTB, 0:P], ACT.Copy)
                    act.activation(oT_tail[0:TAIL], ps[0:TAIL, ACTB, P:2 * P], ACT.Copy).then_inc(act_read, 1)
                if n == X1:
                    modulate(j, t, 1, post_layer(j), SHIFT2)
                if n == fc1_at(j, 0) and is_moe(j):
                    act.wait_ge(top_ready.sem, top_ready.upto(j, t, 1))
                    act.activation(gex[:], lg[:], ACT.Exp, bias=neg_top[:]).then_inc(gate_exp.sem, 1)
                for e in range(experts(j)):
                    if n == fc1_at(j, e):
                        square_hidden(j, t, e)
                    if n == inner_at(j, e):
                        tanh_hidden(j, t, e)

            def pre(n, j, t):
                l = pre_layer(j)
                if n == X2:
                    modulate(j, t, 1 + has_post(j), l, SHIFT1)
                if n == QKV:
                    act.wait_ge(qkv_psum.sem, qkv_psum.upto(j, t, 1))
                    act.activation(v_all[:, bass.ds(((j % B) * NT + t) * C, C)], ps[:, WIDE, 2 * C:3 * C],
                                   ACT.Copy).then_inc(v_stored.sem, 1)
                    if l == 1:
                        act.activation(sq[:], ps[:, WIDE, 0:2 * C].rearrange("p (h d) -> p h d", d=HD),
                                       ACT.Square).then_inc(qk_squared.sem, 1)
                if n == (split_at(j) if normed(j) else QKV):
                    src = ps[:, WIDE, 0:2 * C].rearrange("p (h d) -> p h d", d=HD)
                    if normed(j):
                        act.wait_ge(qk_ready.sem, qk_ready.upto(j, t, 1))
                        src = qk[:]
                    act.activation(q_parts[:, :, 0:HD], src[:, 0:H], ACT.Copy)
                    act.activation(k_parts[:, :, 0:HD], src[:, H:2 * H], ACT.Copy).then_inc(high_ready.sem, 1)

            def store_q(j, t, g):
                act.wait_ge(rows_psum.sem, rows_psum.upto(j, t, 2 * g + 1))
                act.activation(rows_of(q_rows, j, t, g), ps[0:MROW, ACTB].rearrange("p (h q) -> p h q", h=G),
                               ACT.Copy).then_inc(act_read, 1)

            def slot(p, j, s, A, M, N, D, R):
                if isinstance(s, int) and s == 0 and j == 1:
                    act.wait_ge(mods_ready, LAYERS)
                mp, mg, m0 = of_maxima(p, s)
                for n in range(length(j, s, M, D, R)):
                    m = n - m0
                    for kind, i in chores_at(n, p, s):
                        if kind == "gate":
                            take_gate(i)
                    if A and n < STEPS:
                        exps(p, s, n)
                    if A and n == 0:
                        store_max(p, s, G - 1)
                    if M and m % NT == 1 and NT < m < STEPS:
                        store_max(mp, mg, m // NT - 1)
                    if N and n == VALUES:
                        act.wait_ge(pv_done, unit(p, s - 1) + 2)
                        act.activation(attn_t[:], ps[:, OUTB], ACT.Copy).then_inc(attn_t_ready, 1)
                    if R and rows_at(n, j, s) in (0, 2, 4, 6):
                        store_q(j, s - 1, rows_at(n, j, s) // 2)
                    if R:
                        pre(n, j, s - 1)
                    if D and has_post(j):
                        post(n, j, s)

            slots(slot, act)

        @block.vector
        def _(dve):
            link = Chain(dve, vchain)
            from_bank = Chain(dve, dve_read)
            from_bank.n = 1

            def scale_q(l):
                for m in (W[l]["qkv"][:, 0:C], W[l]["qkv_tail"][0:ONE + 1, 0:C]):
                    last = dve.tensor_scalar(m, m, HD ** -0.5, None, ALU.mult)
                return last

            def scale_w2(l):
                m = W[l]["w2"][:, :, 0:FC - 1]
                dve.tensor_scalar(m, m, 0.5, None, ALU.mult)
                m = W[l]["w2"][0:FR + 1, :, FC - 1]
                dve.tensor_scalar(m, m, 0.5, None, ALU.mult).then_inc(weights_scaled, 1)

            for w in wset:
                for name in ("qkv_tail", "proj_tail", "w1_tail"):
                    if name in w and (w is not wset[2] or name != "w1_tail"):
                        dve.memset(w[name][:], 0.0)
            for w in W[0], W[1], W[2]:
                dve.memset(w["w2"][FR:P, :, FC - 1], 0.0)
            dve.memset(w_gate_tail[:], 0.0).then_inc(rows_cleared, 1)
            dve.memset(q_parts[:], 0.0)
            dve.memset(k_parts[:], 0.0)
            dve.memset(oT_tail[:], 1.0)
            dve.memset(hT_tail[:], 1.0)
            dve.memset(half[:], -0.5).then_inc(half_ready, 1)
            dve.memset(bend[:], 0.0)
            dve.memset(q_rows[MROW:P].bitcast(F32), 0.0)
            dve.memset(sT_tail[:], 1.0).then_inc(tail_set, 1)
            dve.memset(hid[:], 2.0).then_inc(presets, 1)
            dve.memset(rest[:], 0.0).then_inc(act_read, 1)
            dve.memset(hvar[:], 0.0).then_inc(dve_read, 1)
            dve.memset(mx[:], 0.0).then_inc(exp_done, 1)
            dve.memset(st[:], 0.0).then_inc(exp_done, 1)
            dve.memset(mv[:], 0.0).then_inc(max_taken, 1)
            dve.memset(var[:], 0.0).then_inc(max_taken, 1)
            dve.memset(rstd[:], 0.0).then_inc(attn_t_ready, 1)
            dve.memset(rank[:], 0.0)
            dve.memset(gsum[:], 0.0).then_inc(pv_done, 1)
            dve.wait_ge(silu_exp, 1)
            link(dve.tensor_scalar(sT[:], sT[:], 1.0, None, ALU.add))
            link(dve.tensor_scalar(sT_tail[0:TAIL], sT_tail[0:TAIL], 1.0, None, ALU.add))
            link(dve.reciprocal(sT[:], sT[:]))
            link(dve.reciprocal(sT_tail[0:TAIL], sT_tail[0:TAIL]))
            link(dve.tensor_tensor(sT[:], sT[:], cT[:], ALU.mult))
            link(dve.tensor_tensor(sT_tail[0:TAIL], sT_tail[0:TAIL], cT_tail[0:TAIL], ALU.mult))
            dve.tensor_copy(sB[:], sT[:].unsqueeze(2).broadcast_to([P, B, P])).then_inc(silu_ready, 1)
            dve.tensor_copy(sB_tail[0:ONE + 1], sT_tail[0:ONE + 1].unsqueeze(2).broadcast_to([ONE + 1, B, P])
                            ).then_inc(silu_ready, 1)
            dve.wait_ge(small_in, 16 * 6)
            link(dve.tensor_scalar(one_gain[:, 0:2], one_gain[:, 0:2], C ** 0.5, None, ALU.mult))
            link(dve.tensor_scalar(one_gain[:, 3:4], one_gain[:, 3:4], HD ** 0.5, None, ALU.mult))
            link(dve.tensor_scalar(head_gain[:, 0], head_gain[:, 0], HD ** -0.5, None, ALU.mult))

            def take_mods(l):
                dve.wait_ge(mods_psum, l + 1)
                dve.tensor_copy(mod[:, l], ps[:, OUTB, 0:4 * B].rearrange("p (i b) -> p i b", b=B))
                link(dve.tensor_copy(mod_tail[0:TAIL, l], ps[0:TAIL, OUTB, P:P + 4 * B].rearrange(
                    "p (i b) -> p i b", b=B)))
                for m, r in ((mod, P), (mod_tail, TAIL)):
                    for g, i in enumerate((SCALE1, SCALE2)):
                        link(dve.tensor_scalar(m[0:r, l, i], m[0:r, l, i], 1.0, None, ALU.add))
                        last = dve.tensor_scalar(m[0:r, l, i], m[0:r, l, i],
                                                 one_gain[0:r, g:g + 1] if l == 1 else 1.0, None, ALU.mult)
                last.then_inc(mods_ready, 1)

            def take_turn(i):
                dve.wait_ge(turn_psum, i + 1)
                for n, (src, dst) in enumerate(turn_groups[i]):
                    k, m = src.shape[0], src.shape[1]
                    last = dve.tensor_copy(dst, ps[0:m, MAXB + i % 2, n * P:n * P + k])
                last.then_inc(turns_read, 1)

            take_mods(0)
            dve.wait_ge(first_in, QKV_LOADS)
            scale_q(0).then_inc(first_scaled, 1)
            dve.wait_ge(x_in, 16)

            def maxima(p, s, n):
                h, qt = divmod(n, NT)
                dve.wait_ge(max_scores, unit(p, s) * STEPS + n + 1)
                dve.tensor_reduce(mx[:, h, qt:qt + 1], ps[:, MAXB + n % 2], AX.X, ALU.max).then_inc(max_taken, 1)

            def split_max(p, s, h):
                dve.wait_ge(max_taken, unit(p, s) * STEPS + (h + 1) * NT + 2)
                link(dve.tensor_copy(mx_parts[:, h, :, 0], mx[:, h]))
                dve.tensor_tensor(mx_parts[:, h, :, 1], mx[:, h], mx_parts[:, h, :, 0],
                                  ALU.subtract).then_inc(max_split, 1)

            def normalize(p, u):
                dve.wait_ge(attn_psum, unit(p, u) + 1)
                o = ps[:, DVEB].rearrange("p (t h r) -> p t h r", t=NT, h=G)
                link(dve.reciprocal(rsum[:], o[:, :, :, HD]))
                dve.tensor_tensor(group_of(attn, p, u), o[:, :, :, 0:HD], rsum[:].unsqueeze(3).broadcast_to([P, NT, G, HD]),
                                  ALU.mult).then_inc(dve_read, 1)
                from_bank.n += 1

            def norm_sum(l, x):
                if l == 1:
                    link(dve.tensor_tensor_reduce(tmp[:], x[:], x[:], 1.0, 0.0, ALU.mult, ALU.add, st[:, 0:1]))
                    dve.tensor_scalar(var[:], st[:, 0:1], TINY, None, ALU.max).then_inc(var_ready.sem, 1)
                else:
                    link(dve.bn_stats(st[:], x[:]))
                    dve.memset(pause[:], 0.0)
                    link(dve.bn_aggr(mv[:], st[:]))
                    dve.tensor_scalar(var[:], mv[:, 1:2], LN_EPS, None, ALU.add).then_inc(var_ready.sem, 1)

            def norm(j, t, k, l, x):
                if not (start_of(0, j, t) and k == 1):
                    dve.wait_ge(xT_psum.sem, xT_psum.upto(j, t, k - 1))
                dve.wait_ge(rstd_ready.sem, rstd_ready.upto(j, t, k))
                if l == 1:
                    dve.tensor_scalar(xn[:], x[:], rstd[:], None, ALU.mult).then_inc(x_normed.sem, 1)
                else:
                    dve.tensor_scalar(xn[:], x[:], mv[:, 0:1], rstd[:], ALU.subtract,
                                      ALU.mult).then_inc(x_normed.sem, 1)

            def route(j, t):
                dve.wait_ge(logits_psum.sem, logits_psum.upto(j, t, 1))
                from_bank(dve.tensor_copy(lg[:], ps[:, DVEB, 0:NE]))
                dve.tensor_reduce(neg_top[:], lg[:], AX.X, ALU.max, negate=True).then_inc(top_ready.sem, 1)
                own = lg[:].unsqueeze(2).broadcast_to([P, NE, NE])
                other = lg[:].unsqueeze(1).broadcast_to([P, NE, NE])
                dve.tensor_tensor(above[:], other, own, ALU.is_gt)
                link(dve.tensor_tensor(ties[:], other, own, ALU.is_equal))
                link(dve.tensor_tensor(ties[:], ties[:], earlier[:], ALU.mult))
                link(dve.tensor_tensor(above[:], above[:], ties[:], ALU.add))
                link(dve.tensor_reduce(rank[:], above[:], AX.X, ALU.add))
                link(dve.tensor_scalar(rank[:], rank[:], 1.5, None, ALU.is_lt))
                dve.wait_ge(gate_exp.sem, gate_exp.upto(j, t, 1))
                link(dve.tensor_tensor(cw[:], gex[:], rank[:], ALU.mult))
                link(dve.tensor_reduce(gsum[:], cw[:], AX.X, ALU.add))
                link(dve.reciprocal(gsum[:], gsum[:]))
                link(dve.tensor_scalar(cw[:], cw[:], gsum[:], None, ALU.mult))

            def take_mlp(j, t, e):
                l, b = post_layer(j), j % B
                dve.wait_ge(mlp_psum.sem, mlp_psum.upto(j, t, e + 1))
                out = ps[:, DVEB, 0:C]
                if not is_moe(j):
                    from_bank(dve.tensor_tensor(tmp[:], out, gate[:, l, 1, b], ALU.mult))
                elif e == 0:
                    from_bank(dve.tensor_scalar(acc[:], out, cw[:, 0:1], None, ALU.mult))
                else:
                    from_bank(dve.scalar_tensor_tensor(out=acc[:], in0=out, scalar=cw[:, e:e + 1], in1=acc[:],
                                                       op0=ALU.mult, op1=ALU.add))
                if e + 1 < experts(j):
                    return
                if is_moe(j):
                    link(dve.tensor_tensor(tmp[:], acc[:], gate[:, l, 1, b], ALU.mult))
                dve.tensor_tensor(X[:, bass.ds((b * NT + t) * C, C)], xa[:], tmp[:],
                                  ALU.add).then_inc(x_stored.sem, 1)
                link(dve.tensor_tensor(xm[:], xa[:], tmp[:], ALU.add))

            def root_heads():
                link(dve.tensor_scalar(newton[:].bitcast(I32), hvar[:].bitcast(I32), 1, None,
                                       ALU.logical_shift_right))
                dve.tensor_scalar(hvar[:], hvar[:], -0.5, None, ALU.mult)
                link(dve.tensor_scalar(hrstd[:].bitcast(I32), newton[:].bitcast(I32), -1.0, ROOT_GUESS,
                                       ALU.mult, ALU.add))
                for _ in range(3):
                    link(dve.tensor_tensor(newton[:], hrstd[:], hrstd[:], ALU.mult))
                    link(dve.tensor_tensor(newton[:], newton[:], hvar[:], ALU.mult))
                    link(dve.scalar_tensor_tensor(out=hrstd[:], in0=newton[:], scalar=1.5, in1=hrstd[:],
                                                  op0=ALU.add, op1=ALU.mult))

            def hidden_inner(j, t, e):
                dve.wait_ge(hid_squared.sem, hid_squared.upto(j, t, e + 1))
                main, last = flat(bend[:, 0:FC - 1]), bend[0:FR, FC - 1]
                dve.scalar_tensor_tensor(out=main, in0=main, scalar=1.0, in1=ps[:, WIDE], op0=ALU.add,
                                         op1=ALU.mult)
                dve.scalar_tensor_tensor(out=last, in0=last, scalar=1.0, in1=x_last[:], op0=ALU.add,
                                         op1=ALU.mult).then_inc(hid_inner.sem, 1)

            def hidden_outer(j, t, e):
                dve.wait_ge(hid_tanh.sem, hid_tanh.upto(j, t, e + 1))
                if e:
                    dve.wait_ge(mlp_psum.sem, mlp_psum.upto(j, t, e))
                dve.scalar_tensor_tensor(out=flat(hid[:, 0:FC - 1]), in0=flat(bend[:, 0:FC - 1]), scalar=1.0,
                                         in1=ps[:, WIDE], op0=ALU.add, op1=ALU.mult)
                dve.scalar_tensor_tensor(out=hid[0:FR, FC - 1], in0=bend[0:FR, FC - 1], scalar=1.0,
                                         in1=x_last[:], op0=ALU.add, op1=ALU.mult).then_inc(hid_ready.sem, 1)

            def normalize_heads(n, j, t):
                src = ps[:, WIDE, 0:2 * C].rearrange("p (h d) -> p h d", d=HD)
                heads = lambda m: m.unsqueeze(2).broadcast_to([P, 2 * H, HD])
                three = pre_layer(j) == 3
                if n == VARIANCE:
                    if three:
                        dve.wait_ge(v_stored.sem, v_stored.upto(j, t, 1))
                        link(dve.tensor_reduce(hsum[:], src, AX.X, ALU.add))
                        link(dve.tensor_scalar(hsum[:], hsum[:], 1.0 / HD, None, ALU.mult))
                        link(dve.tensor_tensor(qk[:], src, heads(hsum[:]), ALU.subtract))
                        link(dve.tensor_tensor(sq[:], qk[:], qk[:], ALU.mult))
                    else:
                        dve.wait_ge(qk_squared.sem, qk_squared.upto(j, t, 1))
                    link(dve.tensor_reduce(hvar[:], sq[:], AX.X, ALU.add))
                    if three:
                        link(dve.tensor_scalar(hvar[:], hvar[:], 1.0 / HD, LN_EPS, ALU.mult, ALU.add))
                    else:
                        link(dve.tensor_scalar(hvar[:], hvar[:], TINY, None, ALU.max))
                if n == ROOT:
                    root_heads()
                if n == HEADS and three:
                    link(dve.tensor_tensor(qk[:], qk[:], heads(hrstd[:]), ALU.mult))
                    two = qk[:].rearrange("p (s h) d -> p s h d", s=2)
                    dve.tensor_tensor(two, two, head_gain[:].unsqueeze(2).broadcast_to([P, 2, H, HD]),
                                      ALU.mult).then_inc(qk_ready.sem, 1)
                if n == HEADS and not three:
                    for i in range(2):
                        part = hrstd[:, i * H:(i + 1) * H]
                        link(dve.tensor_scalar(part, part, one_gain[:, 2 + i:3 + i], None, ALU.mult))
                    dve.tensor_tensor(qk[:], src, heads(hrstd[:]), ALU.mult).then_inc(qk_ready.sem, 1)

            def split_qk(n, j, t):
                src = qk[:] if normed(j) else ps[:, WIDE, 0:2 * C].rearrange("p (h d) -> p h d", d=HD)
                part = lambda m, i: m[:, :, i * HD:(i + 1) * HD]
                if n == split_at(j):
                    dve.wait_ge(high_ready.sem, high_ready.upto(j, t, 1))
                    dve.tensor_tensor(rest[:, 0:H], src[:, 0:H], part(q_parts, 0), ALU.subtract)
                    link(dve.tensor_tensor(rest[:, H:2 * H], src[:, H:2 * H], part(k_parts, 0), ALU.subtract))
                    dve.tensor_copy(part(k_parts, 3), part(k_parts, 0))
                    dve.tensor_copy(part(q_parts, 1), rest[:, 0:H])
                    link(dve.tensor_copy(part(k_parts, 1), rest[:, H:2 * H]))
                if n == split_at(j) + SPLIT_REST:
                    dve.tensor_copy(part(k_parts, 4), part(k_parts, 1))
                    dve.tensor_tensor(part(q_parts, 2), rest[:, 0:H], part(q_parts, 1), ALU.subtract)
                    dve.tensor_tensor(part(k_parts, 2), rest[:, H:2 * H], part(k_parts, 1),
                                      ALU.subtract).then_inc(parts_ready.sem, 1)

            def residual(n, j, t):
                l, b = post_layer(j), j % B
                here = X[:, bass.ds((b * NT + t) * C, C)]
                if has_post(j):
                    if n == SUM:
                        dve.wait_ge(proj_psum.sem, proj_psum.upto(j, t, 1))
                        from_bank(dve.tensor_tensor(tmp[:], ps[:, DVEB, 0:C], gate[:, l, 0, b], ALU.mult))
                        link(dve.tensor_tensor(xa[:], here, tmp[:], ALU.add))
                        norm_sum(l, xa)
                    if n == XN1:
                        norm(j, t, 1, l, xa)
                    if n == fc1_at(j, 0) and is_moe(j):
                        route(j, t)
                    for e in range(experts(j)):
                        if n == inner_at(j, e):
                            hidden_inner(j, t, e)
                        if n == outer_at(j, e):
                            hidden_outer(j, t, e)
                        if n == fc1_at(j, e + 1):
                            take_mlp(j, t, e)
                elif n == added_at(j):
                    if not start_of(0, j, t):
                        dve.wait_ge(x_normed.sem, x_normed.upto(j, t, 0))
                    link(dve.tensor_scalar(xm[:], here, 1.0, None, ALU.mult))
                if n == added_at(j) and has_pre(j):
                    norm_sum(pre_layer(j), xm)
                if n == added_at(j) + 1 and has_pre(j):
                    norm(j, t, 1 + has_post(j), pre_layer(j), xm)

            def pre(n, j, t):
                if normed(j):
                    normalize_heads(n, j, t)
                split_qk(n, j, t)

            def store_k(j, t, g):
                dve.wait_ge(rows_psum.sem, rows_psum.upto(j, t, 2 * g + 2))
                dve.tensor_scalar(rows_of(k_rows, j, t, g), ps[0:MROW, DVEB].rearrange("p (h q) -> p h q", h=G),
                                  1.0, None, ALU.mult).then_inc(dve_read, 1)
                from_bank.n += 1

            def links(j, A, M, N, D, R):
                norm_links = lambda l: 1 if l == 1 else 2
                n = G * M + N
                if D and has_post(j):
                    n += 2 + norm_links(post_layer(j)) + (10 if is_moe(j) else 0)
                if D and has_pre(j):
                    n += norm_links(pre_layer(j)) + (not has_post(j))
                if R:
                    n += 2 + {1: 4 + 11, 3: 7 + 11}.get(pre_layer(j), 0)
                return n

            def slot(p, j, s, A, M, N, D, R):
                if isinstance(s, int) and s == 0 and j in (1, 3, 5):
                    for l in {1: (0, 1), 3: (2,), 5: (3,)}[j]:
                        dve.wait_ge(w_in[l], W_LOADS[l])
                        if l and l not in NORMED:
                            scale_q(l)
                        scale_w2(l)
                if isinstance(s, int) and s == 0 and j == 1:
                    dve.wait_ge(gates_ready, len(gate_list))
                mp, mg, m0 = of_maxima(p, s)
                for n in range(length(j, s, M, D, R)):
                    m = n - m0
                    for kind, i in chores_at(n, p, s):
                        if kind == "turn":
                            take_turn(i)
                        if kind == "mods":
                            take_mods(i)
                    if M and 0 <= m < STEPS:
                        maxima(mp, mg, m)
                        if m % NT == NT - 1:
                            split_max(mp, mg, m // NT)
                    if N and n == TURN:
                        normalize(p, s - 1)
                    if R and rows_at(n, j, s) in (1, 3, 5, 7):
                        store_k(j, s - 1, rows_at(n, j, s) // 2)
                    if R:
                        pre(n, j, s - 1)
                    if D:
                        residual(n, j, s)

            slots(slot, dve, (link, links), (from_bank, dve_uses))

        @block.gpsimd
        def _(pool):
            link = Chain(pool, pchain)
            for m in (ident, identb):
                link(pool.memset(m[:], 0.0))
                link(pool.affine_select(out=m[:], in_=m[:], compare_op=ALU.not_equal, fill=1.0, base=0,
                                        pattern=[[-1, P]], channel_multiplier=1))
            pool.memset(v_unit[:], 0.0).then_inc(ident_made, 1)
            pool.wait_ge(ident_made, 1)
            link(pool.memset(v_unit[:, :, :, HD:HD + 1], 1.0))
            link(pool.memset(earlier[:], 0.0))
            for e in range(1, NE):
                link(pool.memset(earlier[:, e, 0:e], 1.0))
            def minus_ones(b):
                m = k_rows[MROW:P, b * H * L:(b + 1) * H * L].bitcast(F32)
                pool.memset(m, MINUS_ONES).then_inc(pool_presets, 1)
                pool.wait_ge(pool_presets, b + 1)

            minus_ones(0)
            pool.wait_ge(half_ready, 1)

            def root(steps, ready, j, t, k, dst, src):
                pool.wait_ge(ready.sem, ready.upto(j, t, k))
                pool.tensor_tensor(dst, src, half[:], ALU.pow).then_inc(steps.sem, 1)
                pool.wait_ge(steps.sem, steps.upto(j, t, k))

            def stage_v(p, u):
                pool.wait_ge(pv_done, unit(p, u) + 1)
                pool.tensor_copy(v_unit[:, :, :, 0:HD], group_of(v_all, p, u)).then_inc(v_staged, 1)
                pool.wait_ge(v_staged, unit(p, u) + 1)

            def slot(p, j, s, A, M, N, D, R):
                if D and has_post(j):
                    pool.wait_ge(dve_read, attended(j - 2))
                    if not start_of(2, j, s):
                        pool.wait_ge(oT_psum.sem, oT_psum.upto(j, s, 0))
                    pool.tensor_copy(o_tile[:], attn[:, bass.ds(((j % B) * NT + s) * C, C)]).then_inc(o_staged.sem, 1)
                    pool.wait_ge(o_staged.sem, o_staged.upto(j, s, 1))
                if A:
                    pool.wait_ge(v_stored.sem, v_stored.upto(p, NT, 0))
                    stage_v(p, s)
                if D and has_post(j):
                    root(rstd_ready, var_ready, j, s, 1, rstd[:], var[:])
                if D and has_pre(j):
                    root(rstd_ready, var_ready, j, s, 1 + has_post(j), rstd[:], var[:])
                if isinstance(s, int) and s == 0 and j == 1:
                    pool.wait_ge(mods_psum, LAYERS)
                    pool.wait_ge(gates_psum, len(gate_list))
                    pool.memset(W[2]["w1_tail"], 0.0).then_inc(rows_cleared, 1)
                    pool.wait_ge(rows_cleared, 2)
                    pool.wait_ge(turn_psum, len(turn_groups))
                    minus_ones(1)

            slots(slot, pool)


_OUTS = [((2, 512, 144), "float32")]


def kernel(**inputs):
    import numpy as _np
    import concourse.bacc as _bacc
    from concourse import mybir as _mybir
    from concourse.bass_utils import run_bass_kernel_spmd as _run

    nc = _bacc.Bacc("TRN2", target_bir_lowering=False, num_devices=1)
    arrays, args = {}, {}
    for name, value in inputs.items():
        v = _np.ascontiguousarray(value)
        arrays[f"in_{name}_dram"] = v
        args[name] = nc.dram_tensor(f"in_{name}_dram", v.shape, _mybir.dt.from_np(v.dtype), kind="ExternalInput").ap()
    shape, dtype = _OUTS[0]
    out = nc.dram_tensor("out_0_dram", shape, _mybir.dt.from_np(_np.dtype(dtype)), kind="ExternalOutput").ap()
    build(nc, args, out)
    r = _run(nc, [arrays], core_ids=[0])
    return r.results[0]["out_0_dram"]
```

```python
import math
import struct
from contextlib import ExitStack

import concourse.bass as bass
from concourse import mybir

ALU = mybir.AluOpType
ACT = mybir.ActivationFunctionType
AX = mybir.AxisListType
F32 = mybir.dt.float32
BF16 = mybir.dt.bfloat16
I32 = mybir.dt.int32

P = 128
B, L, C = 2, 512, 144
H, HD = 16, 9
TAIL = C - P
ONE = TAIL
FF = 4 * C
FC = -(-FF // P)
FR = FF - (FC - 1) * P
NT = L // P
NK = L // P
G = 4
NG = H // G
NE = 4
SPLIT = 3
BLOCK = 32
MROW = SPLIT * BLOCK
KW = 2 * SPLIT * HD
OC = 32
STEPS = G * NK
LAYERS = 4
PHASES = LAYERS * B
JOBS = PHASES + 2
LN_EPS = 1e-6
TINY = 1e-24
GELU_CUBE = 0.044715
GELU_SCALE = (2 / math.pi) ** 0.5
MINUS_ONES = struct.unpack("f", struct.pack("I", 0xBF80BF80))[0]
FAR = 32.0
ROOT_GUESS = float(0x5F3759DF)
NORMED = (1, 3)
SHIFT1, SCALE1, SHIFT2, SCALE2 = range(4)
ADA = {SHIFT1: 0, SCALE1: 1, SHIFT2: 3, SCALE2: 4}
GATES = (2, 5)


def has_post(j):
    return j >= 2


def has_pre(j):
    return j < PHASES


def post_layer(j):
    return (j - 2) // 2


def pre_layer(j):
    return j // 2


def is_moe(j):
    return has_post(j) and post_layer(j) == 2


def normed(j):
    return has_pre(j) and pre_layer(j) in NORMED


def start_of(job, j, t):
    return j == job and isinstance(t, int) and t == 0


def experts(j):
    return (NE if is_moe(j) else 1) if has_post(j) else 0


class Steps:

    def __init__(self, sem, per):
        self.sem, self.per = sem, per

    def upto(self, j, t, k):
        return sum(NT * int(self.per(i)) for i in range(j)) + t * int(self.per(j)) + k


class Count:

    def __init__(self):
        self.base, self.n = 0, 0

    def loop(self, i, first, per):
        self.start, self.per = self.base + self.n, per
        self.base, self.n = self.start + (i - first) * per, 0

    def end_loop(self, count):
        assert self.n == self.per, f"counts in the loop's body: {self.n}"
        self.base, self.n = self.start + count * self.per, 0

    def value(self):
        return self.base + self.n


class Chain(Count):

    def __init__(self, eng, sem):
        super().__init__()
        self.eng, self.sem = eng, sem

    def __call__(self, ins):
        self.n += 1
        ins.then_inc(self.sem, 1)
        self.eng.wait_ge(self.sem, self.value())


def build(nc, a, out):
    with ExitStack() as ctx:
        def sb(name, shape, dt=F32):
            return ctx.enter_context(nc.sbuf_tensor(name, shape, dt))

        def sem(name):
            return ctx.enter_context(nc.semaphore(name))

        ps = ctx.enter_context(nc.psum_tensor("ps", [P, 8, 512], F32))
        MAXB, KEYB, OUTB, DVEB, ACTB, WIDE = 0, 2, 4, 5, 6, 7
        ident = sb("ident", [P, P])
        identb = sb("identb", [P, P], BF16)
        X = sb("X", [P, B * NT * C])
        q_rows = sb("q_rows", [P, B * H * L], BF16)
        k_rows = sb("k_rows", [P, B * H * L], BF16)
        probs = sb("probs", [P, NK, G, L])
        v_all = sb("v_all", [P, B * NT * C])
        v_unit = sb("v_unit", [P, NK, G, OC])
        attn = sb("attn", [P, B * NT * C])
        attn_t = sb("attn_t", [P, L])
        mx = sb("mx", [P, G, NK])
        mx_parts = sb("mx_parts", [P, G, NK, 2], BF16)
        rsum = sb("rsum", [P, NT, G])
        o_tile = sb("o_tile", [P, C])
        oT = sb("oT", [P, P])
        oT_tail = sb("oT_tail", [P, P])
        hT = sb("hT", [P, 2, P])
        hT_tail = sb("hT_tail", [P, 2, P])
        xa = sb("xa", [P, 2, C])
        xm = sb("xm", [P, C])
        xn = sb("xn", [P, C])
        tmp = sb("tmp", [P, C])
        acc = sb("acc", [P, C])
        st = sb("st", [P, 6])
        mv = sb("mv", [P, 2])
        var = sb("var", [P, 1])
        pause = sb("pause", [P, 1])
        rstd = sb("rstd", [P, 1])
        hid_x = sb("hid_x", [P, 2, FC, P])
        hid = sb("hid", [P, 2, FC, P])
        qk = sb("qk", [P, 2 * H, HD])
        sq = sb("sq", [P, 2 * H, HD])
        rest = sb("rest", [P, 2 * H, HD])
        q_parts = sb("q_parts", [P, H, BLOCK], BF16)
        k_parts = sb("k_parts", [P, H, KW], BF16)
        hsum = sb("hsum", [P, 2 * H])
        hvar = sb("hvar", [P, 2 * H])
        hrstd = sb("hrstd", [P, 2 * H])
        newton = sb("newton", [P, 2 * H])
        one = sb("one", [P, 1])
        half = sb("half", [P, 1])
        one_gain = sb("one_gain", [P, 4])
        head_gain = sb("head_gain", [P, 2, HD])
        lg = sb("lg", [P, NE])
        neg_top = sb("neg_top", [P, 1])
        above = sb("above", [P, NE, NE])
        ties = sb("ties", [P, NE, NE])
        earlier = sb("earlier", [P, NE, NE])
        rank = sb("rank", [P, NE])
        gex = sb("gex", [P, NE])
        gsum = sb("gsum", [P, 1])
        cw = sb("cw", [P, NE])
        cT = sb("cT", [P, B])
        cT_tail = sb("cT_tail", [P, B])
        sT = sb("sT", [P, B])
        sT_tail = sb("sT_tail", [P, B])
        sB = sb("sB", [P, B, P])
        sB_tail = sb("sB_tail", [P, B, P])
        mod = sb("mod", [P, LAYERS, 4, B])
        mod_tail = sb("mod_tail", [P, LAYERS, 4, B])
        gate = sb("gate", [P, LAYERS, 2, B, C])

        wset = []
        for n in range(3):
            wset.append({
                "qkv": sb(f"wqkv{n}", [P, 3 * C]), "qkv_tail": sb(f"wqkv_tail{n}", [P, 3 * C]),
                "proj": sb(f"wproj{n}", [P, C]), "proj_tail": sb(f"wproj_tail{n}", [P, C]),
            })
            if n < 2:
                wset[n].update({"w1": sb(f"w1_{n}", [P, 1, FF]), "w1_tail": sb(f"w1_tail{n}", [P, 1, FF]),
                                "w2": sb(f"w2_{n}", [P, 1, FC, C])})
        W = [wset[0], wset[1], wset[2], wset[0]]
        big = sb("big", [P, NE * (2 * FF + FC * C)])
        W[2]["w1"] = big[:, 0:NE * FF].rearrange("p (e f) -> p e f", e=NE)
        W[2]["w1_tail"] = big[:, NE * FF:2 * NE * FF].rearrange("p (e f) -> p e f", e=NE)
        W[2]["w2"] = big[:, 2 * NE * FF:].rearrange("p (e c n) -> p e c n", e=NE, c=FC)
        w_gate = sb("w_gate", [P, NE])
        w_gate_tail = sb("w_gate_tail", [P, NE])
        ada = big[:, 0:LAYERS * 6 * C].rearrange("p (l n) -> p l n", l=LAYERS)
        assert LAYERS * 6 * C <= 2 * NE * FF
        ada_tail = probs[:].rearrange("p k g q -> p (k g q)")[:, 0:LAYERS * 6 * C].rearrange(
            "p (l n) -> p l n", l=LAYERS)
        raw = probs[:].rearrange("p k g q -> p (k g q)")[:, LAYERS * 6 * C:]
        raw_qkv = raw[:, 0:4 * C].rearrange("p (r n) -> p r n", r=4)
        raw_proj = raw[:, 4 * C:6 * C].rearrange("p (r n) -> p r n", r=2)
        raw2 = k_rows[:, H * L:].bitcast(F32)
        raw_fc1 = raw2[:, 0:5 * C].rearrange("p (r n) -> p r n", r=5)
        raw_fc2 = raw2[:, 5 * C:5 * C + 2 * FF].rearrange("p (r n) -> p r n", r=2)
        raw_ada = raw2[:, 13 * C:20 * C].rearrange("p (r n) -> p r n", r=7)

        x_in = sem("x_in")
        c_in = sem("c_in")
        small_in = sem("small_in")
        ada_in = sem("ada_in")
        first_ada_in = sem("first_ada_in")
        raw_in = sem("raw_in")
        w_in = [sem(f"w{n}_in") for n in range(LAYERS)]
        out_stored = sem("out_stored")
        ident_made = sem("ident_made")
        rows_cleared = sem("rows_cleared")
        first_in = sem("first_in")
        first_scaled = sem("first_scaled")
        presets = sem("presets")
        pool_presets = sem("pool_presets")
        half_ready = sem("half_ready")
        silu_exp = sem("silu_exp")
        tail_set = sem("tail_set")
        silu_ready = sem("silu_ready")
        turn_psum = sem("turn_psum")
        turns_read = sem("turns_read")
        mods_psum = sem("mods_psum")
        mods_ready = sem("mods_ready")
        gates_psum = sem("gates_psum")
        gates_ready = sem("gates_ready")
        weights_scaled = sem("weights_scaled")
        vchain = sem("vchain")
        pchain = sem("pchain")

        key_scores = sem("key_scores")
        exp_done = sem("exp_done")
        max_scores = sem("max_scores")
        max_taken = sem("max_taken")
        max_split = sem("max_split")
        max_rows = sem("max_rows")
        v_staged = sem("v_staged")
        pv_done = sem("pv_done")
        attn_t_ready = sem("attn_t_ready")
        attn_psum = sem("attn_psum")

        def unit(p, u):
            return p * NG + u

        norms = lambda j: has_post(j) + has_pre(j)
        o_staged = Steps(sem("o_staged"), has_post)
        oT_psum = Steps(sem("oT_psum"), has_post)
        proj_psum = Steps(sem("proj_psum"), has_post)
        var_ready = Steps(sem("var_ready"), norms)
        rstd_ready = Steps(sem("rstd_ready"), norms)
        x_normed = Steps(sem("x_normed"), norms)
        xT_psum = Steps(sem("xT_psum"), norms)
        logits_psum = Steps(sem("logits_psum"), is_moe)
        top_ready = Steps(sem("top_ready"), is_moe)
        gate_exp = Steps(sem("gate_exp"), is_moe)
        hid_psum = Steps(sem("hid_psum"), experts)
        hid_squared = Steps(sem("hid_squared"), experts)
        hid_inner = Steps(sem("hid_inner"), experts)
        hid_tanh = Steps(sem("hid_tanh"), experts)
        hid_ready = Steps(sem("hid_ready"), experts)
        mlp_psum = Steps(sem("mlp_psum"), experts)
        x_stored = Steps(sem("x_stored"), has_post)
        qkv_psum = Steps(sem("qkv_psum"), has_pre)
        v_stored = Steps(sem("v_stored"), has_pre)
        qk_squared = Steps(sem("qk_squared"), normed)
        qk_ready = Steps(sem("qk_ready"), normed)
        high_ready = Steps(sem("high_ready"), has_pre)
        q_middle = Steps(sem("q_middle"), lambda j: 2 * has_pre(j))
        q_parts_ready = Steps(sem("q_parts_ready"), has_pre)
        k_parts_ready = Steps(sem("k_parts_ready"), has_pre)
        rows_psum = Steps(sem("rows_psum"), lambda j: 2 * NG * has_pre(j))
        act_read = sem("act_read")
        dve_read = sem("dve_read")

        block = ctx.enter_context(nc.Block())

        turns = []
        for r in range(7):
            n = min(P, 6 * C - P * r)
            turns.append((raw_ada[0:n, r, 0:P], ada[:, 1, P * r:P * r + n]))
            turns.append((raw_ada[0:n, r, P:C], ada_tail[0:TAIL, 1, P * r:P * r + n]))
        for r in range(4):
            n = min(P, 3 * C - P * r)
            turns.append((raw_qkv[0:n, r, 0:P], W[1]["qkv"][:, P * r:P * r + n]))
            turns.append((raw_qkv[0:n, r, P:C], W[1]["qkv_tail"][0:TAIL, P * r:P * r + n]))
        for r in range(2):
            n = min(P, C - P * r)
            turns.append((raw_proj[0:n, r, 0:P], W[1]["proj"][:, P * r:P * r + n]))
            turns.append((raw_proj[0:n, r, P:C], W[1]["proj_tail"][0:TAIL, P * r:P * r + n]))
        for r in range(5):
            n = min(P, FF - P * r)
            turns.append((raw_fc1[0:n, r, 0:P], W[1]["w1"][:, 0, P * r:P * r + n]))
            turns.append((raw_fc1[0:n, r, P:C], W[1]["w1_tail"][0:TAIL, 0, P * r:P * r + n]))
        for c in range(FC):
            m = min(P, FF - P * c)
            for r in range(2):
                n = min(P, C - P * r)
                turns.append((raw_fc2[0:n, r, P * c:P * c + m], W[1]["w2"][0:m, 0, c, P * r:P * r + n]))
        ada_turns = 2 * -(-6 * C // P)
        turn_groups = ([turns[i:min(i + 4, ada_turns)] for i in range(0, ada_turns, 4)]
                       + [turns[i:i + 4] for i in range(ada_turns, len(turns), 4)])
        gate_list = [(l, g) for l in range(LAYERS) for g in range(2)]
        first = -(-ada_turns // 4)
        chores = [[("turn", i) for i in range(first)]]
        for s in range(1, NT):
            share = lambda n0, n: range(n0 + (n - n0) * (s - 1) // (NT - 1), n0 + (n - n0) * s // (NT - 1))
            chores.append([("mods", s)] + [("gate", i) for i in share(0, len(gate_list))]
                          + [("turn", i) for i in share(first, len(turn_groups))])
        assert NT == LAYERS

        def chores_at(n, p, s):
            if p >= 0 or is_turnover(0, s):
                return []
            todo = chores[s]
            return todo[len(todo) * n // STEPS:len(todo) * (n + 1) // STEPS]

        def rows_of(rows, j, t, g):
            n = (j % B) * H + g * G
            return rows[0:MROW].rearrange("p (n l) -> p n l", l=L)[:, n:n + G, bass.ds(t * P, P)]

        def flat(m):
            return m.rearrange("p c q -> p (c q)")

        def twice(i):
            return k_parts[:].rearrange("p h (n x) -> p h n x", n=2)[:, :, :, i * HD:(i + 1) * HD]

        def for_both(m):
            return m.unsqueeze(2).broadcast_to([P, H, 2, HD])

        def group_of(m, p, u):
            n = (p % B) * NT
            return m[:].rearrange("p (t h d) -> p t h d", t=B * NT, d=HD)[:, n:n + NT, bass.ds(u * G, G), :]

        @block.sync
        def _(sp):
            n_small = [0]

            def rows(dst, src, s):
                sp.dma_start(dst, src).then_inc(s, 16)

            sp.dma_start(X[:].rearrange("p (t c) -> p t c", c=C),
                         a["x"].rearrange("b (t p) c -> p (b t) c", p=P)).then_inc(x_in, 16)
            cond = a["cond_1152"].rearrange("b c -> c b")
            sp.dma_start(cT[:], cond[0:P], allow_slow_non_contiguous=True).then_inc(c_in, 16)
            sp.dma_start(cT_tail[0:TAIL, :], cond[P:C], allow_slow_non_contiguous=True).then_inc(c_in, 16)
            ada_w = {0: "L0_cond_W_ada", 2: "L2_cond_w_adaln", 3: "L3_cond_w_mod"}
            ada_b = ["L0_cond_b_ada", "L1_cond_ada_b", "L2_cond_b_adaln", "L3_cond_b_mod"]
            def load_ada(l, s):
                if l != 1:
                    rows(ada[:, l], a[ada_w[l]][0:P], s)
                    rows(ada_tail[0:TAIL, l], a[ada_w[l]][P:C], s)
                rows(ada_tail[ONE:ONE + 1, l], a[ada_b[l]].rearrange("(o n) -> o n", o=1), s)

            load_ada(0, first_ada_in)
            for n, g in enumerate(("g1", "g2", "qg", "kg")):
                rows(one_gain[:, n:n + 1], a["L1_cond_" + g].rearrange("(o n) -> o n", o=1).broadcast_to([P, 1]), small_in)
            rows(head_gain[:, 0, :], a["L3_cond_g_q"].rearrange("(o n) -> o n", o=1).broadcast_to([P, HD]), small_in)
            rows(head_gain[:, 1, :], a["L3_cond_g_k"].rearrange("(o n) -> o n", o=1).broadcast_to([P, HD]), small_in)

            def line(name):
                return a[name].rearrange("(o n) -> o n", o=1)

            def load_qkv(l, qkv, bqkv, s):
                rows(W[l]["qkv"][:], a[qkv][0:P], s)
                rows(W[l]["qkv_tail"][0:TAIL], a[qkv][P:C], s)
                rows(W[l]["qkv_tail"][ONE:ONE + 1], line(bqkv), s)

            def load(l, proj, bproj, w1=None, b1=None, w2=None, b2=None):
                w, s = W[l], w_in[l]
                rows(w["proj"][:], a[proj][0:P], s)
                rows(w["proj_tail"][0:TAIL], a[proj][P:C], s)
                rows(w["proj_tail"][ONE:ONE + 1], line(bproj), s)
                if w1:
                    rows(w["w1"][:, 0], a[w1][0:P], s)
                    rows(w["w1_tail"][0:TAIL, 0], a[w1][P:C], s)
                    rows(w["w1_tail"][ONE:ONE + 1, 0], line(b1), s)
                    rows(w["w2"][:, 0, 0:FC - 1], a[w2][0:(FC - 1) * P].rearrange("(c p) n -> p c n", p=P), s)
                    rows(w["w2"][0:FR, 0, FC - 1], a[w2][(FC - 1) * P:FF], s)
                    rows(w["w2"][FR:FR + 1, 0, FC - 1], line(b2), s)

            sp.wait_ge(rows_cleared, 1)
            load_qkv(0, "L0_cond_W_qkv", "L0_cond_b_qkv", first_in)
            rows(raw_ada[:, 0:6], a["L1_cond_ada_w"][0:6 * P].rearrange("(r p) n -> p r n", p=P), raw_in)
            rows(raw_ada[0:6 * C - 6 * P, 6], a["L1_cond_ada_w"][6 * P:6 * C], raw_in)
            for l in range(1, LAYERS):
                load_ada(l, ada_in)
            w = W[1]
            rows(raw_qkv[:, 0:3], a["L1_cond_qkv_w"][0:3 * P].rearrange("(r p) n -> p r n", p=P), raw_in)
            rows(raw_qkv[0:3 * C - 3 * P, 3], a["L1_cond_qkv_w"][3 * P:3 * C], raw_in)
            rows(raw_proj[:, 0], a["L1_cond_proj_w"][0:P], raw_in)
            rows(raw_proj[0:TAIL, 1], a["L1_cond_proj_w"][P:C], raw_in)
            rows(raw_fc1[:, 0:4], a["L1_cond_fc1_w"][0:4 * P].rearrange("(r p) n -> p r n", p=P), raw_in)
            rows(raw_fc1[0:FR, 4], a["L1_cond_fc1_w"][4 * P:FF], raw_in)
            rows(raw_fc2[:, 0], a["L1_cond_fc2_w"][0:P], raw_in)
            rows(raw_fc2[0:TAIL, 1], a["L1_cond_fc2_w"][P:C], raw_in)
            rows(w["qkv_tail"][ONE:ONE + 1], line("L1_cond_qkv_b"), w_in[1])
            rows(w["proj_tail"][ONE:ONE + 1], line("L1_cond_proj_b"), w_in[1])
            rows(w["w1_tail"][ONE:ONE + 1, 0], line("L1_cond_fc1_b"), w_in[1])
            rows(w["w2"][FR:FR + 1, 0, FC - 1], line("L1_cond_fc2_b"), w_in[1])
            load(0, *["L0_cond_" + n for n in ("W_proj", "b_proj", "W_fc1", "b_fc1", "W_fc2", "b_fc2")])
            load_qkv(2, "L2_cond_w_qkv", "L2_cond_b_qkv", w_in[2])
            load(2, "L2_cond_w_proj", "L2_cond_b_proj")
            rows(w_gate[:], a["L2_cond_w_gate"][0:P], w_in[2])
            rows(w_gate_tail[0:TAIL], a["L2_cond_w_gate"][P:C], w_in[2])
            sp.wait_ge(mods_psum, LAYERS)
            sp.wait_ge(gates_psum, len(gate_list))
            sp.wait_ge(rows_cleared, 2)
            w = W[2]
            w1, b1 = a["L2_cond_w1"], a["L2_cond_b1"]
            w2, b2 = a["L2_cond_w2"], a["L2_cond_b2"]
            rows(w["w1"], w1[:, 0:P].rearrange("e p n -> p e n"), w_in[2])
            rows(w["w1_tail"][0:TAIL], w1[:, P:C].rearrange("e p n -> p e n"), w_in[2])
            rows(w["w1_tail"][ONE:ONE + 1], b1.rearrange("(o e) n -> o e n", o=1), w_in[2])
            for e in range(NE):
                rows(w["w2"][:, e, 0:FC - 1], w2[e, 0:(FC - 1) * P].rearrange("(c p) n -> p c n", p=P), w_in[2])
            rows(w["w2"][0:FR, :, FC - 1], w2[:, (FC - 1) * P:FF].rearrange("e p n -> p e n"), w_in[2])
            rows(w["w2"][FR:FR + 1, :, FC - 1], b2.rearrange("(o e) n -> o e n", o=1), w_in[2])
            sp.wait_ge(mlp_psum.sem, mlp_psum.upto(3, NT, 0))
            load_qkv(3, "L3_cond_w_qkv", "L3_cond_b_qkv", w_in[3])
            load(3, *["L3_cond_" + n for n in ("w_proj", "b_proj", "w1", "b1", "w2", "b2")])
            y = out.rearrange("b (t p) c -> p (b t) c", p=P)
            for j in (PHASES, PHASES + 1):
                for t in range(NT):
                    sp.wait_ge(x_stored.sem, x_stored.upto(j, t, 1))
                    n = (j % B) * NT + t
                    sp.dma_start(y[:, n], X[:, n * C:(n + 1) * C]).then_inc(out_stored, 16)
            sp.wait_ge(out_stored, 16 * B * NT)

        SCALED = (1, 2, 3, 4)
        QKV_LOADS = 16 * 3
        W_LOADS = [16 * 9, 16 * 4, 16 * (6 + 2 + 3 + NE + 2), 16 * 12]
        RAW_LOADS = 16 * 10
        FIRST_ADA_LOADS, ADA_LOADS = 16 * 3, 16 * (2 * 2 + 3)

        def act_uses(j, A, M, N, D, R):
            return A + (G - 1) * M + D * (2 * has_post(j) + experts(j)) + (1 + NG) * R

        def dve_uses(j, A, M, N, D, R):
            return N + D * (has_post(j) + is_moe(j) + experts(j)) + NG * R

        def attended(p):
            n = 1
            for i in range(-1, p + 1):
                R = has_pre(i + 1)
                n += sum(dve_uses(i + 1, i >= 0, i >= 0 and s < NG - 1, i >= 0 and s > 0, True, R and s > 0)
                         for s in range(NG))
                if i < p:
                    n += dve_uses(i + 1, False, R, i >= 0, False, R)
            return n + 1

        def slots(slot, eng, *counts):
            def loop(p, last, parts):
                with eng.Fori(1, last + 1) as s:
                    for count, per in counts:
                        count.loop(s, 1, per(p + 1, *parts))
                    slot(p, p + 1, s, *parts)
                for count, per in counts:
                    count.end_loop(last)

            slot(-1, 0, 0, False, False, False, True, False)
            for s in range(1, NG):
                slot(-1, 0, s, False, False, False, True, True)
            slot(-1, 0, NG, False, True, False, False, True)
            for p in range(PHASES):
                R = has_pre(p + 1)
                slot(p, p + 1, 0, True, True, False, True, False)
                loop(p, NG - 2, (True, True, True, True, R))
                slot(p, p + 1, NG - 1, True, False, True, True, R)
                slot(p, p + 1, NG, False, R, True, False, R)
            for s in range(NT + 1):
                slot(PHASES, JOBS - 1, s, False, False, False, True, False)

        X2 = (1, 1, 0, 0, 0, 0)
        QKV = (3, 3, 2, 3, 2, 2)
        VARIANCE = (0, 4, 0, 4, 0, 1)
        ROOT = (0, 5, 0, 5, 0, 1)
        HEADS = (0, 5, 0, 5, 0, 0)
        SPLIT_QK = (5, 6, 3, 6, 3, 3)
        SPLIT_REST = (5, 6, 3, 6, 3, 2)
        O = (0, 3, 2, 2, 2, 1)
        PROJ = (0, 5, 4, 4, 3, 2)
        SUM = (0, 5, 4, 4, 3, 2)
        XN1 = (0, 5, 5, 4, 4, 3)
        X1 = (0, 6, 6, 5, 6, 3)
        FC1 = (0, 8, 8, 6, 8, 0)
        INNER = (0, 1, 1, 1, 1, 1)
        OUTER = (0, 2, 2, 2, 1, 2)
        FC2 = (0, 3, 4, 2, 3, 4)
        ROWS0 = (7, 8, 10, 11, 12, 14, 15, 16)
        ROWS1 = (7, 8, 9, 10, 11, 12, 15, 17)
        ROWS2 = (6, 7, 9, 10, 11, 13, 14, 15)
        ROWS3 = (7, 8, 9, 10, 11, 12, 15, 16)
        ROWS = (ROWS0, ROWS1, ROWS2, ROWS3, (), ())
        K_BY_ACT = (0, 3, 0, 2, 0, 0)
        BETWEEN_K_BY_ACT = (3, 4, 4, 4, 1, 0)
        VALUES = (1, 1, 0, 0, 2, 0)
        TURN = (3, 3, 1, 2, 4, 0)
        BETWEEN_ROWS0 = (5, 6, 9, 10, 11, 13, 16, 18)
        BETWEEN_ROWS1 = (7, 9, 10, 11, 13, 14, 16, 18)
        BETWEEN_ROWS2 = (5, 6, 8, 10, 12, 15, 16, 18)
        BETWEEN_ROWS3 = (7, 9, 12, 14, 16, 18, 20, 21)
        BETWEEN_ROWS = (BETWEEN_ROWS0, BETWEEN_ROWS1, BETWEEN_ROWS2, BETWEEN_ROWS3, (), ())
        BETWEEN_MAX = (9, 10, 9, 13, 0, 0)

        def at(table, j):
            return table[j // 2 + (j == JOBS - 1)]

        def tiles(j, s):
            if j < JOBS - 1:
                return s, s
            return (s if s < NT else None), (s - 1 if s else None)

        def place(j, t):
            return t % 2 if j == JOBS - 1 else 0

        def fc1_at(j, e):
            return at(FC1, j) + e * at(FC2, j)

        def inner_at(j, e):
            return fc1_at(j, e) + at(INNER, j)

        def outer_at(j, e):
            return fc1_at(j, e) + at(OUTER, j)

        def added_at(j):
            return fc1_at(j, experts(j)) if has_post(j) else 1

        def length(j, s, M, D, R):
            n = STEPS + of_maxima(j - 1, s)[2]
            if not M and is_turnover(j, s):
                n = at(TURN, j) + 1
            return max(n, added_at(j) + 2 if D else 0, rows_table(j, s)[-1] + 1 if R else 0)

        def k_by_act(j, s):
            return (1, 3, 5, 7)[:at(BETWEEN_K_BY_ACT if is_turnover(j, s) else K_BY_ACT, j)]

        def rows_table(j, s):
            return at(BETWEEN_ROWS if is_turnover(j, s) else ROWS, j)

        def is_turnover(j, s):
            return isinstance(s, int) and s == NG and j < JOBS - 1

        def of_maxima(p, s):
            if is_turnover(p + 1, s):
                return p + 1, 0, at(BETWEEN_MAX, p + 1)
            return p, s + 1, 0

        def rows_at(n, j, s):
            table = rows_table(j, s)
            return table.index(n) if n in table else None

        @block.tensor
        def _(pe):
            act_bank, dve_bank = Count(), Count()

            def take(bank):
                read = act_read if bank is act_bank else dve_read
                pe.wait_ge(read, bank.value() + 1)
                bank.n += 1
                return read, bank.value() + 1

            def mods(l):
                if l:
                    pe.wait_ge(mods_ready, l)
                for i in range(4):
                    c0, o = ADA[i] * C, i * B
                    pe.matmul(ps[:, OUTB, o:o + B], ada[:, l, c0:c0 + P], sT[:], start=True, stop=False)
                    pe.matmul(ps[:, OUTB, o:o + B], ada_tail[0:ONE + 1, l, c0:c0 + P], sT_tail[0:ONE + 1, :],
                              start=False, stop=True)
                    o += P
                    pe.matmul(ps[0:TAIL, OUTB, o:o + B], ada[:, l, c0 + P:c0 + C], sT[:], start=True, stop=False)
                    last = pe.matmul(ps[0:TAIL, OUTB, o:o + B], ada_tail[0:ONE + 1, l, c0 + P:c0 + C],
                                     sT_tail[0:ONE + 1, :], start=False, stop=True)
                last.then_inc(mods_psum, 1)

            def chore(kind, i):
                if kind == "turn":
                    if i == 0:
                        pe.wait_ge(raw_in, RAW_LOADS)
                    if i > 1:
                        pe.wait_ge(turns_read, i - 1)
                    for n, (src, _) in enumerate(turn_groups[i]):
                        k, m = src.shape[0], src.shape[1]
                        last = pe.transpose(ps[0:m, MAXB + i % 2, n * P:n * P + k], src, ident[0:k, 0:k])
                    last.then_inc(turn_psum, 1)
                if kind == "mods":
                    if i == 1:
                        pe.wait_ge(ada_in, ADA_LOADS)
                        pe.wait_ge(turns_read, len(chores[0]))
                    mods(i)
                if kind == "gate":
                    if i > 1:
                        pe.wait_ge(gates_ready, i - 1)
                    l, g = gate_list[i]
                    w = slice(GATES[g] * C, (GATES[g] + 1) * C)
                    for b in range(B):
                        o = ps[:, KEYB + i % 2, b * C:(b + 1) * C]
                        pe.matmul(o, sB[:, b], ada[:, l, w], start=True, stop=False)
                        last = pe.matmul(o, sB_tail[0:ONE + 1, b], ada_tail[0:ONE + 1, l, w],
                                         start=False, stop=True)
                    last.then_inc(gates_psum, 1)

            pe.wait_ge(ident_made, 1)
            pe.wait_ge(presets, 1)
            pe.wait_ge(silu_ready, 2)
            pe.wait_ge(first_ada_in, FIRST_ADA_LOADS)
            mods(0)

            def score_keys(p, u, n, last_rows):
                kt, h = divmod(n, G)
                if kt == 0 and h == G - 1:
                    pe.wait_ge(*last_rows)
                pe.wait_ge(exp_done, unit(p, u) * STEPS + n + 1)
                head = ((p % B) * H + u * G + h) * L
                pe.matmul(ps[:, KEYB + n % 2], k_rows[:, bass.ds(head + kt * P, P)],
                          q_rows[:, bass.ds(head, L)], start=True, stop=True).then_inc(key_scores, 1)

            def score_queries(p, u, n):
                h, qt = divmod(n, NT)
                pe.wait_ge(max_taken, unit(p, u) * STEPS + n + 1)
                head = ((p % B) * H + u * G + h) * L
                pe.matmul(ps[:, MAXB + n % 2], q_rows[0:MROW, bass.ds(head + qt * P, P)],
                          k_rows[0:MROW, bass.ds(head, L)], start=True, stop=True).then_inc(max_scores, 1)

            def turn_max(p, s, h):
                pe.wait_ge(max_split, unit(p, s) * G + h + 1)
                rows_stored = take(act_bank)
                for qt in range(NT):
                    last = pe.matmul(ps[MROW:MROW + 2, ACTB, qt * P:(qt + 1) * P], mx_parts[:, h, qt, :],
                                     identb[:], start=True, stop=True)
                last.then_inc(max_rows, 1)
                return rows_stored

            def values(p, u, kt):
                pe.wait_ge(exp_done, unit(p, u) * STEPS + (kt + 1) * G + 2)
                if kt == 0:
                    pe.wait_ge(v_staged, unit(p, u) + 1)
                    pe.wait_ge(attn_t_ready, unit(p, u) + 1)
                for h in range(G):
                    last = pe.matmul(ps[OC * h:OC * (h + 1), OUTB], v_unit[:, kt, h, :], probs[:, kt, h, :],
                                     start=(kt == 0), stop=(kt == NK - 1))
                if kt == NK - 1:
                    last.then_inc(pv_done, 1)

            def turn_attn(p, u):
                pe.wait_ge(attn_t_ready, unit(p, u) + 2)
                take(dve_bank)
                for qt in range(NT):
                    last = pe.transpose(ps[:, DVEB, qt * P:(qt + 1) * P], attn_t[:, qt * P:(qt + 1) * P], ident[:])
                last.then_inc(attn_psum, 1)

            def turn_x(j, t, k):
                pe.wait_ge(x_normed.sem, x_normed.upto(j, t, k))
                hT_ready = take(act_bank)
                pe.transpose(ps[:, ACTB, 0:P], xn[:, 0:P], ident[:])
                pe.transpose(ps[0:TAIL, ACTB, P:2 * P], xn[:, P:C], ident[:]).then_inc(xT_psum.sem, 1)
                return hT_ready

            ready = {}

            def front(n, j, t):
                l = post_layer(j)
                if n == at(O, j):
                    pe.wait_ge(o_staged.sem, o_staged.upto(j, t, 1))
                    ready["oT"] = take(act_bank)
                    pe.transpose(ps[:, ACTB, 0:P], o_tile[:, 0:P], ident[:])
                    pe.transpose(ps[0:TAIL, ACTB, P:2 * P], o_tile[:, P:C], ident[:]).then_inc(oT_psum.sem, 1)
                if n == at(PROJ, j):
                    if isinstance(t, int) and t == 0 and j % 2 == 0:
                        pe.wait_ge(w_in[l], W_LOADS[l])
                        pe.wait_ge(weights_scaled, SCALED[l])
                    pe.wait_ge(*ready["oT"])
                    take(dve_bank)
                    w = W[l]
                    pe.matmul(ps[:, DVEB, 0:C], oT[:], w["proj"][:], start=True, stop=False)
                    pe.matmul(ps[:, DVEB, 0:C], oT_tail[:], w["proj_tail"][:],
                              start=False, stop=True).then_inc(proj_psum.sem, 1)
                if n == at(X1, j):
                    ready["hT", place(j, t)] = turn_x(j, t, 1)

            def back(n, j, t):
                if n == fc1_at(j, 0):
                    pe.wait_ge(*ready["hT", place(j, t)])
                    pe.wait_ge(v_stored.sem, v_stored.upto(j, t, 0))
                    if is_moe(j):
                        take(dve_bank)
                        pe.matmul(ps[:, DVEB, 0:NE], hT[:, 0], w_gate[:], start=True, stop=False)
                        pe.matmul(ps[:, DVEB, 0:NE], hT_tail[:, 0], w_gate_tail[:],
                                  start=False, stop=True).then_inc(logits_psum.sem, 1)
                for e in range(experts(j) + 1):
                    if n == fc1_at(j, e):
                        if e < experts(j):
                            if e:
                                pe.wait_ge(hid_squared.sem, hid_squared.upto(j, t, e))
                            fc1(j, t, e)
                        if e:
                            fc2(j, t, e - 1)

            def pre(n, j, t):
                l = pre_layer(j)
                if n == at(X2, j):
                    ready["hT before QKV"] = turn_x(j, t, 1 + has_post(j))
                if n == at(QKV, j):
                    if start_of(0, j, t):
                        pe.wait_ge(first_in, QKV_LOADS)
                        pe.wait_ge(first_scaled, 1)
                    elif isinstance(t, int) and t == 0 and j % 2 == 0:
                        pe.wait_ge(w_in[l], W_LOADS[l])
                        pe.wait_ge(weights_scaled, SCALED[l])
                    pe.wait_ge(*ready["hT before QKV"])
                    if not has_post(j) and not start_of(0, j, t):
                        pe.wait_ge(v_stored.sem, v_stored.upto(j, t, 0))
                    w = W[l]
                    pe.matmul(ps[:, WIDE, 0:3 * C], hT[:, 0], w["qkv"][:], start=True, stop=False)
                    pe.matmul(ps[:, WIDE, 0:3 * C], hT_tail[:, 0], w["qkv_tail"][:],
                              start=False, stop=True).then_inc(qkv_psum.sem, 1)

            def turn_rows(j, t, i):
                if i < 2:
                    ready_parts = k_parts_ready if i else q_parts_ready
                    pe.wait_ge(ready_parts.sem, ready_parts.upto(j, t, 1))
                take(dve_bank if i % 2 else act_bank)
                bank = DVEB if i % 2 else ACTB
                g, parts, step = i // 2, k_parts if i % 2 else q_parts, HD if i % 2 else 0
                for h in range(G):
                    for r in range(SPLIT):
                        last = pe.matmul(ps[r * BLOCK:(r + 1) * BLOCK, bank, h * P:(h + 1) * P],
                                         parts[:, g * G + h, r * step:r * step + BLOCK], identb[:],
                                         start=True, stop=True)
                last.then_inc(rows_psum.sem, 1)

            def fc1(j, t, e):
                take(act_bank)
                w = W[post_layer(j)]
                for c in range(FC):
                    m = min(P, FF - c * P)
                    o = ps[0:m, WIDE, c * P:(c + 1) * P] if c < FC - 1 else ps[0:m, ACTB, 0:P]
                    pe.matmul(o, w["w1"][:, e, c * P:c * P + m], hT[:, place(j, t)], start=True, stop=False)
                    last = pe.matmul(o, w["w1_tail"][:, e, c * P:c * P + m], hT_tail[:, place(j, t)],
                                     start=False, stop=True)
                last.then_inc(hid_psum.sem, 1)

            def fc2(j, t, e):
                w = W[post_layer(j)]
                pe.wait_ge(hid_ready.sem, hid_ready.upto(j, t, e + 1))
                take(dve_bank)
                for c in range(FC):
                    last = pe.matmul(ps[:, DVEB, 0:C], hid[:, e % 2, c, :], w["w2"][:, e, c, :],
                                     start=(c == 0), stop=(c == FC - 1))
                last.then_inc(mlp_psum.sem, 1)

            def slot(p, j, s, A, M, N, D, R):
                if p in (0, 1) and isinstance(s, int) and s == 0:
                    pe.wait_ge(pool_presets, p + 1)
                if p == -1 and is_turnover(j, s):
                    pe.wait_ge(turns_read, len(turn_groups))
                    pe.wait_ge(gates_ready, len(gate_list))
                    pe.wait_ge(mods_ready, LAYERS)
                mp, mg, m0 = of_maxima(p, s)
                for n in range(length(j, s, M, D, R)):
                    m = n - m0
                    for kind, i in chores_at(n, p, s):
                        chore(kind, i)
                    if A and n < STEPS:
                        score_keys(p, s, n, ready.get("rows"))
                    if M and 0 <= m < STEPS:
                        if is_turnover(j, s) and m == 0:
                            pe.wait_ge(act_read, act_bank.value() + 1)
                            pe.wait_ge(dve_read, dve_bank.value() + 1)
                        score_queries(mp, mg, m)
                    if A and n == 0:
                        ready["rows"] = turn_max(p, s, G - 1)
                    if A and n % G == 1 and G < n < STEPS:
                        values(p, s, n // G - 1)
                    if M and m % NT == 1 and NT < m < STEPS:
                        turn_max(mp, mg, m // NT - 1)
                    if N and n == at(VALUES, j):
                        values(p, s - 1, NK - 1)
                    if N and n == at(TURN, j):
                        turn_attn(p, s - 1)
                    if R and rows_at(n, j, s) is not None:
                        turn_rows(j, s - 1, rows_at(n, j, s))
                    if R:
                        pre(n, j, s - 1)
                    if D and has_post(j):
                        head, tail = tiles(j, s)
                        if head is not None:
                            front(n, j, head)
                        if tail is not None:
                            back(n, j, tail)

            slots(slot, pe, (act_bank, act_uses), (dve_bank, dve_uses))

        @block.scalar
        def _(act):
            act.wait_ge(c_in, 32)
            act.wait_ge(tail_set, 1)
            act.activation(sT[:], cT[:], ACT.Exp, scale=-1.0)
            act.activation(sT_tail[0:TAIL], cT_tail[0:TAIL], ACT.Exp, scale=-1.0).then_inc(silu_exp, 1)
            act.wait_ge(presets, 1)
            act.wait_ge(mods_ready, 1)

            def take_gate(i):
                l, g = gate_list[i]
                act.wait_ge(gates_psum, i + 1)
                act.activation(gate[:, l, g], ps[:, KEYB + i % 2, 0:B * C].rearrange("p (b c) -> p b c", b=B),
                               ACT.Tanh if l == 1 else ACT.Copy).then_inc(gates_ready, 1)

            def exps(p, u, n):
                act.wait_ge(key_scores, unit(p, u) * STEPS + n + 1)
                act.activation(probs[:, n // G, n % G], ps[:, KEYB + n % 2], ACT.Exp).then_inc(exp_done, 1)

            def store_max(p, s, h):
                act.wait_ge(max_rows, unit(p, s) * G + h + 1)
                head = ((p % B) * H + s * G + h) * L
                act.activation(q_rows[MROW:MROW + 2, bass.ds(head, L)], ps[MROW:MROW + 2, ACTB],
                               ACT.Copy).then_inc(act_read, 1)

            def modulate(j, t, k, l, first):
                b, i = j % B, place(j, t)
                act.wait_ge(xT_psum.sem, xT_psum.upto(j, t, k))
                act.activation(hT[:, i], ps[:, ACTB, 0:P], ACT.Identity,
                               bias=mod[:, l, first, b:b + 1], scale=mod[:, l, first + 1, b:b + 1])
                act.activation(hT_tail[0:TAIL, i], ps[0:TAIL, ACTB, P:2 * P], ACT.Identity,
                               bias=mod_tail[0:TAIL, l, first, b:b + 1],
                               scale=mod_tail[0:TAIL, l, first + 1, b:b + 1]).then_inc(act_read, 1)

            def take_hidden(j, t, e):
                act.wait_ge(hid_psum.sem, hid_psum.upto(j, t, e + 1))
                x, square, last = hid_x[:, e % 2], hid[:, e % 2], ps[0:FR, ACTB, 0:P]
                act.activation(x[0:FR, FC - 1], last, ACT.Copy)
                act.activation(square[0:FR, FC - 1], last, ACT.Square, scale=GELU_CUBE ** 0.5).then_inc(act_read, 1)
                act.activation(flat(x[:, 0:FC - 1]), ps[:, WIDE], ACT.Copy)
                act.activation(flat(square[:, 0:FC - 1]), ps[:, WIDE], ACT.Square,
                               scale=GELU_CUBE ** 0.5).then_inc(hid_squared.sem, 1)

            def tanh_hidden(j, t, e):
                act.wait_ge(hid_inner.sem, hid_inner.upto(j, t, e + 1))
                m = flat(hid[:, e % 2])
                act.activation(m, m, ACT.Tanh, scale=GELU_SCALE).then_inc(hid_tanh.sem, 1)

            def front(n, j, t):
                if n == at(O, j):
                    act.wait_ge(oT_psum.sem, oT_psum.upto(j, t, 1))
                    act.activation(oT[:], ps[:, ACTB, 0:P], ACT.Copy)
                    act.activation(oT_tail[0:TAIL], ps[0:TAIL, ACTB, P:2 * P], ACT.Copy).then_inc(act_read, 1)
                if n == at(X1, j):
                    modulate(j, t, 1, post_layer(j), SHIFT2)

            def back(n, j, t):
                if n == fc1_at(j, 0) and is_moe(j):
                    act.wait_ge(top_ready.sem, top_ready.upto(j, t, 1))
                    act.activation(gex[:], lg[:], ACT.Exp, bias=neg_top[:]).then_inc(gate_exp.sem, 1)
                for e in range(experts(j)):
                    if n == fc1_at(j, e):
                        take_hidden(j, t, e)
                    if n == inner_at(j, e):
                        tanh_hidden(j, t, e)

            def pre(n, j, t):
                l = pre_layer(j)
                if n == at(X2, j):
                    modulate(j, t, 1 + has_post(j), l, SHIFT1)
                if n == at(QKV, j):
                    act.wait_ge(qkv_psum.sem, qkv_psum.upto(j, t, 1))
                    q_and_k = ps[:, WIDE, 0:2 * C].rearrange("p (h d) -> p h d", d=HD)
                    if normed(j):
                        act.activation(qk[:], q_and_k, ACT.Copy)
                        act.activation(sq[:], q_and_k, ACT.Square).then_inc(qk_squared.sem, 1)
                    else:
                        act.activation(q_parts[:, :, 0:HD], q_and_k[:, 0:H], ACT.Copy)
                        act.activation(twice(0), for_both(q_and_k[:, H:2 * H]), ACT.Copy)
                        act.activation(qk[:], q_and_k, ACT.Copy).then_inc(high_ready.sem, 1)
                    act.activation(v_all[:, bass.ds(((j % B) * NT + t) * C, C)], ps[:, WIDE, 2 * C:3 * C],
                                   ACT.Copy).then_inc(v_stored.sem, 1)
                if n == at(SPLIT_QK, j) and normed(j):
                    act.wait_ge(qk_ready.sem, qk_ready.upto(j, t, 1))
                    act.activation(q_parts[:, :, 0:HD], qk[:, 0:H], ACT.Copy)
                    act.activation(twice(0), for_both(qk[:, H:2 * H]), ACT.Copy).then_inc(high_ready.sem, 1)

            def store_q(j, t, g):
                act.wait_ge(rows_psum.sem, rows_psum.upto(j, t, 2 * g + 1))
                act.activation(rows_of(q_rows, j, t, g), ps[0:MROW, ACTB].rearrange("p (h q) -> p h q", h=G),
                               ACT.Copy).then_inc(act_read, 1)

            def store_k(j, t, g):
                act.wait_ge(rows_psum.sem, rows_psum.upto(j, t, 2 * g + 2))
                act.activation(rows_of(k_rows, j, t, g), ps[0:MROW, DVEB].rearrange("p (h q) -> p h q", h=G),
                               ACT.Copy).then_inc(dve_read, 1)

            def slot(p, j, s, A, M, N, D, R):
                if isinstance(s, int) and s == 0 and j == 1:
                    act.wait_ge(mods_ready, LAYERS)
                mp, mg, m0 = of_maxima(p, s)
                for n in range(length(j, s, M, D, R)):
                    m = n - m0
                    for kind, i in chores_at(n, p, s):
                        if kind == "gate":
                            take_gate(i)
                    if A and n < STEPS:
                        exps(p, s, n)
                    if A and n == 0:
                        store_max(p, s, G - 1)
                    if M and m % NT == 1 and NT < m < STEPS:
                        store_max(mp, mg, m // NT - 1)
                    if N and n == at(VALUES, j):
                        act.wait_ge(pv_done, unit(p, s - 1) + 2)
                        act.activation(attn_t[:], ps[:, OUTB], ACT.Copy).then_inc(attn_t_ready, 1)
                    if R and rows_at(n, j, s) in (0, 2, 4, 6):
                        store_q(j, s - 1, rows_at(n, j, s) // 2)
                    if R and rows_at(n, j, s) in k_by_act(j, s):
                        store_k(j, s - 1, rows_at(n, j, s) // 2)
                    if R:
                        pre(n, j, s - 1)
                    if D and has_post(j):
                        head, tail = tiles(j, s)
                        if head is not None:
                            front(n, j, head)
                        if tail is not None:
                            back(n, j, tail)

            slots(slot, act)

        @block.vector
        def _(dve):
            link = Chain(dve, vchain)
            from_bank = Chain(dve, dve_read)
            from_bank.n = 1

            def scale_q(l):
                for m in (W[l]["qkv"][:, 0:C], W[l]["qkv_tail"][0:ONE + 1, 0:C]):
                    last = dve.tensor_scalar(m, m, HD ** -0.5, None, ALU.mult)
                return last

            def centre_heads(l):
                for m, r in ((W[l]["qkv"], P), (W[l]["qkv_tail"], ONE + 1)):
                    heads = m[0:r, 0:2 * C].rearrange("p (h d) -> p h d", d=HD)
                    link(dve.tensor_reduce(hsum[0:r], heads, AX.X, ALU.add))
                    link(dve.tensor_scalar(hsum[0:r], hsum[0:r], 1.0 / HD, None, ALU.mult))
                    link(dve.tensor_tensor(heads, heads, hsum[0:r].unsqueeze(2).broadcast_to([r, 2 * H, HD]),
                                           ALU.subtract))

            def scale_w2(l):
                m = W[l]["w2"][:, :, 0:FC - 1]
                dve.tensor_scalar(m, m, 0.5, None, ALU.mult)
                m = W[l]["w2"][0:FR, :, FC - 1]
                dve.tensor_scalar(m, m, 0.5, None, ALU.mult)
                m = W[l]["w2"][FR:FR + 1, :, FC - 1]
                dve.tensor_scalar(m, m, 0.5 / FAR, None, ALU.mult).then_inc(weights_scaled, 1)

            dve.memset(sT_tail[:], 1.0).then_inc(tail_set, 1)
            for w in wset:
                for name in ("qkv_tail", "proj_tail", "w1_tail"):
                    if name in w and (w is not wset[2] or name != "w1_tail"):
                        dve.memset(w[name][:], 0.0)
            for w in W[0], W[1], W[2]:
                dve.memset(w["w2"][FR:P, :, FC - 1], 0.0)
            dve.memset(w_gate_tail[:], 0.0).then_inc(rows_cleared, 1)
            dve.wait_ge(silu_exp, 1)
            link(dve.tensor_scalar(sT[:], sT[:], 1.0, None, ALU.add))
            link(dve.tensor_scalar(sT_tail[0:TAIL], sT_tail[0:TAIL], 1.0, None, ALU.add))
            link(dve.reciprocal(sT[:], sT[:]))
            link(dve.reciprocal(sT_tail[0:TAIL], sT_tail[0:TAIL]))
            link(dve.tensor_tensor(sT[:], sT[:], cT[:], ALU.mult))
            link(dve.tensor_tensor(sT_tail[0:TAIL], sT_tail[0:TAIL], cT_tail[0:TAIL], ALU.mult))
            dve.tensor_copy(sB[:], sT[:].unsqueeze(2).broadcast_to([P, B, P])).then_inc(silu_ready, 1)
            dve.tensor_copy(sB_tail[0:ONE + 1], sT_tail[0:ONE + 1].unsqueeze(2).broadcast_to([ONE + 1, B, P])
                            ).then_inc(silu_ready, 1)
            dve.memset(q_parts[:], 0.0)
            dve.memset(k_parts[:], 0.0)
            dve.memset(oT_tail[:], 1.0)
            dve.memset(hT_tail[:], 1.0)
            dve.memset(one[:], 1.0)
            dve.memset(half[:], -0.5).then_inc(half_ready, 1)
            dve.memset(hid[:], 0.0)
            link(dve.memset(hid_x[FR:P, :, FC - 1], 0.0))
            dve.memset(hid_x[FR:FR + 1, :, FC - 1], FAR).then_inc(presets, 1)
            dve.memset(rest[:], 0.0).then_inc(act_read, 1)
            dve.memset(hvar[:], 0.0).then_inc(dve_read, 1)
            dve.memset(mx[:], 0.0).then_inc(exp_done, 1)
            dve.memset(st[:], 0.0).then_inc(exp_done, 1)
            dve.memset(mv[:], 0.0).then_inc(max_taken, 1)
            dve.memset(var[:], 0.0).then_inc(max_taken, 1)
            dve.memset(rstd[:], 0.0).then_inc(attn_t_ready, 1)
            dve.memset(rank[:], 0.0)
            dve.memset(gsum[:], 0.0).then_inc(pv_done, 1)
            dve.wait_ge(small_in, 16 * 6)
            link(dve.tensor_scalar(one_gain[:, 0:2], one_gain[:, 0:2], C ** 0.5, None, ALU.mult))
            link(dve.tensor_scalar(one_gain[:, 3:4], one_gain[:, 3:4], HD ** 0.5, None, ALU.mult))
            link(dve.tensor_scalar(head_gain[:, 0], head_gain[:, 0], HD ** -0.5, None, ALU.mult))

            def take_mods(l):
                dve.wait_ge(mods_psum, l + 1)
                dve.tensor_copy(mod[:, l], ps[:, OUTB, 0:4 * B].rearrange("p (i b) -> p i b", b=B))
                link(dve.tensor_copy(mod_tail[0:TAIL, l], ps[0:TAIL, OUTB, P:P + 4 * B].rearrange(
                    "p (i b) -> p i b", b=B)))
                for m, r in ((mod, P), (mod_tail, TAIL)):
                    for g, i in enumerate((SCALE1, SCALE2)):
                        link(dve.tensor_scalar(m[0:r, l, i], m[0:r, l, i], 1.0, None, ALU.add))
                        last = dve.tensor_scalar(m[0:r, l, i], m[0:r, l, i],
                                                 one_gain[0:r, g:g + 1] if l == 1 else 1.0, None, ALU.mult)
                last.then_inc(mods_ready, 1)

            def take_turn(i):
                dve.wait_ge(turn_psum, i + 1)
                for n, (src, dst) in enumerate(turn_groups[i]):
                    k, m = src.shape[0], src.shape[1]
                    last = dve.tensor_copy(dst, ps[0:m, MAXB + i % 2, n * P:n * P + k])
                last.then_inc(turns_read, 1)

            take_mods(0)
            dve.wait_ge(first_in, QKV_LOADS)
            scale_q(0).then_inc(first_scaled, 1)
            dve.wait_ge(x_in, 16)

            def maxima(p, s, n):
                h, qt = divmod(n, NT)
                dve.wait_ge(max_scores, unit(p, s) * STEPS + n + 1)
                dve.tensor_reduce(mx[:, h, qt:qt + 1], ps[:, MAXB + n % 2], AX.X, ALU.max).then_inc(max_taken, 1)

            def split_max(p, s, h):
                dve.wait_ge(max_taken, unit(p, s) * STEPS + (h + 1) * NT + 2)
                link(dve.tensor_copy(mx_parts[:, h, :, 0], mx[:, h]))
                dve.tensor_tensor(mx_parts[:, h, :, 1], mx[:, h], mx_parts[:, h, :, 0],
                                  ALU.subtract).then_inc(max_split, 1)

            def normalize(p, u):
                dve.wait_ge(attn_psum, unit(p, u) + 1)
                o = ps[:, DVEB].rearrange("p (t h r) -> p t h r", t=NT, h=G)
                link(dve.reciprocal(rsum[:], o[:, :, :, HD]))
                dve.tensor_tensor(group_of(attn, p, u), o[:, :, :, 0:HD], rsum[:].unsqueeze(3).broadcast_to([P, NT, G, HD]),
                                  ALU.mult).then_inc(dve_read, 1)
                from_bank.n += 1

            def norm_sum(l, x):
                if l == 1:
                    link(dve.tensor_tensor_reduce(tmp[:], x, x, 1.0, 0.0, ALU.mult, ALU.add, st[:, 0:1]))
                    dve.tensor_scalar(var[:], st[:, 0:1], TINY, None, ALU.max).then_inc(var_ready.sem, 1)
                else:
                    link(dve.bn_stats(st[:], x))
                    dve.memset(pause[:], 0.0)
                    link(dve.bn_aggr(mv[:], st[:]))
                    dve.tensor_scalar(var[:], mv[:, 1:2], LN_EPS, None, ALU.add).then_inc(var_ready.sem, 1)

            def norm(j, t, k, l, x):
                if not (start_of(0, j, t) and k == 1):
                    dve.wait_ge(xT_psum.sem, xT_psum.upto(j, t, k - 1))
                dve.wait_ge(rstd_ready.sem, rstd_ready.upto(j, t, k))
                if l == 1:
                    dve.tensor_scalar(xn[:], x, rstd[:], None, ALU.mult).then_inc(x_normed.sem, 1)
                else:
                    dve.tensor_scalar(xn[:], x, mv[:, 0:1], rstd[:], ALU.subtract,
                                      ALU.mult).then_inc(x_normed.sem, 1)

            def route(j, t):
                dve.wait_ge(logits_psum.sem, logits_psum.upto(j, t, 1))
                from_bank(dve.tensor_copy(lg[:], ps[:, DVEB, 0:NE]))
                dve.tensor_reduce(neg_top[:], lg[:], AX.X, ALU.max, negate=True).then_inc(top_ready.sem, 1)
                own = lg[:].unsqueeze(2).broadcast_to([P, NE, NE])
                other = lg[:].unsqueeze(1).broadcast_to([P, NE, NE])
                dve.tensor_tensor(above[:], other, own, ALU.is_gt)
                link(dve.tensor_tensor(ties[:], other, own, ALU.is_equal))
                link(dve.tensor_tensor(ties[:], ties[:], earlier[:], ALU.mult))
                link(dve.tensor_tensor(above[:], above[:], ties[:], ALU.add))
                link(dve.tensor_reduce(rank[:], above[:], AX.X, ALU.add))
                link(dve.tensor_scalar(rank[:], rank[:], 1.5, None, ALU.is_lt))
                dve.wait_ge(gate_exp.sem, gate_exp.upto(j, t, 1))
                link(dve.tensor_tensor(cw[:], gex[:], rank[:], ALU.mult))
                link(dve.tensor_reduce(gsum[:], cw[:], AX.X, ALU.add))
                link(dve.reciprocal(gsum[:], gsum[:]))
                link(dve.tensor_scalar(cw[:], cw[:], gsum[:], None, ALU.mult))

            def take_mlp(j, t, e):
                l, b = post_layer(j), j % B
                dve.wait_ge(mlp_psum.sem, mlp_psum.upto(j, t, e + 1))
                out = ps[:, DVEB, 0:C]
                if not is_moe(j):
                    from_bank(dve.tensor_tensor(tmp[:], out, gate[:, l, 1, b], ALU.mult))
                elif e == 0:
                    from_bank(dve.tensor_scalar(acc[:], out, cw[:, 0:1], None, ALU.mult))
                else:
                    from_bank(dve.scalar_tensor_tensor(out=acc[:], in0=out, scalar=cw[:, e:e + 1], in1=acc[:],
                                                       op0=ALU.mult, op1=ALU.add))
                if e + 1 < experts(j):
                    return
                if is_moe(j):
                    link(dve.tensor_tensor(tmp[:], acc[:], gate[:, l, 1, b], ALU.mult))
                dve.tensor_tensor(X[:, bass.ds((b * NT + t) * C, C)], xa[:, place(j, t)], tmp[:],
                                  ALU.add).then_inc(x_stored.sem, 1)
                link(dve.tensor_tensor(xm[:], xa[:, place(j, t)], tmp[:], ALU.add))

            def root_heads():
                link(dve.tensor_scalar(newton[:].bitcast(I32), hvar[:].bitcast(I32), 1, None,
                                       ALU.logical_shift_right))
                dve.tensor_scalar(hvar[:], hvar[:], -0.5, None, ALU.mult)
                link(dve.tensor_scalar(hrstd[:].bitcast(I32), newton[:].bitcast(I32), -1.0, ROOT_GUESS,
                                       ALU.mult, ALU.add))
                for _ in range(3):
                    link(dve.tensor_tensor(newton[:], hrstd[:], hrstd[:], ALU.mult))
                    link(dve.tensor_tensor(newton[:], newton[:], hvar[:], ALU.mult))
                    link(dve.scalar_tensor_tensor(out=hrstd[:], in0=newton[:], scalar=1.5, in1=hrstd[:],
                                                  op0=ALU.add, op1=ALU.mult))

            def hidden_inner(j, t, e):
                dve.wait_ge(hid_squared.sem, hid_squared.upto(j, t, e + 1))
                m = flat(hid[:, e % 2])
                dve.scalar_tensor_tensor(out=m, in0=m, scalar=1.0, in1=flat(hid_x[:, e % 2]), op0=ALU.add,
                                         op1=ALU.mult).then_inc(hid_inner.sem, 1)

            def hidden_outer(j, t, e):
                dve.wait_ge(hid_tanh.sem, hid_tanh.upto(j, t, e + 1))
                m = flat(hid[:, e % 2])
                dve.scalar_tensor_tensor(out=m, in0=m, scalar=1.0, in1=flat(hid_x[:, e % 2]), op0=ALU.add,
                                         op1=ALU.mult).then_inc(hid_ready.sem, 1)

            def normalize_heads(n, j, t):
                heads = lambda m: m.unsqueeze(2).broadcast_to([P, 2 * H, HD])
                three = pre_layer(j) == 3
                if n == at(VARIANCE, j):
                    dve.wait_ge(qk_squared.sem, qk_squared.upto(j, t, 1))
                    link(dve.tensor_reduce(hvar[:], sq[:], AX.X, ALU.add))
                    if three:
                        link(dve.tensor_scalar(hvar[:], hvar[:], 1.0 / HD, LN_EPS, ALU.mult, ALU.add))
                    else:
                        link(dve.tensor_scalar(hvar[:], hvar[:], TINY, None, ALU.max))
                if n == at(ROOT, j):
                    root_heads()
                if n == at(HEADS, j) and three:
                    link(dve.tensor_tensor(qk[:], qk[:], heads(hrstd[:]), ALU.mult))
                    two = qk[:].rearrange("p (s h) d -> p s h d", s=2)
                    dve.tensor_tensor(two, two, head_gain[:].unsqueeze(2).broadcast_to([P, 2, H, HD]),
                                      ALU.mult).then_inc(qk_ready.sem, 1)
                if n == at(HEADS, j) and not three:
                    for i in range(2):
                        part = hrstd[:, i * H:(i + 1) * H]
                        link(dve.tensor_scalar(part, part, one_gain[:, 2 + i:3 + i], None, ALU.mult))
                    dve.tensor_tensor(qk[:], qk[:], heads(hrstd[:]), ALU.mult).then_inc(qk_ready.sem, 1)

            def split_k(n, j, t):
                part = lambda m, i: m[:, :, i * HD:(i + 1) * HD]
                if n == at(SPLIT_QK, j):
                    dve.wait_ge(high_ready.sem, high_ready.upto(j, t, 1))
                    link(dve.tensor_tensor(rest[:, H:2 * H], qk[:, H:2 * H], part(k_parts, 0), ALU.subtract))
                    link(dve.tensor_copy(twice(1), for_both(rest[:, H:2 * H])))
                if n == at(SPLIT_REST, j):
                    dve.tensor_tensor(part(k_parts, 2), rest[:, H:2 * H], part(k_parts, 1),
                                      ALU.subtract).then_inc(k_parts_ready.sem, 1)

            def front(n, j, t):
                l, b = post_layer(j), j % B
                here, after = X[:, bass.ds((b * NT + t) * C, C)], xa[:, place(j, t)]
                if n == at(SUM, j):
                    dve.wait_ge(proj_psum.sem, proj_psum.upto(j, t, 1))
                    from_bank(dve.tensor_tensor(tmp[:], ps[:, DVEB, 0:C], gate[:, l, 0, b], ALU.mult))
                    link(dve.tensor_tensor(after, here, tmp[:], ALU.add))
                    norm_sum(l, after)
                if n == at(XN1, j):
                    norm(j, t, 1, l, after)

            def back(n, j, t):
                if n == fc1_at(j, 0) and is_moe(j):
                    route(j, t)
                for e in range(experts(j)):
                    if n == inner_at(j, e):
                        hidden_inner(j, t, e)
                    if n == outer_at(j, e):
                        hidden_outer(j, t, e)
                    if n == fc1_at(j, e + 1):
                        take_mlp(j, t, e)

            def next_norm(n, j, t):
                if not has_post(j) and n == added_at(j):
                    if not start_of(0, j, t):
                        dve.wait_ge(x_normed.sem, x_normed.upto(j, t, 0))
                    link(dve.tensor_scalar(xm[:], X[:, bass.ds(((j % B) * NT + t) * C, C)], 1.0, None, ALU.mult))
                if n == added_at(j) and has_pre(j):
                    norm_sum(pre_layer(j), xm[:])
                if n == added_at(j) + 1 and has_pre(j):
                    norm(j, t, 1 + has_post(j), pre_layer(j), xm[:])

            def pre(n, j, t):
                if normed(j):
                    normalize_heads(n, j, t)
                split_k(n, j, t)

            def store_k(j, t, g):
                dve.wait_ge(rows_psum.sem, rows_psum.upto(j, t, 2 * g + 2))
                dve.tensor_scalar(rows_of(k_rows, j, t, g), ps[0:MROW, DVEB].rearrange("p (h q) -> p h q", h=G),
                                  1.0, None, ALU.mult).then_inc(dve_read, 1)
                from_bank.n += 1

            def links(j, A, M, N, D, R):
                norm_links = lambda l: 1 if l == 1 else 2
                n = G * M + N
                if D and has_post(j):
                    n += 2 + norm_links(post_layer(j)) + (10 if is_moe(j) else 0)
                if D and has_pre(j):
                    n += norm_links(pre_layer(j)) + (not has_post(j))
                if R:
                    n += 2 + {1: 4 + 11, 3: 3 + 11}.get(pre_layer(j), 0)
                return n

            def slot(p, j, s, A, M, N, D, R):
                if isinstance(s, int) and s == 0 and j in (1, 3, 5):
                    for l in {1: (0, 1), 3: (2,), 5: (3,)}[j]:
                        dve.wait_ge(w_in[l], W_LOADS[l])
                        if l and l not in NORMED:
                            scale_q(l)
                        if l == 3:
                            centre_heads(l)
                        scale_w2(l)
                if isinstance(s, int) and s == 0 and j == 1:
                    dve.wait_ge(gates_ready, len(gate_list))
                mp, mg, m0 = of_maxima(p, s)
                for n in range(length(j, s, M, D, R)):
                    m = n - m0
                    for kind, i in chores_at(n, p, s):
                        if kind == "turn":
                            take_turn(i)
                        if kind == "mods":
                            take_mods(i)
                    if M and 0 <= m < STEPS:
                        maxima(mp, mg, m)
                        if m % NT == NT - 1:
                            split_max(mp, mg, m // NT)
                    if N and n == at(TURN, j):
                        normalize(p, s - 1)
                    if R and rows_at(n, j, s) in (1, 3, 5, 7):
                        if rows_at(n, j, s) in k_by_act(j, s):
                            from_bank.n += 1
                        else:
                            store_k(j, s - 1, rows_at(n, j, s) // 2)
                    if R:
                        pre(n, j, s - 1)
                    if D and has_post(j):
                        head, tail = tiles(j, s)
                        if head is not None:
                            front(n, j, head)
                        if tail is not None:
                            back(n, j, tail)
                    if D:
                        next_norm(n, j, s)

            slots(slot, dve, (link, links), (from_bank, dve_uses))

        @block.gpsimd
        def _(pool):
            link = Chain(pool, pchain)
            for m in (ident, identb):
                link(pool.memset(m[:], 0.0))
                link(pool.affine_select(out=m[:], in_=m[:], compare_op=ALU.not_equal, fill=1.0, base=0,
                                        pattern=[[-1, P]], channel_multiplier=1))
            pool.memset(v_unit[:], 0.0).then_inc(ident_made, 1)
            pool.wait_ge(ident_made, 1)
            link(pool.memset(v_unit[:, :, :, HD:HD + 1], 1.0))
            link(pool.memset(earlier[:], 0.0))
            for e in range(1, NE):
                link(pool.memset(earlier[:, e, 0:e], 1.0))
            def minus_ones(b):
                m = k_rows[MROW:P, b * H * L:(b + 1) * H * L].bitcast(F32)
                pool.memset(m, MINUS_ONES).then_inc(pool_presets, 1)
                pool.wait_ge(pool_presets, b + 1)

            link(pool.memset(q_rows[MROW:P].bitcast(F32), 0.0))
            minus_ones(0)
            pool.wait_ge(half_ready, 1)

            def root(steps, ready, j, t, k, dst, src):
                pool.wait_ge(ready.sem, ready.upto(j, t, k))
                pool.tensor_tensor(dst, src, half[:], ALU.pow).then_inc(steps.sem, 1)
                pool.wait_ge(steps.sem, steps.upto(j, t, k))

            def stage_v(p, u):
                pool.wait_ge(pv_done, unit(p, u) + 1)
                pool.tensor_copy(v_unit[:, :, :, 0:HD], group_of(v_all, p, u)).then_inc(v_staged, 1)
                pool.wait_ge(v_staged, unit(p, u) + 1)

            def split_q(j, t):
                part = lambda i: q_parts[:, :, i * HD:(i + 1) * HD]
                ones = one[:].unsqueeze(2).broadcast_to([P, H, HD])
                pool.wait_ge(high_ready.sem, high_ready.upto(j, t, 1))
                pool.tensor_tensor(rest[:, 0:H], qk[:, 0:H], part(0), ALU.subtract).then_inc(q_middle.sem, 1)
                pool.wait_ge(q_middle.sem, q_middle.upto(j, t, 1))
                pool.tensor_tensor(part(1), rest[:, 0:H], ones, ALU.mult).then_inc(q_middle.sem, 1)
                pool.wait_ge(q_middle.sem, q_middle.upto(j, t, 2))
                pool.tensor_tensor(part(2), rest[:, 0:H], part(1), ALU.subtract).then_inc(q_parts_ready.sem, 1)
                pool.wait_ge(q_parts_ready.sem, q_parts_ready.upto(j, t, 1))

            def slot(p, j, s, A, M, N, D, R):
                D = D and tiles(j, s)[0] is not None
                if D and has_post(j):
                    pool.wait_ge(dve_read, attended(j - 2))
                    if not start_of(2, j, s):
                        pool.wait_ge(oT_psum.sem, oT_psum.upto(j, s, 0))
                    pool.tensor_copy(o_tile[:], attn[:, bass.ds(((j % B) * NT + s) * C, C)]).then_inc(o_staged.sem, 1)
                    pool.wait_ge(o_staged.sem, o_staged.upto(j, s, 1))
                if A:
                    pool.wait_ge(v_stored.sem, v_stored.upto(p, NT, 0))
                    stage_v(p, s)
                for n in range(length(j, s, M, D, R)):
                    if R and n == at(SPLIT_QK, j):
                        split_q(j, s - 1)
                    if D and has_post(j) and n == at(SUM, j):
                        root(rstd_ready, var_ready, j, s, 1, rstd[:], var[:])
                    if D and has_pre(j) and n == added_at(j):
                        root(rstd_ready, var_ready, j, s, 1 + has_post(j), rstd[:], var[:])
                if isinstance(s, int) and s == 0 and j == 1:
                    pool.wait_ge(mods_psum, LAYERS)
                    pool.wait_ge(gates_psum, len(gate_list))
                    pool.memset(W[2]["w1_tail"], 0.0).then_inc(rows_cleared, 1)
                    pool.wait_ge(rows_cleared, 2)
                    pool.wait_ge(turn_psum, len(turn_groups))
                    minus_ones(1)

            slots(slot, pool)


_OUTS = [((2, 512, 144), "float32")]


def kernel(**inputs):
    import numpy as _np
    import concourse.bacc as _bacc
    from concourse import mybir as _mybir
    from concourse.bass_utils import run_bass_kernel_spmd as _run

    nc = _bacc.Bacc("TRN2", target_bir_lowering=False, num_devices=1)
    arrays, args = {}, {}
    for name, value in inputs.items():
        v = _np.ascontiguousarray(value)
        arrays[f"in_{name}_dram"] = v
        args[name] = nc.dram_tensor(f"in_{name}_dram", v.shape, _mybir.dt.from_np(v.dtype), kind="ExternalInput").ap()
    shape, dtype = _OUTS[0]
    out = nc.dram_tensor("out_0_dram", shape, _mybir.dt.from_np(_np.dtype(dtype)), kind="ExternalOutput").ap()
    build(nc, args, out)
    r = _run(nc, [arrays], core_ids=[0])
    return r.results[0]["out_0_dram"]
```
